# Optimizing a Trainium2 kernel written in Bass

```python
import numpy as np
import jax
import jax.numpy as jnp

def _softmax(x, axis=-1):
    return jax.nn.softmax(x, axis=axis)

def _gelu(x):
    return jax.nn.gelu(x, approximate=True)

def _silu(x):
    return jax.nn.silu(x)

def _sigmoid(x):
    return jax.nn.sigmoid(x)

def _layernorm(x, axis=-1, eps=1e-05):
    m = jnp.mean(x, axis=axis, keepdims=True)
    v = jnp.var(x, axis=axis, keepdims=True)
    return (x - m) / jnp.sqrt(v + eps)

def _scatter_add(tgt, idx, src, axis=0):
    return tgt.at[idx].add(src)

def _segment_sum(src, seg, n):
    return jax.ops.segment_sum(src, seg, n)
kernel_name = 'mk_hybrid_d1_jaxref_r8_ba1d81'

def setup_inputs(seed: int=0):
    np.random.seed(seed)
    _w = jnp.asarray

    def _L0_attn_a_setup():
        import jax, jax.numpy as jnp
        import numpy as np
        B, S = (1, 512)
        HID, H, D = (256, 16, 128)
        KVC, QC, RD = (64, 192, 64)
        THETA = 10000.0

        def _mla_forward(hidden_states, W_DKV, b_DKV, W_UK, b_UK, W_UV, b_UV, W_DQ, b_DQ, W_UQ, b_UQ, W_QR, W_KR, W_O, b_O):
            b, s, _ = hidden_states.shape
            c_kv = hidden_states @ W_DKV + b_DKV
            k = (c_kv @ W_UK + b_UK).reshape(b, s, H, D)
            v = (c_kv @ W_UV + b_UV).reshape(b, s, H, D)
            c_q = hidden_states @ W_DQ + b_DQ
            q = (c_q @ W_UQ + b_UQ).reshape(b, s, H, D)
            half = RD // 2
            inv_freq = 1.0 / THETA ** (jnp.arange(0, RD, 2, dtype=jnp.float32) / RD)
            t = jnp.arange(s, dtype=jnp.float32)
            freqs = t[:, None] * inv_freq[None, :]
            cos = jnp.cos(freqs)[None, :, None, :]
            sin = jnp.sin(freqs)[None, :, None, :]
            q_r = q @ W_QR
            k_r = k @ W_KR

            def rope(x):
                x1, x2 = (x[..., :half], x[..., half:])
                first = x1 * cos - x2 * sin
                return jnp.concatenate([first, jnp.zeros_like(first)], axis=-1)
            q = q.at[..., :RD].set(rope(q_r))
            k = k.at[..., :RD].set(rope(k_r))
            scores = jnp.einsum('bqhd,bkhd->bhqk', q, k) / jnp.sqrt(jnp.float32(D))
            probs = jax.nn.softmax(scores, axis=-1)
            ctx = jnp.einsum('bhqk,bkhd->bqhd', probs, v).reshape(b, s, H * D)
            return ctx @ W_O + b_O
        key = jax.random.key(seed)
        ks = jax.random.split(key, 16)
        w = lambda k, shp: jax.random.normal(k, shp, jnp.float32) * 0.02
        return {'hidden_states': jax.random.normal(ks[0], (B, S, HID), jnp.float32), 'W_DKV': w(ks[1], (HID, KVC)), 'b_DKV': jnp.zeros((KVC,), jnp.float32), 'W_UK': w(ks[2], (KVC, H * D)), 'b_UK': jnp.zeros((H * D,), jnp.float32), 'W_UV': w(ks[3], (KVC, H * D)), 'b_UV': jnp.zeros((H * D,), jnp.float32), 'W_DQ': w(ks[4], (HID, QC)), 'b_DQ': jnp.zeros((QC,), jnp.float32), 'W_UQ': w(ks[5], (QC, H * D)), 'b_UQ': jnp.zeros((H * D,), jnp.float32), 'W_QR': w(ks[6], (D, RD)), 'W_KR': w(ks[7], (D, RD)), 'W_O': w(ks[8], (H * D, HID)), 'b_O': jnp.zeros((HID,), jnp.float32)}
    _L0_attn_a_in = _L0_attn_a_setup()

    def _L0_attn_b_setup():
        import jax, jax.numpy as jnp
        import numpy as np
        NH = 16
        key = jax.random.key(seed)
        ks = jax.random.split(key, 5)
        B, T, D = (2, 256, 256)
        scale = 0.02
        return {'x': jax.random.normal(ks[0], (B, T, D), dtype=jnp.float32), 'Wq': jax.random.normal(ks[1], (D, D), dtype=jnp.float32) * scale, 'Wk': jax.random.normal(ks[2], (D, D), dtype=jnp.float32) * scale, 'Wv': jax.random.normal(ks[3], (D, D), dtype=jnp.float32) * scale, 'Wo': jax.random.normal(ks[4], (D, D), dtype=jnp.float32) * scale}
    _L0_attn_b_in = _L0_attn_b_setup()

    def _L0_ffn_setup():
        import jax, jax.numpy as jnp
        import numpy as np
        H = 256
        NH = 32
        KVH = 4
        HD = 128
        E = 32
        TOPK = 8
        I = 128
        EPS = 1e-05
        THETA = 10000.0

        def _rmsnorm(x, w, eps=EPS):
            xf = x.astype(jnp.float32)
            var = jnp.mean(xf * xf, axis=-1, keepdims=True)
            return (w * (xf * jax.lax.rsqrt(var + eps))).astype(x.dtype)

        def _rope(x, pos):
            d = x.shape[-1]
            inv_freq = 1.0 / THETA ** (jnp.arange(0, d, 2, dtype=jnp.float32) / d)
            ang = pos.astype(jnp.float32)[:, None] * inv_freq[None, :]
            cos = jnp.cos(ang)[None, :, None, :]
            sin = jnp.sin(ang)[None, :, None, :]
            x1, x2 = jnp.split(x, 2, axis=-1)
            return jnp.concatenate([x1 * cos - x2 * sin, x1 * sin + x2 * cos], axis=-1)
        key = jax.random.key(seed)
        ks = jax.random.split(key, 16)
        s = 0.02
        n = lambda k, shape: jax.random.normal(k, shape, dtype=jnp.float32) * s
        return {'hidden_states': jax.random.normal(ks[0], (1, 64, H), dtype=jnp.float32), 'ln1_w': jnp.ones((H,), jnp.float32), 'ln2_w': jnp.ones((H,), jnp.float32), 'Wq': n(ks[1], (H, NH * HD)), 'Wk': n(ks[2], (H, KVH * HD)), 'Wv': n(ks[3], (H, KVH * HD)), 'Wo': n(ks[4], (NH * HD, H)), 'Wr': n(ks[5], (H, E)), 'expert_bias': jax.random.normal(ks[6], (E,), dtype=jnp.float32) * 0.1, 'Wg': n(ks[7], (E, H, I)), 'Wu': n(ks[8], (E, H, I)), 'Wd': n(ks[9], (E, I, H)), 'Wsg': n(ks[10], (H, I)), 'Wsu': n(ks[11], (H, I)), 'Wsd': n(ks[12], (I, H))}
    _L0_ffn_in = _L0_ffn_setup()
    _d = {'L0_attn_a_hidden_states': _L0_attn_a_in['hidden_states'], 'L0_attn_a_W_DKV': _L0_attn_a_in['W_DKV'], 'L0_attn_a_b_DKV': _L0_attn_a_in['b_DKV'], 'L0_attn_a_W_UK': _L0_attn_a_in['W_UK'], 'L0_attn_a_b_UK': _L0_attn_a_in['b_UK'], 'L0_attn_a_W_UV': _L0_attn_a_in['W_UV'], 'L0_attn_a_b_UV': _L0_attn_a_in['b_UV'], 'L0_attn_a_W_DQ': _L0_attn_a_in['W_DQ'], 'L0_attn_a_b_DQ': _L0_attn_a_in['b_DQ'], 'L0_attn_a_W_UQ': _L0_attn_a_in['W_UQ'], 'L0_attn_a_b_UQ': _L0_attn_a_in['b_UQ'], 'L0_attn_a_W_QR': _L0_attn_a_in['W_QR'], 'L0_attn_a_W_KR': _L0_attn_a_in['W_KR'], 'L0_attn_a_W_O': _L0_attn_a_in['W_O'], 'L0_attn_a_b_O': _L0_attn_a_in['b_O'], 'L0_attn_b_Wq': _L0_attn_b_in['Wq'], 'L0_attn_b_Wk': _L0_attn_b_in['Wk'], 'L0_attn_b_Wv': _L0_attn_b_in['Wv'], 'L0_attn_b_Wo': _L0_attn_b_in['Wo'], 'L0_ffn_ln1_w': _L0_ffn_in['ln1_w'], 'L0_ffn_ln2_w': _L0_ffn_in['ln2_w'], 'L0_ffn_Wq': _L0_ffn_in['Wq'], 'L0_ffn_Wk': _L0_ffn_in['Wk'], 'L0_ffn_Wv': _L0_ffn_in['Wv'], 'L0_ffn_Wo': _L0_ffn_in['Wo'], 'L0_ffn_Wr': _L0_ffn_in['Wr'], 'L0_ffn_expert_bias': _L0_ffn_in['expert_bias'], 'L0_ffn_Wg': _L0_ffn_in['Wg'], 'L0_ffn_Wu': _L0_ffn_in['Wu'], 'L0_ffn_Wd': _L0_ffn_in['Wd'], 'L0_ffn_Wsg': _L0_ffn_in['Wsg'], 'L0_ffn_Wsu': _L0_ffn_in['Wsu'], 'L0_ffn_Wsd': _L0_ffn_in['Wsd']}
    _x0 = _d['L0_attn_a_hidden_states']
    _d['L0_attn_a_hidden_states'] = jax.random.normal(jax.random.fold_in(jax.random.key(seed), 1), (2, 512, 256), dtype=_x0.dtype)
    del _x0
    return _d

def reference(L0_attn_a_hidden_states, L0_attn_a_W_DKV, L0_attn_a_b_DKV, L0_attn_a_W_UK, L0_attn_a_b_UK, L0_attn_a_W_UV, L0_attn_a_b_UV, L0_attn_a_W_DQ, L0_attn_a_b_DQ, L0_attn_a_W_UQ, L0_attn_a_b_UQ, L0_attn_a_W_QR, L0_attn_a_W_KR, L0_attn_a_W_O, L0_attn_a_b_O, L0_attn_b_Wq, L0_attn_b_Wk, L0_attn_b_Wv, L0_attn_b_Wo, L0_ffn_ln1_w, L0_ffn_ln2_w, L0_ffn_Wq, L0_ffn_Wk, L0_ffn_Wv, L0_ffn_Wo, L0_ffn_Wr, L0_ffn_expert_bias, L0_ffn_Wg, L0_ffn_Wu, L0_ffn_Wd, L0_ffn_Wsg, L0_ffn_Wsu, L0_ffn_Wsd):

    def _L0_attn_a_ref(hidden_states, W_DKV, b_DKV, W_UK, b_UK, W_UV, b_UV, W_DQ, b_DQ, W_UQ, b_UQ, W_QR, W_KR, W_O, b_O):
        import jax, jax.numpy as jnp
        import numpy as np
        B, S = (1, 512)
        HID, H, D = (256, 16, 128)
        KVC, QC, RD = (64, 192, 64)
        THETA = 10000.0

        def _mla_forward(hidden_states, W_DKV, b_DKV, W_UK, b_UK, W_UV, b_UV, W_DQ, b_DQ, W_UQ, b_UQ, W_QR, W_KR, W_O, b_O):
            b, s, _ = hidden_states.shape
            c_kv = hidden_states @ W_DKV + b_DKV
            k = (c_kv @ W_UK + b_UK).reshape(b, s, H, D)
            v = (c_kv @ W_UV + b_UV).reshape(b, s, H, D)
            c_q = hidden_states @ W_DQ + b_DQ
            q = (c_q @ W_UQ + b_UQ).reshape(b, s, H, D)
            half = RD // 2
            inv_freq = 1.0 / THETA ** (jnp.arange(0, RD, 2, dtype=jnp.float32) / RD)
            t = jnp.arange(s, dtype=jnp.float32)
            freqs = t[:, None] * inv_freq[None, :]
            cos = jnp.cos(freqs)[None, :, None, :]
            sin = jnp.sin(freqs)[None, :, None, :]
            q_r = q @ W_QR
            k_r = k @ W_KR

            def rope(x):
                x1, x2 = (x[..., :half], x[..., half:])
                first = x1 * cos - x2 * sin
                return jnp.concatenate([first, jnp.zeros_like(first)], axis=-1)
            q = q.at[..., :RD].set(rope(q_r))
            k = k.at[..., :RD].set(rope(k_r))
            scores = jnp.einsum('bqhd,bkhd->bhqk', q, k) / jnp.sqrt(jnp.float32(D))
            probs = jax.nn.softmax(scores, axis=-1)
            ctx = jnp.einsum('bhqk,bkhd->bqhd', probs, v).reshape(b, s, H * D)
            return ctx @ W_O + b_O
        return _mla_forward(hidden_states, W_DKV, b_DKV, W_UK, b_UK, W_UV, b_UV, W_DQ, b_DQ, W_UQ, b_UQ, W_QR, W_KR, W_O, b_O)

    def _L0_attn_b_ref(x, Wq, Wk, Wv, Wo):
        import jax, jax.numpy as jnp
        import numpy as np
        NH = 16
        B, T, D = x.shape
        hd = D // NH
        q = (x @ Wq.T).reshape(B, T, NH, hd).transpose(0, 2, 1, 3)
        k = (x @ Wk.T).reshape(B, T, NH, hd).transpose(0, 2, 1, 3)
        v = (x @ Wv.T).reshape(B, T, NH, hd).transpose(0, 2, 1, 3)
        att = jnp.einsum('bhtd,bhsd->bhts', q, k) / jnp.sqrt(jnp.asarray(hd, x.dtype))
        neg = jnp.finfo(att.dtype).min
        mask = jnp.triu(jnp.full((T, T), neg, dtype=att.dtype), k=1)
        att = att + mask
        w = jax.nn.softmax(att, axis=-1)
        z = jnp.einsum('bhts,bhsd->bhtd', w, v)
        z = z.transpose(0, 2, 1, 3).reshape(B, T, D)
        return z @ Wo.T

    def _L0_ffn_ref(hidden_states, ln1_w, ln2_w, Wq, Wk, Wv, Wo, Wr, expert_bias, Wg, Wu, Wd, Wsg, Wsu, Wsd):
        import jax, jax.numpy as jnp
        import numpy as np
        H = 256
        NH = 32
        KVH = 4
        HD = 128
        E = 32
        TOPK = 8
        I = 128
        EPS = 1e-05
        THETA = 10000.0

        def _rmsnorm(x, w, eps=EPS):
            xf = x.astype(jnp.float32)
            var = jnp.mean(xf * xf, axis=-1, keepdims=True)
            return (w * (xf * jax.lax.rsqrt(var + eps))).astype(x.dtype)

        def _rope(x, pos):
            d = x.shape[-1]
            inv_freq = 1.0 / THETA ** (jnp.arange(0, d, 2, dtype=jnp.float32) / d)
            ang = pos.astype(jnp.float32)[:, None] * inv_freq[None, :]
            cos = jnp.cos(ang)[None, :, None, :]
            sin = jnp.sin(ang)[None, :, None, :]
            x1, x2 = jnp.split(x, 2, axis=-1)
            return jnp.concatenate([x1 * cos - x2 * sin, x1 * sin + x2 * cos], axis=-1)
        B, S, _ = hidden_states.shape
        resid = hidden_states
        h = _rmsnorm(hidden_states, ln1_w)
        pos = jnp.arange(S)
        q = (h @ Wq).reshape(B, S, NH, HD)
        k = (h @ Wk).reshape(B, S, KVH, HD)
        v = (h @ Wv).reshape(B, S, KVH, HD)
        q = _rope(q, pos)
        k = _rope(k, pos)
        rep = NH // KVH
        k = jnp.repeat(k, rep, axis=2)
        v = jnp.repeat(v, rep, axis=2)
        scores = jnp.einsum('bqhd,bkhd->bhqk', q, k) / jnp.sqrt(jnp.float32(HD))
        causal = jnp.tril(jnp.ones((S, S), dtype=bool))
        scores = jnp.where(causal[None, None], scores, jnp.float32(-1000000000.0))
        attn = jax.nn.softmax(scores, axis=-1)
        o = jnp.einsum('bhqk,bkhd->bqhd', attn, v).reshape(B, S, NH * HD) @ Wo
        x = resid + o
        resid = x
        h = _rmsnorm(x, ln2_w)
        t = h.reshape(-1, H)
        T = t.shape[0]
        router_scores = jax.nn.sigmoid(t @ Wr)
        _, idx = jax.lax.top_k(router_scores + expert_bias[None, :], TOPK)
        w = jnp.take_along_axis(router_scores, idx, axis=1)
        w = w / jnp.sum(w, axis=-1, keepdims=True)
        wfull = jnp.zeros((T, E), jnp.float32).at[jnp.arange(T)[:, None], idx].set(w)
        g = jnp.einsum('th,ehi->tei', t, Wg)
        u = jnp.einsum('th,ehi->tei', t, Wu)
        act = jax.nn.silu(g) * u
        moe = jnp.einsum('tei,te,eih->th', act, wfull, Wd)
        shared = jax.nn.silu(t @ Wsg) * (t @ Wsu) @ Wsd
        return resid + (moe + shared).reshape(B, S, H)
    x = L0_attn_a_hidden_states
    x = x + _L0_attn_a_ref(_layernorm(x, axis=-1), L0_attn_a_W_DKV, L0_attn_a_b_DKV, L0_attn_a_W_UK, L0_attn_a_b_UK, L0_attn_a_W_UV, L0_attn_a_b_UV, L0_attn_a_W_DQ, L0_attn_a_b_DQ, L0_attn_a_W_UQ, L0_attn_a_b_UQ, L0_attn_a_W_QR, L0_attn_a_W_KR, L0_attn_a_W_O, L0_attn_a_b_O)
    x = x + _L0_ffn_ref(_layernorm(x, axis=-1), L0_ffn_ln1_w, L0_ffn_ln2_w, L0_ffn_Wq, L0_ffn_Wk, L0_ffn_Wv, L0_ffn_Wo, L0_ffn_Wr, L0_ffn_expert_bias, L0_ffn_Wg, L0_ffn_Wu, L0_ffn_Wd, L0_ffn_Wsg, L0_ffn_Wsu, L0_ffn_Wsd)
    x = x + _L0_attn_b_ref(_layernorm(x, axis=-1), L0_attn_b_Wq, L0_attn_b_Wk, L0_attn_b_Wv, L0_attn_b_Wo)
    x = x + _L0_ffn_ref(_layernorm(x, axis=-1), L0_ffn_ln1_w, L0_ffn_ln2_w, L0_ffn_Wq, L0_ffn_Wk, L0_ffn_Wv, L0_ffn_Wo, L0_ffn_Wr, L0_ffn_expert_bias, L0_ffn_Wg, L0_ffn_Wu, L0_ffn_Wd, L0_ffn_Wsg, L0_ffn_Wsu, L0_ffn_Wsd)
    return x

_drawn_inputs = setup_inputs


def setup_inputs(seed=0):
    import zlib

    import numpy as np

    out = dict(_drawn_inputs(seed))
    spreads = {'L0_attn_a_b_DKV': (0.0, 0.54),
     'L0_attn_a_b_UK': (0.0, 0.8),
     'L0_attn_a_b_UV': (0.0, 0.1),
     'L0_attn_a_b_DQ': (0.0, 0.8),
     'L0_attn_a_b_UQ': (0.0, 0.8),
     'L0_attn_a_b_O': (0.0, 0.1),
     'L0_ffn_ln1_w': (1.0, 0.6),
     'L0_ffn_ln2_w': (1.0, 0.6)}
    factors = {'L0_attn_a_W_DKV': 8.0,
     'L0_attn_a_W_UK': 8.0,
     'L0_attn_a_W_UV': 3.842,
     'L0_attn_a_W_DQ': 8.0,
     'L0_attn_a_W_UQ': 8.0,
     'L0_attn_a_W_QR': 8.0,
     'L0_attn_a_W_KR': 8.0,
     'L0_attn_b_Wq': 8.0,
     'L0_attn_b_Wk': 8.0,
     'L0_attn_b_Wv': 6.125,
     'L0_attn_b_Wo': 6.181,
     'L0_ffn_Wq': 8.0,
     'L0_ffn_Wk': 8.0,
     'L0_ffn_Wr': 8.0,
     'L0_ffn_expert_bias': 8.0,
     'L0_ffn_Wg': 8.0,
     'L0_ffn_Wu': 8.0,
     'L0_ffn_Wd': 8.0,
     'L0_ffn_Wsg': 5.12,
     'L0_ffn_Wsu': 4.946,
     'L0_ffn_Wsd': 5.007}
    for name, (base, spread) in spreads.items():
        noise = np.random.default_rng([zlib.crc32(name.encode()), seed]).standard_normal(out[name].shape)
        drawn = base * np.exp(spread * noise) if base else spread * noise
        out[name] = jnp.asarray(drawn.astype(out[name].dtype))
    for name, factor in factors.items():
        out[name] = (out[name] * factor).astype(out[name].dtype)
    return out
```

```python
from contextlib import ExitStack

import numpy as np

import concourse.bass as bass
from concourse import mybir

F32 = mybir.dt.float32
F32R = mybir.dt.float32r
BF16 = mybir.dt.bfloat16
ALU = mybir.AluOpType
ACT = mybir.ActivationFunctionType
AX_X = mybir.AxisListType.X

P = 128
BATCH, SEQ, HID = 2, 512, 256
TOK = BATCH * SEQ
TILES = TOK // P
KT = HID // P
QT = SEQ // P
LN_EPS = 1e-5
RMS_EPS = 1e-5
THETA = 10000.0


class Count:

    def __init__(self, sem, credits=0):
        self.sem = sem
        self.credits = credits

    def open(self, eng):
        eng.sem_inc(self.sem, self.credits)

    def at(self, n):
        if isinstance(n, int):
            n = max(n, 0)
        return n + self.credits


def split_product(pe, out, w, x, start, stop):
    pe.matmul(out, w[0], x[0], start=start, stop=False, skip_group_check=True)
    pe.matmul(out, w[1], x[0], start=False, stop=False, skip_group_check=True)
    return pe.matmul(out, w[0], x[1], start=False, stop=stop, skip_group_check=True)


class Chip:

    def __init__(self, nc, ctx, dram, out):
        self.nc, self.ctx, self.dram, self.out = nc, ctx, dram, out
        self.phase_sems = []
        self.x = self.sb(ctx, "x_resid", [P, TILES, HID])
        self.ident = self.sb(ctx, "ident_sb", [P, P])
        self.hT = self.sb(ctx, "hT", [P, KT, TOK])
        self.hT_hi = self.sb(ctx, "hT_hi", [P, KT, TOK], F32R)
        self.hT_lo = self.sb(ctx, "hT_lo", [P, KT, TOK], F32R)

    def sb(self, ctx, name, shape, dt=F32):
        return ctx.enter_context(self.nc.sbuf_tensor(name, shape, dt))

    def ps(self, ctx, name, shape=(P, 512), dt=F32):
        return ctx.enter_context(self.nc.psum_tensor(name, list(shape), dt))

    def sem(self, ctx, name, credits=0):
        sem = self.nc.alloc_semaphore(name)
        self.phase_sems.append(sem)
        if len(self.phase_sems) == 1:
            ctx.callback(self.clear_sems)
        return Count(sem, credits)

    def clear_sems(self):
        self.nc.clear_and_free_semaphores(self.phase_sems)
        self.nc.all_engine_barrier()
        self.phase_sems = []


def load_phase(c):
    with ExitStack() as ctx:
        loaded = c.sem(ctx, "ld_loaded")
        with c.nc.Block() as block:
            @block.sync
            def _(sp):
                sp.dma_start(c.x[:, :, :], c.dram["L0_attn_a_hidden_states"].rearrange(
                    "b (t p) h -> p (b t) h", p=P)).then_inc(loaded.sem, 16)
                sp.dma_start(c.ident[:, :], c.dram["ident"]).then_inc(loaded.sem, 16)
                sp.wait_ge(loaded.sem, loaded.at(32))


def store_phase(c):
    with ExitStack() as ctx:
        stored = c.sem(ctx, "st_stored")
        with c.nc.Block() as block:
            @block.sync
            def _(sp):
                sp.dma_start(c.out.rearrange("b (t p) h -> p (b t) h", p=P),
                             c.x[:, :, :]).then_inc(stored.sem, 16)
                sp.wait_ge(stored.sem, stored.at(16))


def norm_phase(c, name, src, rms, dst=None, weight=None, split=True, transpose=True):
    nc = c.nc
    with ExitStack() as ctx:
        sb = lambda n, s: c.sb(ctx, f"{name}_{n}", s)
        sem = lambda n: c.sem(ctx, f"{name}_{n}")
        stats = sb("stats", [P, TILES, 6])
        mv = sb("mv", [P, TILES, 2])
        ms = sb("ms", [P, TILES])
        sd = sb("sd", [P, TILES])
        rstd = sb("rstd", [P, TILES])
        xn = dst if dst is not None else sb("xn", [P, TILES, HID])
        wcol = sb("wcol", [P, KT]) if weight is not None else None
        banks = [c.ps(ctx, f"{name}_T{n}") for n in range(4)]
        weighed, stat, aggr, msq, shifted, rooted, inverted, normed = [sem(n) for n in (
            "weighed", "stat", "aggr", "msq", "shifted", "rooted", "inverted", "normed")]
        turned, evacuated, hi_done, lo_done = [sem(n) for n in ("turned", "evac", "hi", "lo")]

        with nc.Block() as block:
            @block.sync
            def _(sp):
                if weight is not None:
                    sp.dma_start(wcol[:, :], weight, allow_slow_non_contiguous=True).then_inc(weighed.sem, 16)

            @block.vector
            def _(dve):
                for t in range(TILES):
                    dve.bn_stats(stats[:, t, :], src[:, t, :]).then_inc(stat.sem, 1)
                for t in range(TILES):
                    dve.wait_ge(stat.sem, stat.at(t + 1))
                    dve.bn_aggr(mv[:, t, :], stats[:, t, :]).then_inc(aggr.sem, 1)
                dve.wait_ge(aggr.sem, aggr.at(TILES))
                if rms:
                    dve.tensor_tensor(ms[:, :], mv[:, :, 0], mv[:, :, 0], ALU.mult).then_inc(msq.sem, 1)
                    dve.wait_ge(msq.sem, msq.at(1))
                    dve.scalar_tensor_tensor(out=sd[:, :], in0=ms[:, :], scalar=RMS_EPS, in1=mv[:, :, 1],
                                             op0=ALU.add, op1=ALU.add).then_inc(shifted.sem, 1)
                else:
                    dve.tensor_scalar(sd[:, :], mv[:, :, 1], LN_EPS, None, ALU.add).then_inc(shifted.sem, 1)
                dve.wait_ge(rooted.sem, rooted.at(1))
                dve.reciprocal(rstd[:, :], sd[:, :]).then_inc(inverted.sem, 1)
                dve.wait_ge(inverted.sem, inverted.at(1))
                for t in range(TILES):
                    if rms:
                        ins = dve.tensor_scalar(xn[:, t, :], src[:, t, :], rstd[:, t:t + 1], None, ALU.mult)
                    else:
                        ins = dve.tensor_scalar(xn[:, t, :], src[:, t, :], mv[:, t, 0:1], rstd[:, t:t + 1],
                                                ALU.subtract, ALU.mult)
                    ins.then_inc(normed.sem, 1)
                if not transpose:
                    return
                if weight is not None:
                    dve.wait_ge(weighed.sem, weighed.at(16))
                for n in range(4):
                    dve.wait_ge(turned.sem, turned.at(n + 1))
                    part = c.hT[:, n % 2, n // 2 * 512:n // 2 * 512 + 512]
                    if weight is not None:
                        ins = dve.tensor_scalar(part, banks[n][:, :], wcol[:, n % 2:n % 2 + 1], None, ALU.mult)
                    else:
                        ins = dve.tensor_copy(part, banks[n][:, :])
                    ins.then_inc(evacuated.sem, 1)
                for n in range(4 if split else 0):
                    dve.wait_ge(hi_done.sem, hi_done.at(n + 1))
                    dve.wait_ge(evacuated.sem, evacuated.at(n + 1))
                    at = (slice(None), n % 2, slice(n // 2 * 512, n // 2 * 512 + 512))
                    dve.tensor_tensor(c.hT_lo[at], c.hT[at], c.hT_hi[at].bitcast(F32),
                                      ALU.subtract).then_inc(lo_done.sem, 1)

            @block.scalar
            def _(act):
                act.wait_ge(shifted.sem, shifted.at(1))
                act.activation(sd[:, :], sd[:, :], ACT.Sqrt).then_inc(rooted.sem, 1)
                for n in range(4 if split and transpose else 0):
                    act.wait_ge(evacuated.sem, evacuated.at(n + 1))
                    at = (slice(None), n % 2, slice(n // 2 * 512, n // 2 * 512 + 512))
                    act.copy(c.hT_hi[at], c.hT[at]).then_inc(hi_done.sem, 1)

            @block.tensor
            def _(pe):
                for n in range(4 if transpose else 0):
                    half, kt = n // 2, n % 2
                    pe.wait_ge(normed.sem, normed.at(4 * half + 4))
                    for t in range(4):
                        ins = pe.transpose(banks[n][:, t * P:(t + 1) * P],
                                           xn[:, 4 * half + t, kt * P:(kt + 1) * P], c.ident[:, :])
                    ins.then_inc(turned.sem, 1)



class Attention:

    def __init__(self, c, ctx, name, causal):
        self.c, self.causal = c, causal
        sb = lambda n, s, dt=F32: c.sb(ctx, f"{name}_{n}", s, dt)
        sem = lambda n, k=0: c.sem(ctx, f"{name}_{n}", k)
        self.S = [c.ps(ctx, f"{name}_S{n}") for n in range(2)]
        self.T = [c.ps(ctx, f"{name}_T{n}") for n in range(2)]
        self.O = c.ps(ctx, f"{name}_O")
        self.prob = [sb(f"prob{n}", [P, QT, SEQ]) for n in range(2)]
        self.pt_hi = [sb(f"pt_hi{n}", [P, QT, SEQ], F32R) for n in range(2)]
        self.pt_lo = [sb(f"pt_lo{n}", [P, QT, SEQ], F32R) for n in range(2)]
        self.negmax = sb("negmax", [P, 2 * QT])
        self.rowsum = sb("rowsum", [P, 2 * QT])
        self.rinv = sb("rinv", [P, 2 * QT])
        self.scored, self.maxed, self.exped, self.inverted = sem("scored", 4), sem("maxed"), sem("exped", 4), sem("inverted")
        self.normed, self.turned = sem("normed"), sem("turned", 8)
        self.pt_hi_done, self.pt_lo_done = sem("pt_hi_done"), sem("pt_lo_done", 2)
        self.pv_done, self.o_hi_done, self.o_lo_done = sem("pv_done", 3), sem("o_hi_done"), sem("o_lo_done", 3)
        self.cleared = sem("cleared")

    def width(self, t):
        return max(256, P * (t + 1)) if self.causal else SEQ

    def used(self, t):
        return P * (t + 1) if self.causal else SEQ

    def scores(self, pe, u, par, t, q, k, mask=None):
        e = 4 * u + t
        bank = self.S[t % 2]
        pe.wait_ge(self.exped.sem, self.exped.at(e - 1))
        w = self.width(t)
        ins = split_product(pe, bank[:, 0:w], q, (k[0][:, 0:w], k[1][:, 0:w]), True, mask is None)
        if mask is not None:
            ins = pe.matmul(bank[:, t * P:(t + 1) * P], mask[0], mask[1], start=False, stop=True, skip_group_check=True)
        ins.then_inc(self.scored.sem, 1)

    def maximum(self, dve, u, par, t):
        dve.wait_ge(self.scored.sem, self.scored.at(4 * u + t + 1))
        dve.tensor_reduce(self.negmax[:, 4 * par + t:4 * par + t + 1], self.S[t % 2][:, 0:self.used(t)], AX_X, ALU.max,
                          negate=True).then_inc(self.maxed.sem, 1)

    def exp(self, act, u, par, t, bias=None):
        e = 4 * u + t
        n = slice(4 * par + t, 4 * par + t + 1)
        if bias is None:
            act.wait_ge(self.maxed.sem, self.maxed.at(e + 1))
            bias = self.negmax
        act.wait_ge(self.turned.sem, self.turned.at(e - 7))
        act.activation(self.prob[par][:, t, 0:self.used(t)], self.S[t % 2][:, 0:self.used(t)], ACT.Exp, bias=bias[:, n],
                       accum_out=self.rowsum[:, n]).then_inc(self.exped.sem, 1)

    def invert(self, dve, u, par, t):
        dve.wait_ge(self.exped.sem, self.exped.at(4 * u + t + 1))
        n = slice(4 * par + t, 4 * par + t + 1)
        dve.reciprocal(self.rinv[:, n], self.rowsum[:, n]).then_inc(self.inverted.sem, 1)

    def normalise(self, pool, u, par, t):
        pool.wait_ge(self.inverted.sem, self.inverted.at(4 * u + t + 1))
        n = slice(4 * par + t, 4 * par + t + 1)
        w = self.used(t)
        part = self.prob[par][:, t, 0:w]
        pool.tensor_tensor(part, part, self.rinv[:, n].broadcast_to([P, w]), ALU.mult).then_inc(self.normed.sem, 1)

    def turn(self, pe, u, par, t):
        e = 4 * u + t
        pe.wait_ge(self.normed.sem, self.normed.at(e + 1))
        pe.wait_ge(self.pt_lo_done.sem, self.pt_lo_done.at(e - 1))
        for kt in range(self.used(t) // P):
            ins = pe.transpose(self.T[t % 2][:, kt * P:(kt + 1) * P], self.prob[par][:, t, kt * P:(kt + 1) * P],
                               self.c.ident[:, :])
        ins.then_inc(self.turned.sem, 1)

    def turned_part(self, dst, t):
        n = self.used(t) // P
        return dst[:, 0:n, t * P:(t + 1) * P], self.T[t % 2][:, 0:n * P].rearrange("p (k q) -> p k q", q=P)

    def split_hi(self, act, u, par, t):
        act.wait_ge(self.turned.sem, self.turned.at(4 * u + t + 1))
        act.wait_ge(self.pv_done.sem, self.pv_done.at(u - 1))
        dst, src = self.turned_part(self.pt_hi[par], t)
        act.copy(dst, src).then_inc(self.pt_hi_done.sem, 1)

    def split_lo(self, dve, u, par, t):
        dve.wait_ge(self.pt_hi_done.sem, self.pt_hi_done.at(4 * u + t + 1))
        dst, src = self.turned_part(self.pt_lo[par], t)
        hi, _ = self.turned_part(self.pt_hi[par], t)
        dve.tensor_tensor(dst, src, hi.bitcast(F32), ALU.subtract).then_inc(self.pt_lo_done.sem, 1)

    def values(self, pe, u, par, kts, v, start=True, stop=True):
        pe.wait_ge(self.pt_lo_done.sem, self.pt_lo_done.at(4 * u + 4))
        for kt in kts:
            q0 = min(kt * P, SEQ - 256) if self.causal else 0
            ins = split_product(pe, self.O[:, q0:SEQ], v(kt),
                                (self.pt_hi[par][:, kt, q0:SEQ], self.pt_lo[par][:, kt, q0:SEQ]),
                                start and kt == 0, stop and kt == QT - 1)
        if kts[-1] == QT - 1:
            ins.then_inc(self.pv_done.sem, 1)

    def step_act(self, act, u, par, t, more):
        self.split_hi(act, u, par, t)
        if more:
            self.exp(act, u + 1, 1 - par, t)

    def step_dve(self, dve, u, par, t, more):
        if more:
            self.maximum(dve, u + 1, 1 - par, t)
        self.split_lo(dve, u, par, t)
        if more:
            self.invert(dve, u + 1, 1 - par, t)

    def open(self, eng, which):
        for s in {"pe": (self.scored, self.turned, self.pv_done), "act": (self.exped,),
                  "dve": (self.pt_lo_done, self.o_lo_done)}[which]:
            s.open(eng)

    def clear_unseen(self, dve):
        for part in (*self.pt_hi, *self.pt_lo):
            dve.memset(part[:, QT - 1, 256:384].bitcast(F32), 0.0).then_inc(self.cleared.sem, 1)


MLA_HEADS, MLA_D, KV_LAT, Q_LAT, ROPE = 16, 128, 64, 192, 64
Q_LAT_HALF = Q_LAT // 2
MLA_UNITS = MLA_HEADS * BATCH


def mla_latents(c, ctx_outer, name, ckv, cq):
    nc = c.nc
    with ExitStack() as ctx:
        sb = lambda n, s, dt=F32: c.sb(ctx, f"{name}_{n}", s, dt)
        sem = lambda n, k=0: c.sem(ctx, f"{name}_{n}", k)
        wkv, wq = sb("wkv", [P, KT, KV_LAT]), sb("wq", [P, KT, Q_LAT])
        bkv, bq = sb("bkv", [KV_LAT, 1]), sb("bq", [Q_LAT_HALF, 2])
        banks = [c.ps(ctx, f"{name}_L{n}") for n in range(6)]
        loaded, ones, projected, full_done, hi_done, lo_done = [sem(n) for n in (
            "loaded", "ones", "projected", "full", "hi", "lo")]
        parts = [(KV_LAT, lambda kt: wkv[:, kt, :], bkv[:, 0:1], lambda x, s: x[0:KV_LAT, s]),
                 (Q_LAT_HALF, lambda kt: wq[:, kt, 0:Q_LAT_HALF], bq[:, 0:1], lambda x, s: x[0:Q_LAT_HALF, 0, s]),
                 (Q_LAT_HALF, lambda kt: wq[:, kt, Q_LAT_HALF:Q_LAT], bq[:, 1:2], lambda x, s: x[0:Q_LAT_HALF, 1, s])]
        work = [(b, n) for b in range(BATCH) for n in range(3)]
        outs = (ckv, cq, cq)
        with nc.Block() as block:
            @block.sync
            def _(sp):
                d = lambda n: c.dram["L0_attn_a_" + n]
                sp.dma_start(wkv[:, :, :], d("W_DKV").rearrange("(k p) m -> p k m", p=P)).then_inc(loaded.sem, 16)
                sp.dma_start(wq[:, :, :], d("W_DQ").rearrange("(k p) m -> p k m", p=P)).then_inc(loaded.sem, 16)
                sp.dma_start(bkv[:, :], d("b_DKV").rearrange("(p o) -> p o", o=1)).then_inc(loaded.sem, 16)
                sp.dma_start(bq[:, :], d("b_DQ").rearrange("(k p) -> p k", p=Q_LAT_HALF),
                             allow_slow_non_contiguous=True).then_inc(loaded.sem, 16)

            @block.tensor
            def _(pe):
                pe.wait_ge(loaded.sem, loaded.at(64))
                for i, (b, n) in enumerate(work):
                    rows, w, _, _ = parts[n]
                    for kt in range(KT):
                        ins = pe.matmul(banks[i][0:rows, :], w(kt), c.hT[:, kt, b * SEQ:(b + 1) * SEQ],
                                        start=kt == 0, stop=kt == KT - 1)
                    ins.then_inc(projected.sem, 1)

            @block.vector
            def _(dve):
                dve.memset(ckv[0][KV_LAT:KV_LAT + 1, :].bitcast(F32), 1.0).then_inc(ones.sem, 1)
                dve.memset(ckv[1][KV_LAT:KV_LAT + 1, :].bitcast(F32), 0.0).then_inc(ones.sem, 1)
                dve.memset(ckv[2][KV_LAT:KV_LAT + 1, :], 1.0).then_inc(ones.sem, 1)
                for x in cq[0:2]:
                    dve.memset(x[Q_LAT_HALF:Q_LAT_HALF + 1, :, :].bitcast(F32), 0.0).then_inc(ones.sem, 1)
                dve.wait_ge(ones.sem, ones.at(5))
                dve.memset(cq[0][Q_LAT_HALF:Q_LAT_HALF + 1, 1, :].bitcast(F32), 1.0).then_inc(ones.sem, 1)
                dve.wait_ge(loaded.sem, loaded.at(64))
                for i, (b, n) in enumerate(work):
                    rows, _, bias, at = parts[n]
                    dve.wait_ge(projected.sem, projected.at(i + 1))
                    dve.tensor_scalar(at(outs[n][2], slice(b * SEQ, (b + 1) * SEQ)), banks[i][0:rows, :], bias, None,
                                      ALU.add).then_inc(full_done.sem, 1)
                    dve.wait_ge(hi_done.sem, hi_done.at(i + 1))
                    dve.wait_ge(full_done.sem, full_done.at(i + 1))
                    hi, lo, full = [at(outs[n][k], slice(b * SEQ, (b + 1) * SEQ)) for k in range(3)]
                    dve.tensor_tensor(lo, full, hi.bitcast(F32), ALU.subtract).then_inc(lo_done.sem, 1)

            @block.scalar
            def _(act):
                for i, (b, n) in enumerate(work):
                    act.wait_ge(full_done.sem, full_done.at(i + 1))
                    hi, lo, full = [parts[n][3](outs[n][k], slice(b * SEQ, (b + 1) * SEQ)) for k in range(3)]
                    act.copy(hi, full).then_inc(hi_done.sem, 1)


def mla_phase(c, name):
    nc = c.nc
    SCALE = 1.0 / float(np.sqrt(MLA_D))
    with ExitStack() as ctx:
        sb = lambda n, s, dt=F32: c.sb(ctx, f"{name}_{n}", s, dt)
        sem = lambda n, k=0: c.sem(ctx, f"{name}_{n}", k)
        R2, H1 = KV_LAT + 1, Q_LAT_HALF + 1
        ckv = [sb("ckv_hi", [R2, TOK], F32R), sb("ckv_lo", [R2, TOK], F32R), sb("ckv", [R2, TOK])]
        cq = [sb("cq_hi", [H1, 2, TOK], F32R), sb("cq_lo", [H1, 2, TOK], F32R), sb("cq", [H1, 2, TOK])]
        mla_latents(c, ctx, name + "l", ckv, cq)

        a = Attention(c, ctx, name, causal=False)
        acc = c.ps(ctx, f"{name}_acc")
        X = [c.ps(ctx, f"{name}_X{n}") for n in range(2)]
        kcos, ksin, qrot = sb("kcos", [ROPE, SEQ]), sb("ksin", [ROPE, SEQ]), sb("qrot", [ROPE, SEQ])
        bo = sb("bo", [P, HID])
        wqr = [sb("wqr", [P, ROPE])] + [sb(f"wqr_{n}", [P, ROPE], F32R) for n in ("hi", "lo")]
        wkr = [sb("wkr", [P, 2 * ROPE])] + [sb(f"wkr_{n}", [P, 2 * ROPE], F32R) for n in ("hi", "lo")]
        uq = [sb("uq", [H1, 2, P])] + [sb(f"uq_{n}", [H1, 2, P], F32R) for n in ("hi", "lo")]
        uk = [sb("uk", [R2, P])] + [sb(f"uk_{n}", [R2, P], F32R) for n in ("hi", "lo")]
        uv = sb("uv", [R2, P])
        wo = [sb("wo", [P, HID])] + [sb(f"wo_{n}", [P, HID], F32R) for n in ("hi", "lo")]
        k_hi, k_lo, q_hi, q_lo = [[sb(f"{x}{n}", [P, SEQ], F32R) for n in range(2)] for x in (
            "k_hi", "k_lo", "q_hi", "q_lo")]
        v_hi, v_lo = [[sb(f"{x}{n}", [P, QT, P], F32R) for n in range(2)] for x in ("v_hi", "v_lo")]
        o_hi, o_lo = [[sb(f"{x}{n}", [P, SEQ], F32R) for n in range(2)] for x in ("o_hi", "o_lo")]
        kr_a, kr_b, kr_full, qr_full = [sb(n, [ROPE, SEQ]) for n in ("kr_a", "kr_b", "kr_full", "qr_full")]

        tables, once_hi, once_lo, based = sem("tables"), sem("once_hi"), sem("once_lo"), sem("based")
        uqk_in, uv_in, wo_in = sem("uqk_in"), sem("uv_in"), sem("wo_in")
        uqk_hi_done, uqk_lo_done, wo_hi_done, wo_lo_done = [sem(n) for n in (
            "uqk_hi_done", "uqk_lo_done", "wo_hi_done", "wo_lo_done")]
        k_projected, k_hi_done, k_lo_done, kr_projected, kr_turned, kr_sum, kr_hi_done, kr_lo_done = [sem(n) for n in (
            "k_projected", "k_hi_done", "k_lo_done", "kr_projected", "kr_turned", "kr_sum", "kr_hi_done",
            "kr_lo_done")]
        q_projected, q_hi_done, q_lo_done, qr_projected, qr_turned, qr_hi_done, qr_lo_done = [sem(n) for n in (
            "q_projected", "q_hi_done", "q_lo_done", "qr_projected", "qr_turned", "qr_hi_done", "qr_lo_done")]
        v_projected, v_hi_done, v_lo_done = sem("v_projected"), sem("v_hi_done"), sem("v_lo_done")
        out_done, added = sem("out_done", 3), sem("added", 4)

        def keys_pe(pe, h, b):
            n = 2 * h + b
            pe.wait_ge(uqk_lo_done.sem, uqk_lo_done.at(h + 1))
            pe.wait_ge(qr_turned.sem, qr_turned.at(n))
            split_product(pe, X[0][:, :], (uk[1][:, :], uk[2][:, :]),
                          (ckv[0][:, b * SEQ:(b + 1) * SEQ], ckv[1][:, b * SEQ:(b + 1) * SEQ]), True, True
                          ).then_inc(k_projected.sem, 1)

        def keys_act(act, h, b):
            n = 2 * h + b
            act.wait_ge(k_projected.sem, k_projected.at(n + 1))
            act.wait_ge(a.scored.sem, a.scored.at(4 * (n - 1)))
            act.copy(k_hi[b][:, :], X[0][:, :]).then_inc(k_hi_done.sem, 1)

        def keys_dve(dve, h, b):
            dve.wait_ge(k_hi_done.sem, k_hi_done.at(2 * h + b + 1))
            dve.tensor_tensor(k_lo[b][:, :], X[0][:, :], k_hi[b][:, :].bitcast(F32), ALU.subtract
                              ).then_inc(k_lo_done.sem, 1)

        def key_rope_pe(pe, h, b):
            pe.wait_ge(k_lo_done.sem, k_lo_done.at(2 * h + b + 1))
            split_product(pe, X[0][:, :], (wkr[1][:, :], wkr[2][:, :]), (k_hi[b][:, :], k_lo[b][:, :]), True, True
                          ).then_inc(kr_projected.sem, 1)

        def key_rope_dve(dve, h, b):
            n = 2 * h + b
            dve.wait_ge(kr_projected.sem, kr_projected.at(n + 1))
            dve.wait_ge(kr_sum.sem, kr_sum.at(n))
            dve.tensor_tensor(kr_a[:, :], X[0][0:ROPE, :], kcos[:, :], ALU.mult)
            dve.tensor_tensor(kr_b[:, :], X[0][ROPE:2 * ROPE, :], ksin[:, :], ALU.mult).then_inc(kr_turned.sem, 1)

        def key_rope_sum(pool, h, b):
            n = 2 * h + b
            pool.wait_ge(kr_turned.sem, kr_turned.at(n + 1))
            pool.wait_ge(kr_lo_done.sem, kr_lo_done.at(n))
            pool.tensor_tensor(kr_full[:, :], kr_a[:, :], kr_b[:, :], ALU.add).then_inc(kr_sum.sem, 1)

        def key_rope_act(act, h, b):
            act.wait_ge(kr_sum.sem, kr_sum.at(2 * h + b + 1))
            act.copy(k_hi[b][0:ROPE, :], kr_full[:, :]).then_inc(kr_hi_done.sem, 1)

        def key_rope_lo(pool, h, b):
            pool.wait_ge(kr_hi_done.sem, kr_hi_done.at(2 * h + b + 1))
            pool.tensor_tensor(k_lo[b][0:ROPE, :], kr_full[:, :], k_hi[b][0:ROPE, :].bitcast(F32), ALU.subtract
                               ).then_inc(kr_lo_done.sem, 1)

        def queries_pe(pe, h, b, values_before):
            pe.wait_ge(uqk_lo_done.sem, uqk_lo_done.at(h + 1))
            pe.wait_ge(v_lo_done.sem, v_lo_done.at(values_before))
            pe.wait_ge(q_lo_done.sem, q_lo_done.at(2 * h + b))
            for half in range(2):
                s = slice(b * SEQ, (b + 1) * SEQ)
                ins = split_product(pe, X[1][:, :], (uq[1][:, half, :], uq[2][:, half, :]),
                                    (cq[0][:, half, s], cq[1][:, half, s]), half == 0, half == 1)
            ins.then_inc(q_projected.sem, 1)

        def queries_act(act, h, b):
            n = 2 * h + b
            act.wait_ge(q_projected.sem, q_projected.at(n + 1))
            act.wait_ge(a.scored.sem, a.scored.at(4 * (n - 1)))
            act.activation(q_hi[b][:, :], X[1][:, :], ACT.Copy, scale=SCALE).then_inc(q_hi_done.sem, 1)

        def queries_dve(dve, h, b):
            dve.wait_ge(q_hi_done.sem, q_hi_done.at(2 * h + b + 1))
            dve.scalar_tensor_tensor(out=q_lo[b][:, :], in0=X[1][:, :], scalar=SCALE, in1=q_hi[b][:, :].bitcast(F32),
                                     op0=ALU.mult, op1=ALU.subtract).then_inc(q_lo_done.sem, 1)

        def query_rope_pe(pe, h, b):
            n = 2 * h + b
            pe.wait_ge(q_lo_done.sem, q_lo_done.at(n + 1))
            pe.wait_ge(kr_turned.sem, kr_turned.at(n + 1))
            split_product(pe, X[0][0:ROPE, :], (wqr[1][:, :], wqr[2][:, :]), (q_hi[b][:, :], q_lo[b][:, :]),
                          True, True).then_inc(qr_projected.sem, 1)

        def query_rope_dve(dve, h, b):
            n = 2 * h + b
            dve.wait_ge(qr_projected.sem, qr_projected.at(n + 1))
            dve.wait_ge(qr_lo_done.sem, qr_lo_done.at(n))
            dve.tensor_tensor(qr_full[:, :], X[0][0:ROPE, :], qrot[:, :], ALU.mult).then_inc(qr_turned.sem, 1)

        def query_rope_act(act, h, b):
            act.wait_ge(qr_turned.sem, qr_turned.at(2 * h + b + 1))
            act.copy(q_hi[b][0:ROPE, :], qr_full[:, :]).then_inc(qr_hi_done.sem, 1)

        def query_rope_lo(pool, h, b):
            pool.wait_ge(qr_hi_done.sem, qr_hi_done.at(2 * h + b + 1))
            pool.tensor_tensor(q_lo[b][0:ROPE, :], qr_full[:, :], q_hi[b][0:ROPE, :].bitcast(F32), ALU.subtract
                               ).then_inc(qr_lo_done.sem, 1)

        def values_make_pe(pe, h, b, queries_before):
            pe.wait_ge(uv_in.sem, uv_in.at(32 * (h + 1)))
            pe.wait_ge(q_lo_done.sem, q_lo_done.at(queries_before))
            pe.wait_ge(v_lo_done.sem, v_lo_done.at(2 * h + b))
            for t in range(QT):
                ins = pe.matmul(X[1][:, t * P:(t + 1) * P], ckv[2][:, b * SEQ + t * P:b * SEQ + (t + 1) * P],
                                uv[:, :], start=True, stop=True, skip_group_check=True)
            ins.then_inc(v_projected.sem, 1)

        def values_make_act(act, h, b):
            u = 2 * h + b
            act.wait_ge(v_projected.sem, v_projected.at(u + 1))
            act.wait_ge(a.pv_done.sem, a.pv_done.at(u - 1))
            act.copy(v_hi[b][:, :, :], X[1][:, :].rearrange("p (t d) -> p t d", d=P)).then_inc(v_hi_done.sem, 1)

        def values_make_dve(dve, h, b):
            dve.wait_ge(v_hi_done.sem, v_hi_done.at(2 * h + b + 1))
            dve.tensor_tensor(v_lo[b][:, :, :], X[1][:, :].rearrange("p (t d) -> p t d", d=P),
                              v_hi[b][:, :, :].bitcast(F32), ALU.subtract).then_inc(v_lo_done.sem, 1)

        def scores(pe, u, b, t):
            pe.wait_ge(kr_lo_done.sem, kr_lo_done.at(u + 1))
            pe.wait_ge(qr_lo_done.sem, qr_lo_done.at(u + 1))
            a.scores(pe, u, b, t, (q_hi[b][:, t * P:(t + 1) * P], q_lo[b][:, t * P:(t + 1) * P]),
                     (k_hi[b][:, :], k_lo[b][:, :]))

        def values(pe, u, b, kts):
            pe.wait_ge(v_lo_done.sem, v_lo_done.at(u + 1))
            if kts[0] == 0:
                pe.wait_ge(a.o_lo_done.sem, a.o_lo_done.at(u))
            a.values(pe, u, b, kts, lambda kt: (v_hi[b][:, kt, :], v_lo[b][:, kt, :]))

        def take_hi(act, u, b):
            act.wait_ge(a.pv_done.sem, a.pv_done.at(u + 1))
            act.wait_ge(out_done.sem, out_done.at(2 * u - 2))
            act.copy(o_hi[b][:, :], a.O[:, :]).then_inc(a.o_hi_done.sem, 1)

        def take_lo(dve, u, b):
            dve.wait_ge(a.o_hi_done.sem, a.o_hi_done.at(u + 1))
            dve.tensor_tensor(o_lo[b][:, :], a.O[:, :], o_hi[b][:, :].bitcast(F32), ALU.subtract
                              ).then_inc(a.o_lo_done.sem, 1)

        def out_half(pe, h, b, half):
            u = 2 * h + b
            pe.wait_ge(a.o_lo_done.sem, a.o_lo_done.at(u + 1))
            pe.wait_ge(wo_lo_done.sem, wo_lo_done.at(h + 1))
            pe.wait_ge(added.sem, added.at(2 * u + half))
            for t in range(2):
                q = slice((2 * half + t) * P, (2 * half + t + 1) * P)
                ins = split_product(pe, acc[:, t * HID:(t + 1) * HID], (o_hi[b][:, q], o_lo[b][:, q]),
                                    (wo[1][:, :], wo[2][:, :]), True, True)
            ins.then_inc(out_done.sem, 1)

        def add_half(dve, u, b, half):
            n = 2 * u + half
            dve.wait_ge(out_done.sem, out_done.at(n + 1))
            dve.wait_ge(added.sem, added.at(n - 3))
            part = c.x[:, 4 * b + 2 * half:4 * b + 2 * half + 2, :]
            dve.tensor_tensor(part, part, acc[:, :].rearrange("p (t h) -> p t h", h=HID), ALU.add
                              ).then_inc(added.sem, 1)

        def uqk_hi(act, h):
            act.wait_ge(uqk_in.sem, uqk_in.at(80 * (h + 1)))
            act.wait_ge(q_projected.sem, q_projected.at(2 * h))
            act.copy(uq[1][:, :, :], uq[0][:, :, :])
            act.copy(uk[1][:, :], uk[0][:, :]).then_inc(uqk_hi_done.sem, 1)

        def uqk_lo(pool, h):
            pool.wait_ge(uqk_hi_done.sem, uqk_hi_done.at(h + 1))
            pool.tensor_tensor(uq[2][:, :, :], uq[0][:, :, :], uq[1][:, :, :].bitcast(F32), ALU.subtract)
            pool.tensor_tensor(uk[2][:, :], uk[0][:, :], uk[1][:, :].bitcast(F32), ALU.subtract
                               ).then_inc(uqk_lo_done.sem, 1)

        def wo_hi(act, h):
            act.wait_ge(wo_in.sem, wo_in.at(16 * (h + 1)))
            act.wait_ge(out_done.sem, out_done.at(4 * h))
            act.copy(wo[1][:, :], wo[0][:, :]).then_inc(wo_hi_done.sem, 1)

        def wo_lo(pool, h):
            pool.wait_ge(wo_hi_done.sem, wo_hi_done.at(h + 1))
            pool.tensor_tensor(wo[2][:, :], wo[0][:, :], wo[1][:, :].bitcast(F32), ALU.subtract
                               ).then_inc(wo_lo_done.sem, 1)

        def all_heads(step):
            def run(eng):
                step(eng, 0, True, False)
                with eng.Fori(1, MLA_HEADS - 1) as h:
                    step(eng, h, False, False)
                step(eng, MLA_HEADS - 1, False, True)
            return run

        with nc.Block() as block:
            @block.sync
            def _(sp):
                d = lambda n: c.dram["L0_attn_a_" + n]
                cols = lambda n, h, **k: d(n).rearrange("r (n d) -> n r d", d=P)[bass.ds(h, 1), :, :]
                for dst, src in ((kcos, "mla_kcos"), (ksin, "mla_ksin"), (qrot, "mla_qrot")):
                    sp.dma_start(dst[:, :], c.dram[src]).then_inc(tables.sem, 16)
                sp.dma_start(wqr[0][:, :], d("W_QR")).then_inc(tables.sem, 16)
                for n, half in enumerate((0, 0, 1, 1)):
                    sp.dma_start(wkr[0][:, n * 32:(n + 1) * 32], d("W_KR")[:, half * 32:(half + 1) * 32]
                                 ).then_inc(tables.sem, 16)
                sp.dma_start(bo[:, :], d("b_O").rearrange("(o h) -> o h", o=1).broadcast_to([P, HID])
                             ).then_inc(tables.sem, 16)

                def load(h):
                    sp.wait_ge(uqk_lo_done.sem, uqk_lo_done.at(h))
                    for half in range(2):
                        sp.dma_start(uq[0][0:Q_LAT_HALF, half, :], d("W_UQ")[half * 96:half * 96 + 96, :].rearrange(
                            "r (n d) -> n r d", d=P)[bass.ds(h, 1), :, :].rearrange("o r d -> r (o d)")
                                     ).then_inc(uqk_in.sem, 16)
                    sp.dma_start(uq[0][Q_LAT_HALF:H1, 1, :], d("b_UQ").rearrange("(n d) -> n d", d=P)[bass.ds(h, 1), :]
                                 ).then_inc(uqk_in.sem, 16)
                    sp.dma_start(uk[0][0:KV_LAT, :], cols("W_UK", h).rearrange("o r d -> r (o d)")).then_inc(uqk_in.sem, 16)
                    sp.dma_start(uk[0][KV_LAT:R2, :], d("b_UK").rearrange("(n d) -> n d", d=P)[bass.ds(h, 1), :]
                                 ).then_inc(uqk_in.sem, 16)
                    sp.wait_ge(v_projected.sem, v_projected.at(2 * h))
                    sp.dma_start(uv[0:KV_LAT, :], cols("W_UV", h).rearrange("o r d -> r (o d)")).then_inc(uv_in.sem, 16)
                    sp.dma_start(uv[KV_LAT:R2, :], d("b_UV").rearrange("(n d) -> n d", d=P)[bass.ds(h, 1), :]
                                 ).then_inc(uv_in.sem, 16)
                    if not (isinstance(h, int) and h == 0):
                        load_wo(h - 1)

                def load_wo(h):
                    sp.wait_ge(wo_lo_done.sem, wo_lo_done.at(h))
                    sp.dma_start(wo[0][:, :], d("W_O").rearrange("(n p) h -> n p h", p=P)[bass.ds(h, 1), :, :].rearrange(
                        "o p h -> p (o h)")).then_inc(wo_in.sem, 16)
                load(0)
                load(1)
                with sp.Fori(2, MLA_HEADS) as h:
                    load(h)
                load_wo(MLA_HEADS - 1)

            @block.tensor
            def _(pe):
                a.open(pe, "pe")
                out_done.open(pe)
                pe.wait_ge(once_lo.sem, once_lo.at(2))
                for b in range(BATCH):
                    keys_pe(pe, 0, b)
                    key_rope_pe(pe, 0, b)
                    queries_pe(pe, 0, b, 0)
                    query_rope_pe(pe, 0, b)
                for t in range(QT):
                    scores(pe, 0, 0, t)

                def step(pe, h, first, last):
                    for b in range(BATCH):
                        u = 2 * h + b
                        n = (h + 1, b)
                        for t in range(QT):
                            if not (last and b == 1):
                                scores(pe, u + 1, 1 - b, t)
                            a.turn(pe, u, b, t)
                            prev = not (first and b == 0)
                            if t == 0:
                                values_make_pe(pe, h, b, 2 * MLA_HEADS if last else u + 2)
                                if not last:
                                    keys_pe(pe, *n)
                            if t == 1:
                                if prev:
                                    values(pe, u - 1, 1 - b, [0])
                                if not first:
                                    out_half(pe, h - 1, b, 0)
                                if not last:
                                    key_rope_pe(pe, *n)
                            if t == 2:
                                if not last:
                                    queries_pe(pe, *n, u + 1)
                                if prev:
                                    values(pe, u - 1, 1 - b, [1])
                            if t == 3:
                                if prev:
                                    values(pe, u - 1, 1 - b, [2, 3])
                                if not first:
                                    out_half(pe, h - 1, b, 1)
                                if not last:
                                    query_rope_pe(pe, *n)
                all_heads(step)(pe)
                h, u = MLA_HEADS - 1, MLA_UNITS - 1
                values(pe, u, 1, [0, 1, 2, 3])
                for b in range(BATCH):
                    out_half(pe, h, b, 0)
                    out_half(pe, h, b, 1)

            @block.scalar
            def _(act):
                a.open(act, "act")
                act.wait_ge(tables.sem, tables.at(16 * 9))
                act.copy(wqr[1][:, :], wqr[0][:, :]).then_inc(once_hi.sem, 1)
                act.copy(wkr[1][:, :], wkr[0][:, :]).then_inc(once_hi.sem, 1)
                act.wait_ge(based.sem, based.at(1))
                uqk_hi(act, 0)
                for b in range(BATCH):
                    keys_act(act, 0, b)
                    key_rope_act(act, 0, b)
                    queries_act(act, 0, b)
                    query_rope_act(act, 0, b)
                for t in range(QT):
                    a.exp(act, 0, 0, t)

                def step(act, h, first, last):
                    for b in range(BATCH):
                        u = 2 * h + b
                        n = (h + 1, b)
                        for t in range(QT):
                            a.step_act(act, u, b, t, not (last and b == 1))
                            if t == 0:
                                if not first:
                                    take_hi(act, u - 2, b)
                                values_make_act(act, h, b)
                                if b == 0 and not last:
                                    uqk_hi(act, h + 1)
                                if not last:
                                    keys_act(act, *n)
                            if t == 2 and not last:
                                key_rope_act(act, *n)
                                queries_act(act, *n)
                            if t == 3:
                                if b == 1:
                                    wo_hi(act, h)
                                if not last:
                                    query_rope_act(act, *n)
                all_heads(step)(act)
                for b in range(BATCH):
                    take_hi(act, MLA_UNITS - 2 + b, b)

            @block.vector
            def _(dve):
                a.open(dve, "dve")
                added.open(dve)
                dve.memset(uq[0][Q_LAT_HALF:H1, 0, :], 0.0).then_inc(based.sem, 1)
                dve.wait_ge(tables.sem, tables.at(16 * 9))
                dve.wait_ge(once_hi.sem, once_hi.at(2))
                dve.tensor_tensor(wqr[2][:, :], wqr[0][:, :], wqr[1][:, :].bitcast(F32), ALU.subtract
                                  ).then_inc(once_lo.sem, 1)
                dve.tensor_tensor(wkr[2][:, :], wkr[0][:, :], wkr[1][:, :].bitcast(F32), ALU.subtract
                                  ).then_inc(once_lo.sem, 1)
                for b in range(BATCH):
                    keys_dve(dve, 0, b)
                    key_rope_dve(dve, 0, b)
                    queries_dve(dve, 0, b)
                    query_rope_dve(dve, 0, b)
                for t in range(QT):
                    a.maximum(dve, 0, 0, t)
                    a.invert(dve, 0, 0, t)
                for t in range(TILES):
                    dve.tensor_tensor(c.x[:, t, :], c.x[:, t, :], bo[:, :], ALU.add).then_inc(based.sem, 1)
                dve.wait_ge(based.sem, based.at(1 + TILES))

                def step(dve, h, first, last):
                    for b in range(BATCH):
                        u = 2 * h + b
                        n = (h + 1, b)
                        for t in range(QT):
                            a.step_dve(dve, u, b, t, not (last and b == 1))
                            if t == 0:
                                if not first:
                                    take_lo(dve, u - 2, b)
                                values_make_dve(dve, h, b)
                                if not last:
                                    keys_dve(dve, *n)
                            if t == 1 and not last:
                                key_rope_dve(dve, *n)
                            if t == 2:
                                if not first:
                                    add_half(dve, u - 2, b, 0)
                                if not last:
                                    queries_dve(dve, *n)
                            if t == 3:
                                if not last:
                                    query_rope_dve(dve, *n)
                                if not first:
                                    add_half(dve, u - 2, b, 1)
                all_heads(step)(dve)
                for b in range(BATCH):
                    take_lo(dve, MLA_UNITS - 2 + b, b)
                    add_half(dve, MLA_UNITS - 2 + b, b, 0)
                    add_half(dve, MLA_UNITS - 2 + b, b, 1)

            @block.gpsimd
            def _(pool):
                pool.wait_ge(based.sem, based.at(1))
                uqk_lo(pool, 0)
                for b in range(BATCH):
                    key_rope_sum(pool, 0, b)
                    key_rope_lo(pool, 0, b)
                    query_rope_lo(pool, 0, b)
                for t in range(QT):
                    a.normalise(pool, 0, 0, t)

                def step(pool, h, first, last):
                    for b in range(BATCH):
                        u = 2 * h + b
                        n = (h + 1, b)
                        for t in range(QT):
                            if not (last and b == 1):
                                a.normalise(pool, u + 1, 1 - b, t)
                            if t == 0 and b == 0 and not last:
                                uqk_lo(pool, h + 1)
                            if t == 2 and not last:
                                key_rope_sum(pool, *n)
                                key_rope_lo(pool, *n)
                            if t == 3:
                                if b == 1:
                                    wo_lo(pool, h)
                                if not last:
                                    query_rope_lo(pool, *n)
                all_heads(step)(pool)


GQA_HEADS, GQA_KV = 32, 4
GQA_REP = GQA_HEADS // GQA_KV
GQA_UNITS = BATCH * GQA_REP


def gqa_jobs():
    jobs = []
    for u in range(GQA_UNITS):
        ahead = u + 3
        jobs.append((u, "q", ahead % GQA_UNITS, ahead >= GQA_UNITS, "A"))
        for at, kind, which, nxt in ((2, "k", 1, False), (4, "v", 1, False), (9, "k", 0, True), (11, "v", 0, True)):
            if u == at:
                jobs.append((u, kind, which, nxt, "B"))
    return jobs


def gqa_phase(c, name, y):
    nc = c.nc
    JOBS = gqa_jobs()
    FIRST = [j for j in JOBS if j[3]]
    ROPE = [j for j in JOBS if j[1] != "v"]
    V = [j for j in JOBS if j[1] == "v"]
    N_J, N_R, N_V = len(JOBS), len(ROPE), len(V)
    F_J, F_R, F_V = len(FIRST), sum(j[1] != "v" for j in FIRST), sum(j[1] == "v" for j in FIRST)

    def number(jobs, per, first, job, g, before_loop):
        if before_loop:
            kinds = [j for j in FIRST if j in jobs]
            return kinds.index(job)
        if isinstance(g, int) and g == GQA_KV - 1:
            jobs = [j for j in jobs if not j[3]]
        return g * per + (first + jobs.index(job))

    with ExitStack() as ctx:
        sb = lambda n, s, dt=F32: c.sb(ctx, f"{name}_{n}", s, dt)
        sem = lambda n, k=0: c.sem(ctx, f"{name}_{n}", k)
        a = Attention(c, ctx, name, causal=True)
        X = c.ps(ctx, f"{name}_X")
        acc = [c.ps(ctx, f"{name}_acc{n}") for n in range(2)]
        cos, sin = sb("cos", [P, SEQ]), sb("sin", [P, SEQ])
        kcos, ksin = sb("kcos", [P, SEQ]), sb("ksin", [P, SEQ])
        eye16, mask16 = sb("eye16", [P, P], BF16), sb("mask16", [P, P], BF16)
        wq_raw = [sb(f"wq_raw{n}", [P, KT, P]) for n in range(4)]
        wo_raw = [sb(f"wo_raw{n}", [P, HID]) for n in range(4)]
        wk_raw, wv_raw = sb("wk_raw", [P, KT, P]), sb("wv_raw", [P, KT, P])
        wq_hi, wq_lo = sb("wq_hi", [P, GQA_REP, KT, P], F32R), sb("wq_lo", [P, GQA_REP, KT, P], F32R)
        wo_hi, wo_lo = sb("wo_hi", [P, GQA_REP, HID], F32R), sb("wo_lo", [P, GQA_REP, HID], F32R)
        wk_hi, wk_lo = sb("wk_hi", [P, KT, P], F32R), sb("wk_lo", [P, KT, P], F32R)
        k_hi, k_lo = sb("k_hi", [P, TOK], F32R), sb("k_lo", [P, TOK], F32R)
        v_hi, v_lo = sb("v_hi", [P, BATCH, QT, P], F32R), sb("v_lo", [P, BATCH, QT, P], F32R)
        q_hi = [sb(f"q_hi{n}", [P, SEQ], F32R) for n in range(4)]
        q_lo = [sb(f"q_lo{n}", [P, SEQ], F32R) for n in range(4)]
        o_hi = [sb(f"o_hi{n}", [P, SEQ], F32R) for n in range(2)]
        o_lo = [sb(f"o_lo{n}", [P, SEQ], F32R) for n in range(2)]
        part_cos, swapped, part_sin, full, vfull = [sb(n, [P, SEQ]) for n in (
            "part_cos", "swapped", "part_sin", "full", "vfull")]
        tables = sem("tables")
        wq_in, wo_in = [sem(f"wq_in{n}") for n in range(4)], [sem(f"wo_in{n}") for n in range(4)]
        wk_in, wv_in = sem("wk_in"), sem("wv_in")
        wq_hi_done, wq_lo_done = sem("wq_hi_done"), sem("wq_lo_done", 4)
        wo_hi_done, wo_lo_done = sem("wo_hi_done"), sem("wo_lo_done", 4)
        wk_hi_done, wk_lo_done = sem("wk_hi_done"), sem("wk_lo_done")
        projected, x_read = sem("projected", 2), sem("x_read", 2)
        cos_done, sin_done, full_done, r_hi_done, r_lo_done = [sem(n, 2) for n in (
            "cos_done", "sin_done", "full_done", "r_hi_done", "r_lo_done")]
        v_hi_done, v_lo_done = sem("v_hi_done"), sem("v_lo_done", 2)
        out_done, flushed = sem("out_done", 2), sem("flushed", 4)

        def job_numbers(job, g, before_loop=False):
            j = number(JOBS, N_J, F_J, job, g, before_loop)
            kinds, per, first = (V, N_V, F_V) if job[1] == "v" else (ROPE, N_R, F_R)
            return j, number(kinds, per, first, job, g, before_loop)

        def q_number(g, u):
            if u >= 3:
                return number(ROPE, N_R, F_R, (u - 3, "q", u, False, "A"), g, False)
            return g * N_R + 1 + u

        def job_pe(pe, job, g, before=False):
            j, n = job_numbers(job, g, before)
            _, kind, which, nxt, _ = job
            gg = 0 if before else (g + 1 if nxt else g)
            pe.wait_ge(x_read.sem, x_read.at(j))
            if kind == "q":
                pe.wait_ge(wq_lo_done.sem, wq_lo_done.at(8 * gg + which % 8 + 1))
                w = [(wq_hi[:, which % 8, kt, :], wq_lo[:, which % 8, kt, :]) for kt in range(KT)]
                half = which // 8
            elif kind == "k":
                pe.wait_ge(wk_lo_done.sem, wk_lo_done.at(gg + 1))
                w = [(wk_hi[:, kt, :], wk_lo[:, kt, :]) for kt in range(KT)]
                half = which
            else:
                pe.wait_ge(wv_in.sem, wv_in.at(16 * (gg + 1)))
                for t in range(QT):
                    tok = which * SEQ + t * P
                    for kt in range(KT):
                        ins = pe.matmul(X[:, t * P:(t + 1) * P], c.hT[:, kt, tok:tok + P], wv_raw[:, kt, :],
                                        start=kt == 0, stop=kt == KT - 1, skip_group_check=True)
                ins.then_inc(projected.sem, 1)
                return
            toks = slice(half * SEQ, half * SEQ + SEQ)
            for kt in range(KT):
                ins = split_product(pe, X[:, :], w[kt], (c.hT_hi[:, kt, toks], c.hT_lo[:, kt, toks]),
                                    kt == 0, kt == KT - 1)
            ins.then_inc(projected.sem, 1)

        def job_act_read(act, job, g, before=False):
            j, n = job_numbers(job, g, before)
            if job[1] == "v":
                act.wait_ge(projected.sem, projected.at(j + 1))
                act.wait_ge(v_lo_done.sem, v_lo_done.at(n))
                act.copy(vfull[:, :], X[:, :]).then_inc(x_read.sem, 1)
                return
            act.wait_ge(cos_done.sem, cos_done.at(n + 1))
            act.wait_ge(sin_done.sem, sin_done.at(n))
            act.copy(swapped[0:64, :], X[64:128, :])
            act.copy(swapped[64:128, :], X[0:64, :]).then_inc(x_read.sem, 1)

        def job_act_hi(act, job, g, before=False):
            j, n = job_numbers(job, g, before)
            _, kind, which, nxt, _ = job
            gg = 0 if before else (g + 1 if nxt else g)
            if kind == "v":
                act.wait_ge(x_read.sem, x_read.at(j + 1))
                if not before:
                    act.wait_ge(a.pv_done.sem, a.pv_done.at(16 * gg - 8 if which == 0 else 16 * gg))
                act.copy(v_hi[:, which, :, :], vfull[:, :].rearrange("p (t d) -> p t d", d=P)).then_inc(v_hi_done.sem, 1)
                return
            act.wait_ge(full_done.sem, full_done.at(n + 1))
            if kind == "q":
                if not before:
                    act.wait_ge(a.scored.sem, a.scored.at(4 * (16 * gg + which) - 12))
                dst = q_hi[which % 4][:, :]
            else:
                if not before:
                    act.wait_ge(a.scored.sem, a.scored.at(4 * (16 * gg - 8 if which == 0 else 16 * gg)))
                dst = k_hi[:, which * SEQ:(which + 1) * SEQ]
            act.copy(dst, full[:, :]).then_inc(r_hi_done.sem, 1)

        def job_dve_cos(dve, job, g, before=False):
            if job[1] == "v":
                return
            j, n = job_numbers(job, g, before)
            dve.wait_ge(projected.sem, projected.at(j + 1))
            dve.wait_ge(full_done.sem, full_done.at(n))
            dve.tensor_tensor(part_cos[:, :], X[:, :], (kcos if job[1] == "k" else cos)[:, :], ALU.mult
                              ).then_inc(cos_done.sem, 1)

        def job_dve_full(dve, job, g, before=False):
            if job[1] == "v":
                return
            j, n = job_numbers(job, g, before)
            dve.wait_ge(sin_done.sem, sin_done.at(n + 1))
            dve.wait_ge(cos_done.sem, cos_done.at(n + 1))
            dve.wait_ge(r_lo_done.sem, r_lo_done.at(n))
            dve.tensor_tensor(full[:, :], part_cos[:, :], part_sin[:, :], ALU.add).then_inc(full_done.sem, 1)

        def job_dve_lo(dve, job, g, before=False):
            if job[1] == "v":
                return
            j, n = job_numbers(job, g, before)
            dve.wait_ge(r_hi_done.sem, r_hi_done.at(n + 1))
            which = job[2]
            if job[1] == "q":
                hi, lo = q_hi[which % 4][:, :], q_lo[which % 4][:, :]
            else:
                hi, lo = [x[:, which * SEQ:(which + 1) * SEQ] for x in (k_hi, k_lo)]
            dve.wait_ge(full_done.sem, full_done.at(n + 1))
            dve.tensor_tensor(lo, full[:, :], hi.bitcast(F32), ALU.subtract).then_inc(r_lo_done.sem, 1)

        def job_pool(pool, job, g, before=False):
            j, n = job_numbers(job, g, before)
            if job[1] == "v":
                pool.wait_ge(v_hi_done.sem, v_hi_done.at(n + 1))
                pool.tensor_tensor(v_lo[:, job[2], :, :], vfull[:, :].rearrange("p (t d) -> p t d", d=P),
                                   v_hi[:, job[2], :, :].bitcast(F32), ALU.subtract).then_inc(v_lo_done.sem, 1)
                return
            pool.wait_ge(x_read.sem, x_read.at(j + 1))
            pool.wait_ge(full_done.sem, full_done.at(n))
            pool.tensor_tensor(part_sin[:, :], swapped[:, :], (ksin if job[1] == "k" else sin)[:, :], ALU.mult
                               ).then_inc(sin_done.sem, 1)

        def wq_hi_split(act, n, h, before=False, g=None):
            act.wait_ge(wq_in[h % 4].sem, wq_in[h % 4].at(16 * (n // 4 + 1) if before else (g + 1) * 32 + (h // 4 + 1) * 16))
            if not before:
                act.wait_ge(projected.sem, projected.at(number(JOBS, N_J, F_J, (5 + h, "q", 8 + h, False, "A"), g, False) + 1))
            act.copy(wq_hi[:, h, :, :], wq_raw[h % 4][:, :, :]).then_inc(wq_hi_done.sem, 1)

        def wq_lo_split(pool, n, h):
            pool.wait_ge(wq_hi_done.sem, wq_hi_done.at(n + 1))
            pool.tensor_tensor(wq_lo[:, h, :, :], wq_raw[h % 4][:, :, :], wq_hi[:, h, :, :].bitcast(F32),
                               ALU.subtract).then_inc(wq_lo_done.sem, 1)

        def wo_hi_split(act, n, h, g=None):
            act.wait_ge(wo_in[h % 4].sem, wo_in[h % 4].at(16 * (n // 4 + 1) if g is None else g * 32 + (h // 4 + 1) * 16))
            if g is not None:
                act.wait_ge(out_done.sem, out_done.at(16 * g - 8 + h + 1))
            act.copy(wo_hi[:, h, :], wo_raw[h % 4][:, :]).then_inc(wo_hi_done.sem, 1)

        def wo_lo_split(pool, n, h):
            pool.wait_ge(wo_hi_done.sem, wo_hi_done.at(n + 1))
            pool.tensor_tensor(wo_lo[:, h, :], wo_raw[h % 4][:, :], wo_hi[:, h, :].bitcast(F32),
                               ALU.subtract).then_inc(wo_lo_done.sem, 1)

        def wk_hi_split(act, g):
            act.wait_ge(wk_in.sem, wk_in.at(16 * (g + 1)))
            if not isinstance(g, int):
                act.wait_ge(projected.sem, projected.at(number(JOBS, N_J, F_J, (2, "k", 1, False, "B"), g - 1, False) + 1))
            act.copy(wk_hi[:, :, :], wk_raw[:, :, :]).then_inc(wk_hi_done.sem, 1)

        def wk_lo_split(pool, g):
            pool.wait_ge(wk_hi_done.sem, wk_hi_done.at(g + 1))
            pool.tensor_tensor(wk_lo[:, :, :], wk_raw[:, :, :], wk_hi[:, :, :].bitcast(F32),
                               ALU.subtract).then_inc(wk_lo_done.sem, 1)

        def load_wq(sp, n, h):
            sp.wait_ge(wq_lo_done.sem, wq_lo_done.at(n - 3))
            sp.dma_start(wq_raw[h % 4][:, :, :], c.dram["L0_ffn_Wq"].rearrange("(k p) (n d) -> n p k d", p=P, d=P)[
                bass.ds(n, 1), :, :, :].rearrange("o p k d -> p (o k) d")).then_inc(wq_in[h % 4].sem, 16)

        def load_wo(sp, n, h):
            sp.wait_ge(wo_lo_done.sem, wo_lo_done.at(n - 3))
            sp.dma_start(wo_raw[h % 4][:, :], c.dram["L0_ffn_Wo"].rearrange("(n p) h -> n p h", p=P)[
                bass.ds(n, 1), :, :].rearrange("o p h -> p (o h)")).then_inc(wo_in[h % 4].sem, 16)

        def load_kv(sp, which, g):
            raw, done, w = (wk_raw, wk_in, "L0_ffn_Wk") if which == "k" else (wv_raw, wv_in, "L0_ffn_Wv")
            sp.dma_start(raw[:, :, :], c.dram[w].rearrange("(k p) (n d) -> n p k d", p=P, d=P)[
                bass.ds(g, 1), :, :, :].rearrange("o p k d -> p (o k) d")).then_inc(done.sem, 16)

        def scores(pe, g, u, t):
            gg, v = (g, u) if u < GQA_UNITS else (g + 1, 0)
            if t == 0:
                pe.wait_ge(r_lo_done.sem, r_lo_done.at(q_number(gg, v) + 1))
            b = v // GQA_REP
            a.scores(pe, 16 * gg + v, v % 2, t, (q_hi[v % 4][:, t * P:(t + 1) * P], q_lo[v % 4][:, t * P:(t + 1) * P]),
                     (k_hi[:, b * SEQ:(b + 1) * SEQ], k_lo[:, b * SEQ:(b + 1) * SEQ]), (eye16[:, :], mask16[:, :]))

        def before(g, u, n):
            return (g, u - n) if u >= n else (g - 1, u - n + GQA_UNITS)

        def values(pe, g, u, kts):
            b = u // GQA_REP
            pe.wait_ge(v_lo_done.sem, v_lo_done.at(2 * g + b + 1))
            if kts[0] == 0:
                pe.wait_ge(a.o_lo_done.sem, a.o_lo_done.at(16 * g + u))
            a.values(pe, 16 * g + u, u % 2, kts, lambda kt: (v_hi[:, b, kt, :], v_lo[:, b, kt, :]))

        def out_project(pe, g, u, tiles):
            h = u % GQA_REP
            pe.wait_ge(wo_lo_done.sem, wo_lo_done.at(8 * g + h + 1))
            pe.wait_ge(a.o_lo_done.sem, a.o_lo_done.at(16 * g + u + 1))
            if h == 0 and tiles[0] == 0:
                pe.wait_ge(flushed.sem, flushed.at(2 * (2 * g + u // GQA_REP)))
            for t in tiles:
                ins = split_product(pe, acc[t // 2][:, t % 2 * HID:t % 2 * HID + HID],
                                    (o_hi[u % 2][:, t * P:(t + 1) * P], o_lo[u % 2][:, t * P:(t + 1) * P]),
                                    (wo_hi[:, h, :], wo_lo[:, h, :]), h == 0 and t % 2 == 0, h == GQA_REP - 1)
            if tiles[-1] == QT - 1:
                ins.then_inc(out_done.sem, 1)

        def flush(dve, g, b):
            dve.wait_ge(out_done.sem, out_done.at(16 * g + 8 * b + 8))
            for n in range(2):
                part = y[:, 4 * b + 2 * n:4 * b + 2 * n + 2, :]
                dve.wait_ge(flushed.sem, flushed.at(2 * (2 * g + b) - 4 + n + 1))
                dve.tensor_tensor(part, part, acc[n][:, :].rearrange("p (t h) -> p t h", h=HID), ALU.add
                                  ).then_inc(flushed.sem, 1)

        def take_hi(act, g, u):
            act.wait_ge(a.pv_done.sem, a.pv_done.at(16 * g + u + 1))
            act.wait_ge(out_done.sem, out_done.at(16 * g + u - 1))
            act.copy(o_hi[u % 2][:, :], a.O[:, :]).then_inc(a.o_hi_done.sem, 1)

        def take_lo(dve, g, u):
            dve.wait_ge(a.o_hi_done.sem, a.o_hi_done.at(16 * g + u + 1))
            dve.tensor_tensor(o_lo[u % 2][:, :], a.O[:, :], o_hi[u % 2][:, :].bitcast(F32), ALU.subtract
                              ).then_inc(a.o_lo_done.sem, 1)

        def jobs_of(u, slot, last):
            return [j for j in JOBS if j[0] == u and j[4] == slot and not (last and j[3])]

        def all_units(eng, unit):
            unit(eng, 0, 0, 2, False)
            unit(eng, 0, 1, 1, False)
            with eng.Fori(0, GQA_KV - 1) as g:
                for u in range(2, GQA_UNITS):
                    unit(eng, g, u, 0, False)
                for u in range(2):
                    unit(eng, g + 1, u, 0, False)
            for u in range(2, GQA_UNITS):
                unit(eng, GQA_KV - 1, u, 0, True)

        with nc.Block() as block:
            @block.sync
            def _(sp):
                for dst, src in ((cos, "gqa_cos"), (sin, "gqa_sin"), (kcos, "gqa_kcos"), (ksin, "gqa_ksin"),
                                 (eye16, "eye16"), (mask16, "mask16")):
                    sp.dma_start(dst[:, :], c.dram[src]).then_inc(tables.sem, 16)
                load_kv(sp, "k", 0)
                load_kv(sp, "v", 0)
                for h in range(GQA_REP):
                    load_wq(sp, h, h)
                    load_wo(sp, h, h)

                def body(g):
                    sp.wait_ge(wk_lo_done.sem, wk_lo_done.at(g + 1))
                    load_kv(sp, "k", g + 1)
                    j, _ = job_numbers((4, "v", 1, False, "B"), g)
                    sp.wait_ge(projected.sem, projected.at(j + 1))
                    load_kv(sp, "v", g + 1)
                    for h in range(GQA_REP):
                        load_wq(sp, 8 * g + 8 + h, h)
                        load_wo(sp, 8 * g + 8 + h, h)
                with sp.Fori(0, GQA_KV - 1) as g:
                    body(g)

            @block.tensor
            def _(pe):
                a.open(pe, "pe")
                projected.open(pe)
                out_done.open(pe)
                pe.wait_ge(tables.sem, tables.at(96))
                pe.wait_ge(a.cleared.sem, a.cleared.at(4))
                for job in FIRST:
                    job_pe(pe, job, 0, True)
                for t in range(QT):
                    scores(pe, 0, 0, t)

                def unit(pe, g, u, missing, last):
                    for t in range(QT):
                        if u + 1 < GQA_UNITS or not last:
                            scores(pe, g, u + 1, t)
                        a.turn(pe, 16 * g + u, u % 2, t)
                        if t == 0:
                            for job in jobs_of(u, "A", last):
                                job_pe(pe, job, g)
                        else:
                            if missing < 2:
                                values(pe, *before(g, u, 1), ([0], [1], [2, 3])[t - 1])
                        if t in (1, 2) and missing < 1:
                            out_project(pe, *before(g, u, 2), ([0, 1], [2, 3])[t - 1])
                        if t == 2:
                            for job in jobs_of(u, "B", last):
                                job_pe(pe, job, g)
                all_units(pe, unit)
                values(pe, GQA_KV - 1, GQA_UNITS - 1, [0, 1, 2, 3])
                for u in (GQA_UNITS - 2, GQA_UNITS - 1):
                    out_project(pe, GQA_KV - 1, u, [0, 1, 2, 3])

            @block.scalar
            def _(act):
                a.open(act, "act")
                x_read.open(act)
                r_hi_done.open(act)
                wk_hi_split(act, 0)
                for h in range(GQA_REP):
                    wq_hi_split(act, h, h, before=True)
                    if h < 6:
                        wo_hi_split(act, h, h)
                    if h == 2:
                        for job in FIRST:
                            job_act_read(act, job, 0, True)
                            job_act_hi(act, job, 0, True)
                for t in range(QT):
                    a.exp(act, 0, 0, t)

                def unit(act, g, u, missing, last):
                    gp, up = before(g, u, 1)
                    for t in range(QT):
                        a.step_act(act, 16 * g + u, u % 2, t, u + 1 < GQA_UNITS or not last)
                        if t == 0:
                            if missing < 1:
                                take_hi(act, *before(g, u, 2))
                            for job in jobs_of(up, "B", last):
                                if job[1] == "v" and missing < 2:
                                    job_act_hi(act, job, gp)
                        if t == 1:
                            for job in jobs_of(up, "B", last):
                                if job[1] == "k" and missing < 2:
                                    job_act_hi(act, job, gp)
                            for job in jobs_of(u, "A", last):
                                job_act_read(act, job, g)
                        if t == 3:
                            for job in jobs_of(u, "A", last):
                                job_act_hi(act, job, g)
                            for job in jobs_of(u, "B", last):
                                job_act_read(act, job, g)
                            if u in (0, 1):
                                wo_hi_split(act, 8 * g + 6 + u, 6 + u, g)
                            if not last:
                                if u == 6:
                                    wk_hi_split(act, g + 1)
                                if u >= 8:
                                    wq_hi_split(act, 8 * g + u, u - 8, g=g)
                                if u >= 10:
                                    wo_hi_split(act, 8 * g + u - 2, u - 10, g + 1)
                all_units(act, unit)
                for u in (GQA_UNITS - 2, GQA_UNITS - 1):
                    take_hi(act, GQA_KV - 1, u)

            @block.vector
            def _(dve):
                a.open(dve, "dve")
                for s in (cos_done, full_done, r_lo_done, flushed):
                    s.open(dve)
                a.clear_unseen(dve)
                dve.wait_ge(tables.sem, tables.at(96))
                for job in FIRST:
                    job_dve_cos(dve, job, 0, True)
                    job_dve_full(dve, job, 0, True)
                    job_dve_lo(dve, job, 0, True)
                for t in range(QT):
                    a.maximum(dve, 0, 0, t)
                    a.invert(dve, 0, 0, t)

                def unit(dve, g, u, missing, last):
                    gp, up = before(g, u, 1)
                    for t in range(QT):
                        a.step_dve(dve, 16 * g + u, u % 2, t, u + 1 < GQA_UNITS or not last)
                        if t == 0:
                            if missing < 1:
                                take_lo(dve, *before(g, u, 2))
                            if missing < 2:
                                for job in jobs_of(up, "A", last):
                                    job_dve_lo(dve, job, gp)
                                for job in jobs_of(up, "B", last):
                                    job_dve_full(dve, job, gp)
                        if t == 1:
                            for job in jobs_of(u, "A", last):
                                job_dve_cos(dve, job, g)
                            if missing < 2:
                                for job in jobs_of(up, "B", last):
                                    job_dve_lo(dve, job, gp)
                        if t == 3:
                            for job in jobs_of(u, "A", last):
                                job_dve_full(dve, job, g)
                            for job in jobs_of(u, "B", last):
                                job_dve_cos(dve, job, g)
                            if u == GQA_REP + 1:
                                flush(dve, g, 0)
                            if u == 1 and missing < 1:
                                flush(dve, g - 1, 1)
                all_units(dve, unit)
                for u in (GQA_UNITS - 2, GQA_UNITS - 1):
                    take_lo(dve, GQA_KV - 1, u)
                flush(dve, GQA_KV - 1, 1)

            @block.gpsimd
            def _(pool):
                for s in (sin_done, wq_lo_done, wo_lo_done, v_lo_done):
                    s.open(pool)
                pool.wait_ge(tables.sem, tables.at(96))
                wk_lo_split(pool, 0)
                for h in range(GQA_REP):
                    wq_lo_split(pool, h, h)
                    if h < 6:
                        wo_lo_split(pool, h, h)
                    if h == 2:
                        for job in FIRST:
                            job_pool(pool, job, 0, True)
                for t in range(QT):
                    a.normalise(pool, 0, 0, t)

                def unit(pool, g, u, missing, last):
                    gp, up = before(g, u, 1)
                    for t in range(QT):
                        if u + 1 < GQA_UNITS or not last:
                            a.normalise(pool, 16 * g + u + 1, (u + 1) % 2, t)
                        if t == 0 and missing < 2:
                            for job in jobs_of(up, "B", last):
                                job_pool(pool, job, gp)
                        if t == 1:
                            for job in jobs_of(u, "A", last):
                                job_pool(pool, job, g)
                        if t == 3:
                            if u in (0, 1):
                                wo_lo_split(pool, 8 * g + 6 + u, 6 + u)
                            if not last:
                                if u == 6:
                                    wk_lo_split(pool, g + 1)
                                if u >= 8:
                                    wq_lo_split(pool, 8 * g + u, u - 8)
                                if u >= 10:
                                    wo_lo_split(pool, 8 * g + u - 2, u - 10)
                all_units(pool, unit)


EXPERTS, TOPK, INNER = 32, 8, 128


def router_phase(c, name, w_table):
    nc = c.nc
    with ExitStack() as ctx:
        sb = lambda n, s: c.sb(ctx, f"{name}_{n}", s)
        sem = lambda n: c.sem(ctx, f"{name}_{n}")
        wr = sb("wr", [P, KT, EXPERTS])
        bias = sb("bias", [P, EXPERTS])
        score = sb("score", [P, TILES, EXPERTS])
        biased = sb("biased", [P, TILES, EXPERTS])
        best = sb("best", [P, TILES, 8])
        rest = sb("rest", [P, TILES, EXPERTS])
        chosen = sb("chosen", [P, TILES, EXPERTS])
        wsel = sb("wsel", [P, TILES, EXPERTS])
        total = sb("total", [P, TILES])
        inv = sb("inv", [P, TILES])
        wnorm = sb("wnorm", [P, TILES, EXPERTS])
        wT = sb("wT", [EXPERTS, TOK])
        ones = sb("ones", [1, TOK])
        logits = c.ps(ctx, f"{name}_logits")
        turned_ps = [c.ps(ctx, f"{name}_wT{n}") for n in range(2)]
        (loaded, logit, scored, bias_added, topped, replaced, marked, picked, summed, inverted, weighted,
         turned, copied, one, stored) = [sem(n) for n in (
            "loaded", "logit", "scored", "bias_added", "topped", "replaced", "marked", "picked", "summed",
            "inverted", "weighted", "turned", "copied", "one", "stored")]
        with nc.Block() as block:
            @block.sync
            def _(sp):
                sp.dma_start(wr[:, :, :], c.dram["L0_ffn_Wr"].rearrange("(k p) e -> p k e", p=P)).then_inc(loaded.sem, 16)
                sp.dma_start(bias[:, :], c.dram["L0_ffn_expert_bias"].rearrange("(a e) -> a e", a=1)
                             .partition_broadcast(P)).then_inc(loaded.sem, 16)
                sp.wait_ge(one.sem, one.at(1))
                sp.dma_start(w_table[EXPERTS:EXPERTS + 1, :], ones[:, :]).then_inc(stored.sem, 16)
                sp.wait_ge(copied.sem, copied.at(2))
                sp.dma_start(w_table[0:EXPERTS, :], wT[:, :]).then_inc(stored.sem, 16)
                sp.wait_ge(stored.sem, stored.at(32))

            @block.tensor
            def _(pe):
                pe.wait_ge(loaded.sem, loaded.at(32))
                for t in range(TILES):
                    for kt in range(KT):
                        ins = pe.matmul(logits[:, t * EXPERTS:(t + 1) * EXPERTS], c.hT[:, kt, t * P:(t + 1) * P],
                                        wr[:, kt, :], start=kt == 0, stop=kt == KT - 1)
                ins.then_inc(logit.sem, 1)
                pe.wait_ge(weighted.sem, weighted.at(1))
                for t in range(TILES):
                    ins = pe.transpose(turned_ps[t // 4][0:EXPERTS, t % 4 * P:(t % 4 + 1) * P], wnorm[:, t, :],
                                       c.ident[:, :])
                    if t % 4 == 3:
                        ins.then_inc(turned.sem, 1)

            @block.scalar
            def _(act):
                act.wait_ge(logit.sem, logit.at(1))
                act.activation(score[:, :, :], logits[:, 0:TILES * EXPERTS].rearrange("p (t e) -> p t e", e=EXPERTS),
                               ACT.Sigmoid).then_inc(scored.sem, 1)

            @block.vector
            def _(dve):
                dve.memset(ones[:, :], 1.0).then_inc(one.sem, 1)
                dve.wait_ge(scored.sem, scored.at(1))
                for t in range(TILES):
                    dve.tensor_tensor(biased[:, t, :], score[:, t, :], bias[:, :], ALU.add).then_inc(bias_added.sem, 1)
                for t in range(TILES):
                    dve.wait_ge(bias_added.sem, bias_added.at(t + 1))
                    dve.max(best[:, t, :], biased[:, t, :]).then_inc(topped.sem, 1)
                for t in range(TILES):
                    dve.wait_ge(topped.sem, topped.at(t + 1))
                    dve.match_replace(out=rest[:, t, :], in_to_replace=best[:, t, :], in_values=biased[:, t, :],
                                      imm_value=-3e38).then_inc(replaced.sem, 1)
                dve.wait_ge(replaced.sem, replaced.at(TILES))
                dve.tensor_tensor(chosen[:, :, :], rest[:, :, :], biased[:, :, :], ALU.not_equal).then_inc(marked.sem, 1)
                dve.wait_ge(marked.sem, marked.at(1))
                dve.tensor_tensor(wsel[:, :, :], chosen[:, :, :], score[:, :, :], ALU.mult).then_inc(picked.sem, 1)
                dve.wait_ge(picked.sem, picked.at(1))
                dve.tensor_reduce(total[:, :], wsel[:, :, :], AX_X, ALU.add).then_inc(summed.sem, 1)
                dve.wait_ge(summed.sem, summed.at(1))
                dve.reciprocal(inv[:, :], total[:, :]).then_inc(inverted.sem, 1)
                dve.wait_ge(inverted.sem, inverted.at(1))
                dve.tensor_tensor(wnorm[:, :, :], wsel[:, :, :], inv[:, :].unsqueeze(2).broadcast_to([P, TILES, EXPERTS]),
                                  ALU.mult).then_inc(weighted.sem, 1)
                for n in range(2):
                    dve.wait_ge(turned.sem, turned.at(n + 1))
                    dve.tensor_copy(wT[:, n * 512:(n + 1) * 512], turned_ps[n][0:EXPERTS, :]).then_inc(copied.sem, 1)


def expert_phase(c, name, w_table, y):
    nc = c.nc
    WG, WU, WD = 0, HID, 2 * HID
    COLS = 3 * HID
    units = lambda e, half: 2 * e + half
    with ExitStack() as ctx:
        sb = lambda n, s, dt=F32: c.sb(ctx, f"{name}_{n}", s, dt)
        sem = lambda n, k=0: c.sem(ctx, f"{name}_{n}", k)
        raw = [sb(f"raw{n}", [P, COLS]) for n in range(2)]
        w_hi = [sb(f"w_hi{n}", [P, COLS], F32R) for n in range(2)]
        w_lo = [sb(f"w_lo{n}", [P, COLS], F32R) for n in range(2)]
        weight = [sb(f"weight{n}", [P, TOK]) for n in range(2)]
        gate = [sb(f"gate{n}", [P, 512]) for n in range(2)]
        scaled = [sb(f"scaled{n}", [P, 512]) for n in range(2)]
        inner = [sb(f"inner{n}", [P, 512]) for n in range(2)]
        a_hi = [sb(f"a_hi{n}", [P, 512], F32R) for n in range(2)]
        a_lo = [sb(f"a_lo{n}", [P, 512], F32R) for n in range(2)]
        G = [c.ps(ctx, f"{name}_G{n}") for n in range(2)]
        U = [c.ps(ctx, f"{name}_U{n}") for n in range(2)]
        acc = [c.ps(ctx, f"{name}_acc{n}") for n in range(4)]
        raw_in = [sem(f"raw_in{n}") for n in range(2)]
        weight_in = [sem(f"weight_in{n}") for n in range(2)]
        gu_hi, gu_lo, d_hi, d_lo = sem("gu_hi", 2), sem("gu_lo", 2), sem("d_hi", 2), sem("d_lo", 2)
        projected, gated, weighed, multiplied = sem("projected", 2), sem("gated", 2), sem("weighed", 2), sem("multiplied", 2)
        a_hi_done, a_lo_done, down_done = sem("a_hi_done", 2), sem("a_lo_done", 2), sem("down_done", 4)
        y_added, summed = sem("y_added"), sem("summed")
        GU, DN = slice(0, WD), slice(WD, COLS)

        def load(sp, e, slot, shared=False):
            sp.wait_ge(d_hi.sem, d_hi.at(e - 1))
            sp.wait_ge(d_lo.sem, d_lo.at(e - 1))
            if shared:
                src = [c.dram["L0_ffn_Wsg"], c.dram["L0_ffn_Wsu"], c.dram["L0_ffn_Wsd"]]
            else:
                src = [c.dram[f"L0_ffn_{n}"][bass.ds(e, 1), :, :].rearrange("o a b -> (o a) b") for n in ("Wg", "Wu", "Wd")]
            for n, base in ((0, WG), (1, WU)):
                sp.dma_start(raw[slot][:, base:base + HID].rearrange("p (k i) -> p k i", i=INNER),
                             src[n].rearrange("(k p) i -> p k i", p=P)).then_inc(raw_in[slot].sem, 16)
            sp.dma_start(raw[slot][:, DN], src[2]).then_inc(raw_in[slot].sem, 16)
            sp.wait_ge(weighed.sem, weighed.at(2 * e - 2))
            row = w_table[EXPERTS:EXPERTS + 1, :] if shared else w_table[bass.ds(e, 1), :]
            sp.dma_start(weight[slot][:, :], row.rearrange("o n -> (o n)").partition_broadcast(P)
                         ).then_inc(weight_in[slot].sem, 16)

        def split_hi(act, e, slot, nth, cols):
            act.wait_ge(raw_in[slot].sem, raw_in[slot].at(48 * (nth + 1)))
            used = projected if cols is GU else down_done
            act.wait_ge(used.sem, used.at(2 * e - 2))
            act.copy(w_hi[slot][:, cols], raw[slot][:, cols]).then_inc((gu_hi if cols is GU else d_hi).sem, 1)

        def split_lo(dve, e, slot, cols):
            hi_done, used = (gu_hi, projected) if cols is GU else (d_hi, down_done)
            dve.wait_ge(hi_done.sem, hi_done.at(e + 1))
            dve.wait_ge(used.sem, used.at(2 * e - 2))
            dve.tensor_tensor(w_lo[slot][:, cols], raw[slot][:, cols], w_hi[slot][:, cols].bitcast(F32),
                              ALU.subtract).then_inc((gu_lo if cols is GU else d_lo).sem, 1)

        def project(pe, e, half, slot):
            u = 2 * e + half
            if half == 0:
                pe.wait_ge(gu_lo.sem, gu_lo.at(e + 1))
            pe.wait_ge(gated.sem, gated.at(u - 1))
            for bank, base in ((G[half], WG), (U[half], WU)):
                if base == WU:
                    pe.wait_ge(multiplied.sem, multiplied.at(u - 1))
                for kt in range(KT):
                    cols = slice(base + kt * P, base + (kt + 1) * P)
                    toks = slice(half * 512, half * 512 + 512)
                    ins = split_product(pe, bank[:, :], (w_hi[slot][:, cols], w_lo[slot][:, cols]),
                                        (c.hT_hi[:, kt, toks], c.hT_lo[:, kt, toks]), kt == 0, kt == KT - 1)
            ins.then_inc(projected.sem, 1)

        def down(pe, e, half, slot, first=False):
            if half == 0:
                pe.wait_ge(d_lo.sem, d_lo.at(e + 1))
            pe.wait_ge(a_lo_done.sem, a_lo_done.at(2 * e + half + 1))
            for t in range(4):
                bank = acc[2 * half + t // 2]
                cols = slice(t * P, (t + 1) * P)
                ins = split_product(pe, bank[:, t % 2 * HID:t % 2 * HID + HID], (a_hi[half][:, cols], a_lo[half][:, cols]),
                                    (w_hi[slot][:, DN], w_lo[slot][:, DN]), first and t % 2 == 0, True)
            ins.then_inc(down_done.sem, 1)

        def silu(act, e, half):
            u = 2 * e + half
            act.wait_ge(projected.sem, projected.at(u + 1))
            act.wait_ge(weighed.sem, weighed.at(u - 1))
            act.activation(gate[half][:, :], G[half][:, :], ACT.Silu).then_inc(gated.sem, 1)

        def inner_hi(act, e, half):
            u = 2 * e + half
            act.wait_ge(multiplied.sem, multiplied.at(u + 1))
            act.wait_ge(down_done.sem, down_done.at(u - 1))
            act.copy(a_hi[half][:, :], inner[half][:, :]).then_inc(a_hi_done.sem, 1)

        def weigh(pool, e, half, slot, nth):
            u = 2 * e + half
            pool.wait_ge(weight_in[slot].sem, weight_in[slot].at(16 * (nth + 1)))
            pool.wait_ge(gated.sem, gated.at(u + 1))
            pool.wait_ge(multiplied.sem, multiplied.at(u - 1))
            pool.tensor_tensor(scaled[half][:, :], gate[half][:, :], weight[slot][:, half * 512:half * 512 + 512],
                               ALU.mult).then_inc(weighed.sem, 1)

        def multiply(dve, e, half):
            u = 2 * e + half
            dve.wait_ge(weighed.sem, weighed.at(u + 1))
            dve.wait_ge(projected.sem, projected.at(u + 1))
            dve.wait_ge(a_lo_done.sem, a_lo_done.at(u - 1))
            dve.tensor_tensor(inner[half][:, :], U[half][:, :], scaled[half][:, :], ALU.mult).then_inc(multiplied.sem, 1)

        def inner_lo(dve, e, half):
            u = 2 * e + half
            dve.wait_ge(a_hi_done.sem, a_hi_done.at(u + 1))
            dve.wait_ge(down_done.sem, down_done.at(u - 1))
            dve.tensor_tensor(a_lo[half][:, :], inner[half][:, :], a_hi[half][:, :].bitcast(F32),
                              ALU.subtract).then_inc(a_lo_done.sem, 1)

        PAIRS = EXPERTS // 2
        with nc.Block() as block:
            @block.sync
            def _(sp):
                for e in range(2):
                    load(sp, e, e)
                with sp.Fori(0, PAIRS - 1) as i:
                    for s in range(2):
                        load(sp, i * 2 + s + 2, s)
                load(sp, EXPERTS, 0, shared=True)

            @block.tensor
            def _(pe):
                projected.open(pe)
                down_done.open(pe)
                project(pe, 0, 0, 0)
                project(pe, 0, 1, 0)

                def pair(e, first=False):
                    project(pe, e + 1, 0, 1)
                    down(pe, e, 0, 0, first)
                    project(pe, e + 1, 1, 1)
                    down(pe, e, 1, 0, first)
                    project(pe, e + 2, 0, 0)
                    down(pe, e + 1, 0, 1)
                    project(pe, e + 2, 1, 0)
                    down(pe, e + 1, 1, 1)
                pair(0, True)
                with pe.Fori(1, PAIRS) as i:
                    pair(i * 2)
                down(pe, EXPERTS, 0, 0)
                down(pe, EXPERTS, 1, 0)

            @block.scalar
            def _(act):
                for s in (gu_hi, d_hi, gated, a_hi_done):
                    s.open(act)
                split_hi(act, 0, 0, 0, GU)
                split_hi(act, 0, 0, 0, DN)
                split_hi(act, 1, 1, 0, GU)
                silu(act, 0, 0)
                inner_hi(act, 0, 0)
                silu(act, 0, 1)

                def pair(e, i, last=False):
                    inner_hi(act, e, 1)
                    silu(act, e + 1, 0)
                    split_hi(act, e + 1, 1, i, DN)
                    inner_hi(act, e + 1, 0)
                    split_hi(act, e + 2, 0, i + 1, GU)
                    silu(act, e + 1, 1)
                    inner_hi(act, e + 1, 1)
                    silu(act, e + 2, 0)
                    split_hi(act, e + 2, 0, i + 1, DN)
                    inner_hi(act, e + 2, 0)
                    if not last:
                        split_hi(act, e + 3, 1, i + 1, GU)
                    silu(act, e + 2, 1)
                with act.Fori(0, PAIRS - 1) as i:
                    pair(i * 2, i)
                pair(EXPERTS - 2, PAIRS - 1, last=True)
                inner_hi(act, EXPERTS, 1)

            @block.gpsimd
            def _(pool):
                weighed.open(pool)
                with pool.Fori(0, PAIRS) as i:
                    for s in range(2):
                        for half in range(2):
                            weigh(pool, i * 2 + s, half, s, i)
                for half in range(2):
                    weigh(pool, EXPERTS, half, 0, PAIRS)

            @block.vector
            def _(dve):
                for s in (gu_lo, d_lo, multiplied, a_lo_done):
                    s.open(dve)
                split_lo(dve, 0, 0, GU)
                split_lo(dve, 0, 0, DN)
                split_lo(dve, 1, 1, GU)
                multiply(dve, 0, 0)
                inner_lo(dve, 0, 0)

                def pair(e, last=False):
                    multiply(dve, e, 1)
                    inner_lo(dve, e, 1)
                    split_lo(dve, e + 1, 1, DN)
                    multiply(dve, e + 1, 0)
                    inner_lo(dve, e + 1, 0)
                    split_lo(dve, e + 2, 0, GU)
                    multiply(dve, e + 1, 1)
                    inner_lo(dve, e + 1, 1)
                    split_lo(dve, e + 2, 0, DN)
                    multiply(dve, e + 2, 0)
                    inner_lo(dve, e + 2, 0)
                    if not last:
                        split_lo(dve, e + 3, 1, GU)
                with dve.Fori(0, PAIRS - 1) as i:
                    pair(i * 2)
                pair(EXPERTS - 2, last=True)
                multiply(dve, EXPERTS, 1)
                inner_lo(dve, EXPERTS, 1)
                dve.tensor_tensor(c.x[:, :, :], c.x[:, :, :], y[:, :, :], ALU.add).then_inc(y_added.sem, 1)
                dve.wait_ge(y_added.sem, y_added.at(1))
                dve.wait_ge(down_done.sem, down_done.at(2 * EXPERTS + 2))
                for n in range(4):
                    part = c.x[:, 2 * n:2 * n + 2, :]
                    dve.tensor_tensor(part, part, acc[n][:, :].rearrange("p (t h) -> p t h", h=HID),
                                      ALU.add).then_inc(summed.sem, 1)


MHA_HEADS, MHA_D = 16, 16
GROUP = 4
GROUPS = MHA_HEADS // GROUP
MHA_HALF = MHA_HEADS // 2
DIAG = P + MHA_D
HALF_COLS = MHA_HALF * DIAG


def mha_phase(c, name):
    nc = c.nc
    with ExitStack() as ctx:
        sb = lambda n, s, dt=F32: c.sb(ctx, f"{name}_{n}", s, dt)
        sem = lambda n, k=0: c.sem(ctx, f"{name}_{n}", k)
        a = Attention(c, ctx, name, causal=True)
        X = [c.ps(ctx, f"{name}_X{n}") for n in range(3)]
        acc = X[1:3]
        eye16, mask16 = sb("eye16", [P, P], BF16), sb("mask16", [P, P], BF16)
        w_raw = a.prob[0][:, :, :].rearrange("p a b -> p (a b)").rearrange("p (k m) -> p k m", k=KT)
        wv = a.prob[1][:, 0, :].rearrange("p (k m) -> p k m", k=KT)
        w_hi, w_lo = sb("w_hi", [P, KT, 2 * GROUPS * P], F32R), sb("w_lo", [P, KT, 2 * GROUPS * P], F32R)
        wo = sb("wo", [P, KT, HID])
        qk_hi, qk_lo = sb("qk_hi", [P, 2 * GROUPS, SEQ], F32R), sb("qk_lo", [P, 2 * GROUPS, SEQ], F32R)
        v_full = c.hT[:, :, :].rearrange("p k t -> p (k t)").rearrange("p (t h) -> p t h", h=HID)
        v_hi, v_lo = [sb(n, [P, QT, 2 * HALF_COLS], F32R) for n in ("v_hi", "v_lo")]
        z = sb("z", [P, SEQ])
        loaded, w_hi_done, w_lo_done, zeroed = sem("loaded"), sem("w_hi_done"), sem("w_lo_done"), sem("zeroed")
        v_made, v_kept = sem("v_made"), sem("v_kept")
        projected, qk_hi_done, qk_lo_done = sem("projected"), sem("qk_hi_done"), sem("qk_lo_done", 3)
        v_hi_done, v_lo_done = sem("v_hi_done"), sem("v_lo_done")
        out_done, added = sem("out_done", 2), sem("added", 1)
        JOBS = 2 * GROUPS

        def v_bank(t):
            return (*a.S, *a.T)[t // 2][:, t % 2 * HID:t % 2 * HID + HID]

        def qk_pe(pe, b, n):
            j = JOBS * b + n
            pe.wait_ge(qk_lo_done.sem, qk_lo_done.at(j - 2))
            pe.wait_ge(added.sem, added.at(2 * b))
            for kt in range(KT):
                ins = split_product(pe, X[n % 3][:, :], (w_hi[:, kt, n * P:(n + 1) * P], w_lo[:, kt, n * P:(n + 1) * P]),
                                    (c.hT_hi[:, kt, bass.ds(b * SEQ, SEQ)], c.hT_lo[:, kt, bass.ds(b * SEQ, SEQ)]),
                                    kt == 0, kt == KT - 1)
            ins.then_inc(projected.sem, 1)

        def scale(n):
            return 1.0 / float(np.sqrt(MHA_D)) if n < GROUPS else 1.0

        def qk_act(act, b, n):
            act.wait_ge(projected.sem, projected.at(JOBS * b + n + 1))
            act.activation(qk_hi[:, n, :], X[n % 3][:, :], ACT.Copy, scale=scale(n)).then_inc(qk_hi_done.sem, 1)

        def qk_dve(dve, b, n):
            dve.wait_ge(qk_hi_done.sem, qk_hi_done.at(JOBS * b + n + 1))
            dve.scalar_tensor_tensor(out=qk_lo[:, n, :], in0=X[n % 3][:, :], scalar=scale(n),
                                     in1=qk_hi[:, n, :].bitcast(F32), op0=ALU.mult, op1=ALU.subtract
                                     ).then_inc(qk_lo_done.sem, 1)

        def spread(x, kt):
            return x[:, kt, :].rearrange("p (h c) -> p h c", c=DIAG)[:, :, 0:MHA_D]

        def v_of(b, kt):
            return v_full[:, bass.ds(b * QT + kt, 1), :].rearrange("p o (h d) -> p (o h) d", d=MHA_D)

        def v_split_hi(act, b):
            act.wait_ge(a.pv_done.sem, a.pv_done.at(MHA_HEADS * b))
            for kt in range(QT):
                ins = act.copy(spread(v_hi, kt), v_of(b, kt))
            ins.then_inc(v_hi_done.sem, 1)

        def v_split_lo(pool, b):
            pool.wait_ge(v_hi_done.sem, v_hi_done.at(b + 1))
            for kt in range(QT):
                ins = pool.tensor_tensor(spread(v_lo, kt), v_of(b, kt), spread(v_hi, kt).bitcast(F32), ALU.subtract)
            ins.then_inc(v_lo_done.sem, 1)

        def scores(pe, b, h, t):
            rows = slice(32 * (h % GROUP), 32 * (h % GROUP) + 32)
            q, k = h // GROUP, GROUPS + h // GROUP
            pe.wait_ge(qk_lo_done.sem, qk_lo_done.at(JOBS * b + k + 1))
            a.scores(pe, MHA_HEADS * b + h, h % 2, t,
                     (qk_hi[rows, q, t * P:(t + 1) * P], qk_lo[rows, q, t * P:(t + 1) * P]),
                     (qk_hi[rows, k, :], qk_lo[rows, k, :]), (eye16[:, :], mask16[:, :]))

        def values(pe, b, h, kts):
            j = h % MHA_HALF
            col = h // MHA_HALF * HALF_COLS + j * P
            pe.wait_ge(v_lo_done.sem, v_lo_done.at(b + 1))
            if j == 0 and kts[0] == 0:
                pe.wait_ge(a.o_lo_done.sem, a.o_lo_done.at(2 * b + h // MHA_HALF))
            a.values(pe, MHA_HEADS * b + h, h % 2, kts, lambda kt: (v_hi[:, kt, col:col + P], v_lo[:, kt, col:col + P]),
                     start=j == 0, stop=j == MHA_HALF - 1)

        def take(dve, b, half):
            dve.wait_ge(a.pv_done.sem, a.pv_done.at(MHA_HEADS * b + MHA_HALF * (half + 1)))
            dve.wait_ge(out_done.sem, out_done.at(2 * b + half))
            dve.tensor_copy(z[:, :], a.O[:, :]).then_inc(a.o_lo_done.sem, 1)

        def out_project(pe, b, half):
            pe.wait_ge(a.o_lo_done.sem, a.o_lo_done.at(2 * b + half + 1))
            for t in range(QT):
                ins = pe.matmul(acc[t // 2][:, t % 2 * HID:t % 2 * HID + HID], z[:, t * P:(t + 1) * P],
                                wo[:, half, :], start=half == 0 and t % 2 == 0, stop=half == 1,
                                skip_group_check=True)
            ins.then_inc(out_done.sem, 1)

        def add(dve, b):
            dve.wait_ge(out_done.sem, out_done.at(2 * b + 2))
            for n in range(2):
                part = c.x[:, bass.ds(4 * b + 2 * n, 2), :]
                dve.tensor_tensor(part, part, acc[n][:, :].rearrange("p (t h) -> p t h", h=HID), ALU.add
                                  ).then_inc(added.sem, 1)

        with nc.Block() as block:
            @block.sync
            def _(sp):
                for n, w in enumerate(("mha_wq", "mha_wk")):
                    sp.dma_start(w_raw[:, :, n * GROUPS * P:(n + 1) * GROUPS * P],
                                 c.dram[w].rearrange("(k p) m -> p k m", p=P)).then_inc(loaded.sem, 16)
                sp.dma_start(wv[:, :, :], c.dram["mha_wv"].rearrange("(k p) m -> p k m", p=P)).then_inc(loaded.sem, 16)
                sp.dma_start(wo[:, :, :], c.dram["mha_wo"].rearrange("(k p) m -> p k m", p=P)).then_inc(loaded.sem, 16)
                sp.dma_start(eye16[:, :], c.dram["eye16"]).then_inc(loaded.sem, 16)
                sp.dma_start(mask16[:, :], c.dram["mask16"]).then_inc(loaded.sem, 16)

            @block.tensor
            def _(pe):
                a.open(pe, "pe")
                out_done.open(pe)
                pe.wait_ge(loaded.sem, loaded.at(96))
                for t in range(TILES):
                    for kt in range(KT):
                        ins = pe.matmul(v_bank(t), c.hT[:, kt, t * P:(t + 1) * P], wv[:, kt, :],
                                        start=kt == 0, stop=kt == KT - 1, skip_group_check=True)
                ins.then_inc(v_made.sem, 1)
                pe.wait_ge(v_kept.sem, v_kept.at(TILES))
                pe.wait_ge(w_lo_done.sem, w_lo_done.at(1))
                pe.wait_ge(a.cleared.sem, a.cleared.at(4))
                pe.wait_ge(zeroed.sem, zeroed.at(2))
                with pe.Fori(0, BATCH) as b:
                    for n in range(JOBS):
                        qk_pe(pe, b, n)
                    for t in range(QT):
                        scores(pe, b, 0, t)
                    for h in range(MHA_HEADS):
                        for t in range(QT):
                            if h + 1 < MHA_HEADS:
                                scores(pe, b, h + 1, t)
                            a.turn(pe, MHA_HEADS * b + h, h % 2, t)
                            if h > 0 and t > 0:
                                values(pe, b, h - 1, ([0], [1], [2, 3])[t - 1])
                        if h == MHA_HALF + 1:
                            out_project(pe, b, 0)
                    values(pe, b, MHA_HEADS - 1, [0, 1, 2, 3])
                    out_project(pe, b, 1)

            @block.scalar
            def _(act):
                a.open(act, "act")
                act.wait_ge(loaded.sem, loaded.at(96))
                act.copy(w_hi[:, :, :], w_raw[:, :, :]).then_inc(w_hi_done.sem, 1)
                act.wait_ge(zeroed.sem, zeroed.at(2))
                with act.Fori(0, BATCH) as b:
                    for n in range(JOBS):
                        qk_act(act, b, n)
                    act.wait_ge(v_kept.sem, v_kept.at(TILES))
                    v_split_hi(act, b)
                    for t in range(QT):
                        a.exp(act, MHA_HEADS * b, 0, t)
                    for h in range(MHA_HEADS):
                        for t in range(QT):
                            a.step_act(act, MHA_HEADS * b + h, h % 2, t, h + 1 < MHA_HEADS)

            @block.vector
            def _(dve):
                a.open(dve, "dve")
                qk_lo_done.open(dve)
                added.open(dve)
                dve.wait_ge(v_made.sem, v_made.at(1))
                for t in range(TILES):
                    dve.tensor_copy(v_full[:, t, :], v_bank(t)).then_inc(v_kept.sem, 1)
                a.clear_unseen(dve)
                dve.wait_ge(w_hi_done.sem, w_hi_done.at(1))
                dve.tensor_tensor(w_lo[:, :, :], w_raw[:, :, :], w_hi[:, :, :].bitcast(F32), ALU.subtract
                                  ).then_inc(w_lo_done.sem, 1)
                with dve.Fori(0, BATCH) as b:
                    for n in range(JOBS):
                        qk_dve(dve, b, n)
                    for t in range(QT):
                        a.maximum(dve, MHA_HEADS * b, 0, t)
                        a.invert(dve, MHA_HEADS * b, 0, t)
                    for h in range(MHA_HEADS):
                        for t in range(QT):
                            a.step_dve(dve, MHA_HEADS * b + h, h % 2, t, h + 1 < MHA_HEADS)
                            if h == MHA_HALF + 1 and t == 0:
                                take(dve, b, 0)
                    take(dve, b, 1)
                    add(dve, b)

            @block.gpsimd
            def _(pool):
                for x in (v_hi, v_lo):
                    pool.memset(x[:, :, :].bitcast(F32), 0.0).then_inc(zeroed.sem, 1)
                pool.wait_ge(zeroed.sem, zeroed.at(2))
                with pool.Fori(0, BATCH) as b:
                    v_split_lo(pool, b)
                    for t in range(QT):
                        a.normalise(pool, MHA_HEADS * b, 0, t)
                    for h in range(MHA_HEADS - 1):
                        for t in range(QT):
                            a.normalise(pool, MHA_HEADS * b + h + 1, (h + 1) % 2, t)


def ffn(c, name, w_table):
    with ExitStack() as ctx:
        y = c.sb(ctx, f"{name}_y", [P, TILES, HID])
        column = lambda w: c.dram[w].rearrange("(k p) -> p k", p=P)
        norm_phase(c, f"{name}n1", c.x, False, dst=y, transpose=False)
        norm_phase(c, f"{name}n2", y, True, weight=column("L0_ffn_ln1_w"))
        gqa_phase(c, f"{name}g", y)
        norm_phase(c, f"{name}n3", y, True, weight=column("L0_ffn_ln2_w"))
        router_phase(c, f"{name}r", w_table)
        expert_phase(c, f"{name}e", w_table, y)


def hybrid_kernel(nc, dram, out):
    w_table = nc.dram_tensor("w_table", (EXPERTS + 1, TOK), F32, kind="Internal").ap()
    with ExitStack() as ctx:
        c = Chip(nc, ctx, dram, out)
        load_phase(c)
        norm_phase(c, "an", c.x, False, split=False)
        mla_phase(c, "a")
        ffn(c, "f0", w_table)
        norm_phase(c, "bn", c.x, False)
        mha_phase(c, "b")
        ffn(c, "f1", w_table)
        store_phase(c)



def rotary(dim):
    inv = (1.0 / THETA ** (np.arange(0, dim, 2, dtype=np.float32) / np.float32(dim))).astype(np.float32)
    angle = (np.arange(SEQ, dtype=np.float32)[:, None] * inv[None, :]).astype(np.float32)
    return np.cos(angle).T.astype(np.float32), np.sin(angle).T.astype(np.float32)


def consts():
    bf16 = np.dtype("bfloat16")
    cos, sin = rotary(128)
    k_cos, k_sin = np.concatenate([cos, cos]), np.concatenate([-sin, sin])
    scale = np.float32(1.0 / np.sqrt(128.0))
    above = np.triu(np.full((P, P), -1e30, np.float32), k=1)
    c64, s64 = rotary(64)
    return {
        "mla_kcos": np.concatenate([c64, c64]), "mla_ksin": np.concatenate([-s64, -s64]),
        "mla_qrot": np.concatenate([c64, -s64]),
        "ident": np.eye(P, dtype=np.float32),
        "eye16": np.eye(P).astype(bf16),
        "mask16": above.astype(bf16),
        "gqa_kcos": k_cos, "gqa_ksin": k_sin,
        "gqa_cos": k_cos * scale, "gqa_sin": k_sin * scale,
    }


def mha_columns(w):
    out = np.zeros((HID, MHA_HEADS, 2 * MHA_D), np.float32)
    out[:, :, 0:MHA_D] = w.T.reshape(HID, MHA_HEADS, MHA_D)
    return out.reshape(HID, MHA_HEADS * 2 * MHA_D)


def mha_weights(wq, wk, wv, wo):
    return {"mha_wq": mha_columns(wq), "mha_wk": mha_columns(wk),
            "mha_wv": np.ascontiguousarray(wv.T), "mha_wo": np.ascontiguousarray(wo.T)}


def kernel(**inputs):
    import concourse.bacc as _bacc
    from concourse.bass_utils import run_bass_kernel_spmd as _run

    arrays = {n: np.ascontiguousarray(a) for n, a in inputs.items()}
    arrays.update(mha_weights(*[arrays.pop(f"L0_attn_b_{n}") for n in ("Wq", "Wk", "Wv", "Wo")]))
    arrays.update(consts())
    nc = _bacc.Bacc("TRN2", target_bir_lowering=False, num_devices=1)
    dram = {n: nc.dram_tensor(f"in_{n}", a.shape, mybir.dt.from_np(a.dtype), kind="ExternalInput").ap()
            for n, a in arrays.items()}
    out = nc.dram_tensor("out_0", (BATCH, SEQ, HID), F32, kind="ExternalOutput").ap()
    hybrid_kernel(nc, dram, out)
    r = _run(nc, [{f"in_{n}": a for n, a in arrays.items()}], core_ids=[0])
    return r.results[0]["out_0"]
```

```python
from contextlib import ExitStack

import numpy as np

import concourse.bass as bass
from concourse import mybir

F32 = mybir.dt.float32
F32R = mybir.dt.float32r
BF16 = mybir.dt.bfloat16
ALU = mybir.AluOpType
ACT = mybir.ActivationFunctionType
AX_X = mybir.AxisListType.X

P = 128
BATCH, SEQ, HID = 2, 512, 256
TOK = BATCH * SEQ
TILES = TOK // P
KT = HID // P
QT = SEQ // P
LN_EPS = 1e-5
RMS_EPS = 1e-5
THETA = 10000.0


class Count:

    def __init__(self, sem, credits=0):
        self.sem = sem
        self.credits = credits

    def open(self, eng):
        eng.sem_inc(self.sem, self.credits)

    def at(self, n):
        if isinstance(n, int):
            n = max(n, 0)
        return n + self.credits


def split_product(pe, out, w, x, start, stop):
    pe.matmul(out, w[0], x[0], start=start, stop=False, skip_group_check=True)
    pe.matmul(out, w[1], x[0], start=False, stop=False, skip_group_check=True)
    return pe.matmul(out, w[0], x[1], start=False, stop=stop, skip_group_check=True)


class Chip:

    def __init__(self, nc, ctx, dram, out):
        self.nc, self.ctx, self.dram, self.out = nc, ctx, dram, out
        self.sems = []
        self.x = self.sb(ctx, "x_resid", [P, TILES, HID])
        self.ident = self.sb(ctx, "ident_sb", [P, P])
        self.hT = self.sb(ctx, "hT", [P, KT, TOK])
        self.hT_hi = self.sb(ctx, "hT_hi", [P, KT, TOK], F32R)
        self.hT_lo = self.sb(ctx, "hT_lo", [P, KT, TOK], F32R)

    def sb(self, ctx, name, shape, dt=F32):
        return ctx.enter_context(self.nc.sbuf_tensor(name, shape, dt))

    def ps(self, ctx, name, shape=(P, 512), dt=F32):
        return ctx.enter_context(self.nc.psum_tensor(name, list(shape), dt))

    def sem(self, ctx, name, credits=0):
        sem = self.nc.alloc_semaphore(name)
        self.sems.append(sem)
        return Count(sem, credits)

    def clear_sems(self):
        self.nc.clear_and_free_semaphores(self.sems)
        self.nc.all_engine_barrier()
        self.sems = []


def load_phase(c):
    with ExitStack() as ctx:
        loaded = c.sem(ctx, "ld_loaded")
        with c.nc.Block() as block:
            @block.sync
            def _(sp):
                sp.dma_start(c.x[:, :, :], c.dram["L0_attn_a_hidden_states"].rearrange(
                    "b (t p) h -> p (b t) h", p=P)).then_inc(loaded.sem, 16)
                sp.dma_start(c.ident[:, :], c.dram["ident"]).then_inc(loaded.sem, 16)
                sp.wait_ge(loaded.sem, loaded.at(32))


def store_phase(c):
    with ExitStack() as ctx:
        stored = c.sem(ctx, "st_stored")
        with c.nc.Block() as block:
            @block.sync
            def _(sp):
                sp.dma_start(c.out.rearrange("b (t p) h -> p (b t) h", p=P),
                             c.x[:, :, :]).then_inc(stored.sem, 16)
                sp.wait_ge(stored.sem, stored.at(16))


def norm_phase(c, name, src, rms, dst=None, weight=None, split=True, transpose=True,
               prefetch=None):
    nc = c.nc
    with ExitStack() as ctx:
        sb = lambda n, s: c.sb(ctx, f"{name}_{n}", s)
        sem = lambda n: c.sem(ctx, f"{name}_{n}")
        stats = sb("stats", [P, TILES, 6])
        mv = sb("mv", [P, TILES, 2])
        ms = sb("ms", [P, TILES])
        sd = sb("sd", [P, TILES])
        rstd = sb("rstd", [P, TILES])
        xn = dst if dst is not None else sb("xn", [P, TILES, HID])
        wcol = sb("wcol", [P, KT]) if weight is not None else None
        banks = [c.ps(ctx, f"{name}_T{n}") for n in range(4)]
        weighed, stat, aggr, msq, shifted, rooted, inverted, normed = [sem(n) for n in (
            "weighed", "stat", "aggr", "msq", "shifted", "rooted", "inverted", "normed")]
        turned, evacuated, hi_done, lo_done = [sem(n) for n in ("turned", "evac", "hi", "lo")]

        with nc.Block() as block:
            @block.sync
            def _(sp):
                if weight is not None:
                    sp.dma_start(wcol[:, :], weight, allow_slow_non_contiguous=True).then_inc(weighed.sem, 16)
                if prefetch is not None:
                    prefetch(sp)

            @block.vector
            def _(dve):
                for t in range(TILES):
                    dve.bn_stats(stats[:, t, :], src[:, t, :]).then_inc(stat.sem, 1)
                for t in range(TILES):
                    dve.wait_ge(stat.sem, stat.at(t + 1))
                    dve.bn_aggr(mv[:, t, :], stats[:, t, :]).then_inc(aggr.sem, 1)
                dve.wait_ge(aggr.sem, aggr.at(TILES))
                if rms:
                    dve.tensor_tensor(ms[:, :], mv[:, :, 0], mv[:, :, 0], ALU.mult).then_inc(msq.sem, 1)
                    dve.wait_ge(msq.sem, msq.at(1))
                    dve.scalar_tensor_tensor(out=sd[:, :], in0=ms[:, :], scalar=RMS_EPS, in1=mv[:, :, 1],
                                             op0=ALU.add, op1=ALU.add).then_inc(shifted.sem, 1)
                else:
                    dve.tensor_scalar(sd[:, :], mv[:, :, 1], LN_EPS, None, ALU.add).then_inc(shifted.sem, 1)
                dve.wait_ge(rooted.sem, rooted.at(1))
                dve.reciprocal(rstd[:, :], sd[:, :]).then_inc(inverted.sem, 1)
                dve.wait_ge(inverted.sem, inverted.at(1))
                for t in range(TILES):
                    if rms:
                        ins = dve.tensor_scalar(xn[:, t, :], src[:, t, :], rstd[:, t:t + 1], None, ALU.mult)
                    else:
                        ins = dve.tensor_scalar(xn[:, t, :], src[:, t, :], mv[:, t, 0:1], rstd[:, t:t + 1],
                                                ALU.subtract, ALU.mult)
                    ins.then_inc(normed.sem, 1)
                if not transpose:
                    return
                if weight is not None:
                    dve.wait_ge(weighed.sem, weighed.at(16))
                for n in range(4):
                    dve.wait_ge(turned.sem, turned.at(n + 1))
                    part = c.hT[:, n % 2, n // 2 * 512:n // 2 * 512 + 512]
                    if weight is not None:
                        ins = dve.tensor_scalar(part, banks[n][:, :], wcol[:, n % 2:n % 2 + 1], None, ALU.mult)
                    else:
                        ins = dve.tensor_copy(part, banks[n][:, :])
                    ins.then_inc(evacuated.sem, 1)
                for n in range(4 if split else 0):
                    dve.wait_ge(hi_done.sem, hi_done.at(n + 1))
                    dve.wait_ge(evacuated.sem, evacuated.at(n + 1))
                    at = (slice(None), n % 2, slice(n // 2 * 512, n // 2 * 512 + 512))
                    dve.tensor_tensor(c.hT_lo[at], c.hT[at], c.hT_hi[at].bitcast(F32),
                                      ALU.subtract).then_inc(lo_done.sem, 1)

            @block.scalar
            def _(act):
                act.wait_ge(shifted.sem, shifted.at(1))
                act.activation(sd[:, :], sd[:, :], ACT.Sqrt).then_inc(rooted.sem, 1)
                for n in range(4 if split and transpose else 0):
                    act.wait_ge(evacuated.sem, evacuated.at(n + 1))
                    at = (slice(None), n % 2, slice(n // 2 * 512, n // 2 * 512 + 512))
                    act.copy(c.hT_hi[at], c.hT[at]).then_inc(hi_done.sem, 1)

            @block.tensor
            def _(pe):
                for n in range(4 if transpose else 0):
                    half, kt = n // 2, n % 2
                    pe.wait_ge(normed.sem, normed.at(4 * half + 4))
                    for t in range(4):
                        ins = pe.transpose(banks[n][:, t * P:(t + 1) * P],
                                           xn[:, 4 * half + t, kt * P:(kt + 1) * P], c.ident[:, :])
                    ins.then_inc(turned.sem, 1)



class Attention:

    def __init__(self, c, ctx, name, causal):
        self.c, self.causal = c, causal
        sb = lambda n, s, dt=F32: c.sb(ctx, f"{name}_{n}", s, dt)
        sem = lambda n, k=0: c.sem(ctx, f"{name}_{n}", k)
        self.S = [c.ps(ctx, f"{name}_S{n}") for n in range(2)]
        self.T = [c.ps(ctx, f"{name}_T{n}") for n in range(2)]
        self.O = c.ps(ctx, f"{name}_O")
        self.prob = [sb(f"prob{n}", [P, QT, SEQ]) for n in range(2)]
        self.pt_hi = [sb(f"pt_hi{n}", [P, QT, SEQ], F32R) for n in range(2)]
        self.pt_lo = [sb(f"pt_lo{n}", [P, QT, SEQ], F32R) for n in range(2)]
        self.negmax = sb("negmax", [P, 2 * QT])
        self.rowsum = sb("rowsum", [P, 2 * QT])
        self.rinv = sb("rinv", [P, 2 * QT])
        self.scored, self.maxed, self.exped, self.inverted = sem("scored", 4), sem("maxed"), sem("exped", 4), sem("inverted")
        self.normed, self.turned = sem("normed"), sem("turned", 8)
        self.pt_hi_done, self.pt_lo_done = sem("pt_hi_done"), sem("pt_lo_done", 2)
        self.pv_done, self.o_hi_done, self.o_lo_done = sem("pv_done", 3), sem("o_hi_done"), sem("o_lo_done", 3)
        self.cleared = sem("cleared")

    def width(self, t):
        return max(256, P * (t + 1)) if self.causal else SEQ

    def used(self, t):
        return P * (t + 1) if self.causal else SEQ

    def scores(self, pe, u, par, t, q, k, mask=None):
        e = 4 * u + t
        bank = self.S[t % 2]
        pe.wait_ge(self.exped.sem, self.exped.at(e - 1))
        w = self.width(t)
        ins = split_product(pe, bank[:, 0:w], q, (k[0][:, 0:w], k[1][:, 0:w]), True, mask is None)
        if mask is not None:
            ins = pe.matmul(bank[:, t * P:(t + 1) * P], mask[0], mask[1], start=False, stop=True, skip_group_check=True)
        ins.then_inc(self.scored.sem, 1)

    def maximum(self, dve, u, par, t):
        dve.wait_ge(self.scored.sem, self.scored.at(4 * u + t + 1))
        dve.tensor_reduce(self.negmax[:, 4 * par + t:4 * par + t + 1], self.S[t % 2][:, 0:self.used(t)], AX_X, ALU.max,
                          negate=True).then_inc(self.maxed.sem, 1)

    def exp(self, act, u, par, t, bias=None):
        e = 4 * u + t
        n = slice(4 * par + t, 4 * par + t + 1)
        if bias is None:
            act.wait_ge(self.maxed.sem, self.maxed.at(e + 1))
            bias = self.negmax
        act.wait_ge(self.turned.sem, self.turned.at(e - 7))
        act.activation(self.prob[par][:, t, 0:self.used(t)], self.S[t % 2][:, 0:self.used(t)], ACT.Exp, bias=bias[:, n],
                       accum_out=self.rowsum[:, n]).then_inc(self.exped.sem, 1)

    def invert(self, dve, u, par, t):
        dve.wait_ge(self.exped.sem, self.exped.at(4 * u + t + 1))
        n = slice(4 * par + t, 4 * par + t + 1)
        dve.reciprocal(self.rinv[:, n], self.rowsum[:, n]).then_inc(self.inverted.sem, 1)

    def normalise(self, pool, u, par, t):
        pool.wait_ge(self.inverted.sem, self.inverted.at(4 * u + t + 1))
        n = slice(4 * par + t, 4 * par + t + 1)
        w = self.used(t)
        part = self.prob[par][:, t, 0:w]
        pool.tensor_tensor(part, part, self.rinv[:, n].broadcast_to([P, w]), ALU.mult).then_inc(self.normed.sem, 1)

    def turn(self, pe, u, par, t):
        e = 4 * u + t
        pe.wait_ge(self.normed.sem, self.normed.at(e + 1))
        pe.wait_ge(self.pt_lo_done.sem, self.pt_lo_done.at(e - 1))
        for kt in range(self.used(t) // P):
            ins = pe.transpose(self.T[t % 2][:, kt * P:(kt + 1) * P], self.prob[par][:, t, kt * P:(kt + 1) * P],
                               self.c.ident[:, :])
        ins.then_inc(self.turned.sem, 1)

    def turned_part(self, dst, t):
        n = self.used(t) // P
        return dst[:, 0:n, t * P:(t + 1) * P], self.T[t % 2][:, 0:n * P].rearrange("p (k q) -> p k q", q=P)

    def split_hi(self, act, u, par, t):
        act.wait_ge(self.turned.sem, self.turned.at(4 * u + t + 1))
        act.wait_ge(self.pv_done.sem, self.pv_done.at(u - 1))
        dst, src = self.turned_part(self.pt_hi[par], t)
        act.copy(dst, src).then_inc(self.pt_hi_done.sem, 1)

    def split_lo(self, dve, u, par, t):
        dve.wait_ge(self.pt_hi_done.sem, self.pt_hi_done.at(4 * u + t + 1))
        dst, src = self.turned_part(self.pt_lo[par], t)
        hi, _ = self.turned_part(self.pt_hi[par], t)
        dve.tensor_tensor(dst, src, hi.bitcast(F32), ALU.subtract).then_inc(self.pt_lo_done.sem, 1)

    def values(self, pe, u, par, kts, v, start=True, stop=True):
        pe.wait_ge(self.pt_lo_done.sem, self.pt_lo_done.at(4 * u + 4))
        for kt in kts:
            q0 = min(kt * P, SEQ - 256) if self.causal else 0
            ins = split_product(pe, self.O[:, q0:SEQ], v(kt),
                                (self.pt_hi[par][:, kt, q0:SEQ], self.pt_lo[par][:, kt, q0:SEQ]),
                                start and kt == 0, stop and kt == QT - 1)
        if kts[-1] == QT - 1:
            ins.then_inc(self.pv_done.sem, 1)

    def step_act(self, act, u, par, t, more):
        self.split_hi(act, u, par, t)
        if more:
            self.exp(act, u + 1, 1 - par, t)

    def step_dve(self, dve, u, par, t, more):
        if more:
            self.maximum(dve, u + 1, 1 - par, t)
        self.split_lo(dve, u, par, t)
        if more:
            self.invert(dve, u + 1, 1 - par, t)

    def open(self, eng, which):
        for s in {"pe": (self.scored, self.turned, self.pv_done), "act": (self.exped,),
                  "dve": (self.pt_lo_done, self.o_lo_done)}[which]:
            s.open(eng)

    def clear_unseen(self, dve):
        for part in (*self.pt_hi, *self.pt_lo):
            dve.memset(part[:, QT - 1, 256:384].bitcast(F32), 0.0).then_inc(self.cleared.sem, 1)


MLA_HEADS, MLA_D, KV_LAT, Q_LAT, ROPE = 16, 128, 64, 192, 64
Q_LAT_HALF = Q_LAT // 2
MLA_UNITS = MLA_HEADS * BATCH


def mla_latents(c, name, ckv, cq, prefetch):
    nc = c.nc
    with ExitStack() as ctx:
        sb = lambda n, s, dt=F32: c.sb(ctx, f"{name}_{n}", s, dt)
        sem = lambda n, k=0: c.sem(ctx, f"{name}_{n}", k)
        wkv, wq = sb("wkv", [P, KT, KV_LAT]), sb("wq", [P, KT, Q_LAT])
        bkv, bq = sb("bkv", [KV_LAT, 1]), sb("bq", [Q_LAT_HALF, 2])
        banks = [c.ps(ctx, f"{name}_L{n}") for n in range(6)]
        loaded, ones, projected, full_done, hi_done, lo_done = [sem(n) for n in (
            "loaded", "ones", "projected", "full", "hi", "lo")]
        parts = [(KV_LAT, lambda kt: wkv[:, kt, :], bkv[:, 0:1], lambda x, s: x[0:KV_LAT, s]),
                 (Q_LAT_HALF, lambda kt: wq[:, kt, 0:Q_LAT_HALF], bq[:, 0:1], lambda x, s: x[0:Q_LAT_HALF, 0, s]),
                 (Q_LAT_HALF, lambda kt: wq[:, kt, Q_LAT_HALF:Q_LAT], bq[:, 1:2], lambda x, s: x[0:Q_LAT_HALF, 1, s])]
        work = [(b, n) for b in range(BATCH) for n in range(3)]
        outs = (ckv, cq, cq)
        with nc.Block() as block:
            @block.sync
            def _(sp):
                d = lambda n: c.dram["L0_attn_a_" + n]
                sp.dma_start(wkv[:, :, :], d("W_DKV").rearrange("(k p) m -> p k m", p=P)).then_inc(loaded.sem, 16)
                sp.dma_start(wq[:, :, :], d("W_DQ").rearrange("(k p) m -> p k m", p=P)).then_inc(loaded.sem, 16)
                sp.dma_start(bkv[:, :], d("b_DKV").rearrange("(p o) -> p o", o=1)).then_inc(loaded.sem, 16)
                sp.dma_start(bq[:, :], d("b_DQ").rearrange("(k p) -> p k", p=Q_LAT_HALF),
                             allow_slow_non_contiguous=True).then_inc(loaded.sem, 16)
                prefetch(sp)

            @block.tensor
            def _(pe):
                pe.wait_ge(loaded.sem, loaded.at(64))
                for i, (b, n) in enumerate(work):
                    rows, w, _, _ = parts[n]
                    for kt in range(KT):
                        ins = pe.matmul(banks[i][0:rows, :], w(kt), c.hT[:, kt, b * SEQ:(b + 1) * SEQ],
                                        start=kt == 0, stop=kt == KT - 1)
                    ins.then_inc(projected.sem, 1)

            @block.vector
            def _(dve):
                dve.memset(ckv[0][KV_LAT:KV_LAT + 1, :].bitcast(F32), 1.0).then_inc(ones.sem, 1)
                dve.memset(ckv[1][KV_LAT:KV_LAT + 1, :].bitcast(F32), 0.0).then_inc(ones.sem, 1)
                dve.memset(ckv[2][KV_LAT:KV_LAT + 1, :], 1.0).then_inc(ones.sem, 1)
                for x in cq[0:2]:
                    dve.memset(x[Q_LAT_HALF:Q_LAT_HALF + 1, :, :].bitcast(F32), 0.0).then_inc(ones.sem, 1)
                dve.wait_ge(ones.sem, ones.at(5))
                dve.memset(cq[0][Q_LAT_HALF:Q_LAT_HALF + 1, 1, :].bitcast(F32), 1.0).then_inc(ones.sem, 1)
                dve.wait_ge(loaded.sem, loaded.at(64))
                for i, (b, n) in enumerate(work):
                    rows, _, bias, at = parts[n]
                    dve.wait_ge(projected.sem, projected.at(i + 1))
                    dve.tensor_scalar(at(outs[n][2], slice(b * SEQ, (b + 1) * SEQ)), banks[i][0:rows, :], bias, None,
                                      ALU.add).then_inc(full_done.sem, 1)
                    dve.wait_ge(hi_done.sem, hi_done.at(i + 1))
                    dve.wait_ge(full_done.sem, full_done.at(i + 1))
                    hi, lo, full = [at(outs[n][k], slice(b * SEQ, (b + 1) * SEQ)) for k in range(3)]
                    dve.tensor_tensor(lo, full, hi.bitcast(F32), ALU.subtract).then_inc(lo_done.sem, 1)

            @block.scalar
            def _(act):
                for i, (b, n) in enumerate(work):
                    act.wait_ge(full_done.sem, full_done.at(i + 1))
                    hi, lo, full = [parts[n][3](outs[n][k], slice(b * SEQ, (b + 1) * SEQ)) for k in range(3)]
                    act.copy(hi, full).then_inc(hi_done.sem, 1)


def mla_phase(c, name):
    nc = c.nc
    SCALE = 1.0 / float(np.sqrt(MLA_D))
    with ExitStack() as ctx:
        sb = lambda n, s, dt=F32: c.sb(ctx, f"{name}_{n}", s, dt)
        sem = lambda n, k=0: c.sem(ctx, f"{name}_{n}", k)
        R2, H1 = KV_LAT + 1, Q_LAT_HALF + 1
        ckv = [sb("ckv_hi", [R2, TOK], F32R), sb("ckv_lo", [R2, TOK], F32R), sb("ckv", [R2, TOK])]
        cq = [sb("cq_hi", [H1, 2, TOK], F32R), sb("cq_lo", [H1, 2, TOK], F32R), sb("cq", [H1, 2, TOK])]
        kcos, ksin, qrot = sb("kcos", [ROPE, SEQ]), sb("ksin", [ROPE, SEQ]), sb("qrot", [ROPE, SEQ])
        bo = sb("bo", [P, HID])
        wqr = [sb("wqr", [P, ROPE])] + [sb(f"wqr_{n}", [P, ROPE], F32R) for n in ("hi", "lo")]
        wkr = [sb("wkr", [P, 2 * ROPE])] + [sb(f"wkr_{n}", [P, 2 * ROPE], F32R) for n in ("hi", "lo")]
        uq = [sb("uq", [H1, 2, P])] + [sb(f"uq_{n}", [H1, 2, P], F32R) for n in ("hi", "lo")]
        uk = [sb("uk", [R2, P])] + [sb(f"uk_{n}", [R2, P], F32R) for n in ("hi", "lo")]
        uv = sb("uv", [R2, P])
        wo = [sb("wo", [P, HID])] + [sb(f"wo_{n}", [P, HID], F32R) for n in ("hi", "lo")]
        tables, rot_in, uqk_in = sem("tables"), sem("rot_in"), sem("uqk_in")
        d = lambda n: c.dram["L0_attn_a_" + n]
        head_cols = lambda w, h: w.rearrange("r (n d) -> n r d", d=P)[bass.ds(h, 1), :, :].rearrange("o r d -> r (o d)")
        head_row = lambda w, h: w.rearrange("(n d) -> n d", d=P)[bass.ds(h, 1), :]

        def load_uqk(sp, h):
            for half in range(2):
                rows = slice(half * Q_LAT_HALF, (half + 1) * Q_LAT_HALF)
                sp.dma_start(uq[0][0:Q_LAT_HALF, half, :], head_cols(d("W_UQ")[rows, :], h)).then_inc(uqk_in.sem, 16)
            sp.dma_start(uq[0][Q_LAT_HALF:H1, 1, :], head_row(d("b_UQ"), h)).then_inc(uqk_in.sem, 16)
            sp.dma_start(uk[0][0:KV_LAT, :], head_cols(d("W_UK"), h)).then_inc(uqk_in.sem, 16)
            sp.dma_start(uk[0][KV_LAT:R2, :], head_row(d("b_UK"), h)).then_inc(uqk_in.sem, 16)

        def prefetch(sp):
            load_uqk(sp, 0)
            for n, half in enumerate((0, 0, 1, 1)):
                sp.dma_start(wkr[0][:, n * 32:(n + 1) * 32], d("W_KR")[:, half * 32:(half + 1) * 32]
                             ).then_inc(rot_in.sem, 16)
            sp.dma_start(wqr[0][:, :], d("W_QR")).then_inc(rot_in.sem, 16)
            for dst, src in ((kcos, "mla_kcos"), (ksin, "mla_ksin"), (qrot, "mla_qrot")):
                sp.dma_start(dst[:, :], c.dram[src]).then_inc(tables.sem, 16)
            sp.dma_start(bo[:, :], d("b_O").rearrange("(o h) -> o h", o=1).broadcast_to([P, HID])
                         ).then_inc(tables.sem, 16)
        mla_latents(c, name + "l", ckv, cq, prefetch)

        a = Attention(c, ctx, name, causal=False)
        acc = c.ps(ctx, f"{name}_acc")
        X = [c.ps(ctx, f"{name}_X{n}") for n in range(2)]
        k_hi, k_lo, q_hi, q_lo = [[sb(f"{x}{n}", [P, SEQ], F32R) for n in range(2)] for x in (
            "k_hi", "k_lo", "q_hi", "q_lo")]
        v_hi, v_lo = [[sb(f"{x}{n}", [P, QT, P], F32R) for n in range(2)] for x in ("v_hi", "v_lo")]
        o_hi, o_lo = [[sb(f"{x}{n}", [P, SEQ], F32R) for n in range(2)] for x in ("o_hi", "o_lo")]
        kr_a, kr_b, kr_full, qr_full = [sb(n, [ROPE, SEQ]) for n in ("kr_a", "kr_b", "kr_full", "qr_full")]

        once_hi, once_lo, based = sem("once_hi"), sem("once_lo"), sem("based")
        uv_in, wo_in = sem("uv_in"), sem("wo_in")
        uqk_hi_done, uqk_lo_done, wo_hi_done, wo_lo_done = [sem(n) for n in (
            "uqk_hi_done", "uqk_lo_done", "wo_hi_done", "wo_lo_done")]
        k_projected, k_hi_done, k_lo_done, kr_projected, kr_turned, kr_sum, kr_hi_done, kr_lo_done = [sem(n) for n in (
            "k_projected", "k_hi_done", "k_lo_done", "kr_projected", "kr_turned", "kr_sum", "kr_hi_done",
            "kr_lo_done")]
        q_projected, q_hi_done, q_lo_done, qr_projected, qr_turned, qr_hi_done, qr_lo_done = [sem(n) for n in (
            "q_projected", "q_hi_done", "q_lo_done", "qr_projected", "qr_turned", "qr_hi_done", "qr_lo_done")]
        v_projected, v_hi_done, v_lo_done = sem("v_projected"), sem("v_hi_done"), sem("v_lo_done")
        out_done, added = sem("out_done", 3), sem("added", 4)

        def keys_pe(pe, h, b):
            n = 2 * h + b
            pe.wait_ge(uqk_lo_done.sem, uqk_lo_done.at(h + 1))
            pe.wait_ge(qr_turned.sem, qr_turned.at(n))
            split_product(pe, X[0][:, :], (uk[1][:, :], uk[2][:, :]),
                          (ckv[0][:, b * SEQ:(b + 1) * SEQ], ckv[1][:, b * SEQ:(b + 1) * SEQ]), True, True
                          ).then_inc(k_projected.sem, 1)

        def keys_act(act, h, b):
            n = 2 * h + b
            act.wait_ge(k_projected.sem, k_projected.at(n + 1))
            act.wait_ge(a.scored.sem, a.scored.at(4 * (n - 1)))
            act.copy(k_hi[b][:, :], X[0][:, :]).then_inc(k_hi_done.sem, 1)

        def keys_dve(dve, h, b):
            dve.wait_ge(k_hi_done.sem, k_hi_done.at(2 * h + b + 1))
            dve.tensor_tensor(k_lo[b][:, :], X[0][:, :], k_hi[b][:, :].bitcast(F32), ALU.subtract
                              ).then_inc(k_lo_done.sem, 1)

        def key_rope_pe(pe, h, b):
            pe.wait_ge(k_lo_done.sem, k_lo_done.at(2 * h + b + 1))
            split_product(pe, X[0][:, :], (wkr[1][:, :], wkr[2][:, :]), (k_hi[b][:, :], k_lo[b][:, :]), True, True
                          ).then_inc(kr_projected.sem, 1)

        def key_rope_dve(dve, h, b):
            n = 2 * h + b
            dve.wait_ge(kr_projected.sem, kr_projected.at(n + 1))
            dve.wait_ge(kr_sum.sem, kr_sum.at(n))
            dve.tensor_tensor(kr_a[:, :], X[0][0:ROPE, :], kcos[:, :], ALU.mult)
            dve.tensor_tensor(kr_b[:, :], X[0][ROPE:2 * ROPE, :], ksin[:, :], ALU.mult).then_inc(kr_turned.sem, 1)

        def key_rope_sum(pool, h, b):
            n = 2 * h + b
            pool.wait_ge(kr_turned.sem, kr_turned.at(n + 1))
            pool.wait_ge(kr_lo_done.sem, kr_lo_done.at(n))
            pool.tensor_tensor(kr_full[:, :], kr_a[:, :], kr_b[:, :], ALU.add).then_inc(kr_sum.sem, 1)

        def key_rope_act(act, h, b):
            act.wait_ge(kr_sum.sem, kr_sum.at(2 * h + b + 1))
            act.copy(k_hi[b][0:ROPE, :], kr_full[:, :]).then_inc(kr_hi_done.sem, 1)

        def key_rope_lo(pool, h, b):
            pool.wait_ge(kr_hi_done.sem, kr_hi_done.at(2 * h + b + 1))
            pool.tensor_tensor(k_lo[b][0:ROPE, :], kr_full[:, :], k_hi[b][0:ROPE, :].bitcast(F32), ALU.subtract
                               ).then_inc(kr_lo_done.sem, 1)

        def queries_pe(pe, h, b, values_before):
            pe.wait_ge(uqk_lo_done.sem, uqk_lo_done.at(h + 1))
            pe.wait_ge(v_lo_done.sem, v_lo_done.at(values_before))
            pe.wait_ge(q_lo_done.sem, q_lo_done.at(2 * h + b))
            for half in range(2):
                s = slice(b * SEQ, (b + 1) * SEQ)
                ins = split_product(pe, X[1][:, :], (uq[1][:, half, :], uq[2][:, half, :]),
                                    (cq[0][:, half, s], cq[1][:, half, s]), half == 0, half == 1)
            ins.then_inc(q_projected.sem, 1)

        def queries_act(act, h, b):
            n = 2 * h + b
            act.wait_ge(q_projected.sem, q_projected.at(n + 1))
            act.wait_ge(a.scored.sem, a.scored.at(4 * (n - 1)))
            act.activation(q_hi[b][:, :], X[1][:, :], ACT.Copy, scale=SCALE).then_inc(q_hi_done.sem, 1)

        def queries_dve(dve, h, b):
            dve.wait_ge(q_hi_done.sem, q_hi_done.at(2 * h + b + 1))
            dve.scalar_tensor_tensor(out=q_lo[b][:, :], in0=X[1][:, :], scalar=SCALE, in1=q_hi[b][:, :].bitcast(F32),
                                     op0=ALU.mult, op1=ALU.subtract).then_inc(q_lo_done.sem, 1)

        def query_rope_pe(pe, h, b):
            n = 2 * h + b
            pe.wait_ge(q_lo_done.sem, q_lo_done.at(n + 1))
            pe.wait_ge(kr_turned.sem, kr_turned.at(n + 1))
            split_product(pe, X[0][0:ROPE, :], (wqr[1][:, :], wqr[2][:, :]), (q_hi[b][:, :], q_lo[b][:, :]),
                          True, True).then_inc(qr_projected.sem, 1)

        def query_rope_dve(dve, h, b):
            n = 2 * h + b
            dve.wait_ge(qr_projected.sem, qr_projected.at(n + 1))
            dve.wait_ge(qr_lo_done.sem, qr_lo_done.at(n))
            dve.tensor_tensor(qr_full[:, :], X[0][0:ROPE, :], qrot[:, :], ALU.mult).then_inc(qr_turned.sem, 1)

        def query_rope_act(act, h, b):
            act.wait_ge(qr_turned.sem, qr_turned.at(2 * h + b + 1))
            act.copy(q_hi[b][0:ROPE, :], qr_full[:, :]).then_inc(qr_hi_done.sem, 1)

        def query_rope_lo(pool, h, b):
            pool.wait_ge(qr_hi_done.sem, qr_hi_done.at(2 * h + b + 1))
            pool.tensor_tensor(q_lo[b][0:ROPE, :], qr_full[:, :], q_hi[b][0:ROPE, :].bitcast(F32), ALU.subtract
                               ).then_inc(qr_lo_done.sem, 1)

        def values_make_pe(pe, h, b, queries_before):
            pe.wait_ge(uv_in.sem, uv_in.at(32 * (h + 1)))
            pe.wait_ge(q_lo_done.sem, q_lo_done.at(queries_before))
            pe.wait_ge(v_lo_done.sem, v_lo_done.at(2 * h + b))
            for t in range(QT):
                ins = pe.matmul(X[1][:, t * P:(t + 1) * P], ckv[2][:, b * SEQ + t * P:b * SEQ + (t + 1) * P],
                                uv[:, :], start=True, stop=True, skip_group_check=True)
            ins.then_inc(v_projected.sem, 1)

        def values_make_act(act, h, b):
            u = 2 * h + b
            act.wait_ge(v_projected.sem, v_projected.at(u + 1))
            act.wait_ge(a.pv_done.sem, a.pv_done.at(u - 1))
            act.copy(v_hi[b][:, :, :], X[1][:, :].rearrange("p (t d) -> p t d", d=P)).then_inc(v_hi_done.sem, 1)

        def values_make_dve(dve, h, b):
            dve.wait_ge(v_hi_done.sem, v_hi_done.at(2 * h + b + 1))
            dve.tensor_tensor(v_lo[b][:, :, :], X[1][:, :].rearrange("p (t d) -> p t d", d=P),
                              v_hi[b][:, :, :].bitcast(F32), ALU.subtract).then_inc(v_lo_done.sem, 1)

        def scores(pe, u, b, t):
            pe.wait_ge(kr_lo_done.sem, kr_lo_done.at(u + 1))
            pe.wait_ge(qr_lo_done.sem, qr_lo_done.at(u + 1))
            a.scores(pe, u, b, t, (q_hi[b][:, t * P:(t + 1) * P], q_lo[b][:, t * P:(t + 1) * P]),
                     (k_hi[b][:, :], k_lo[b][:, :]))

        def values(pe, u, b, kts):
            pe.wait_ge(v_lo_done.sem, v_lo_done.at(u + 1))
            if kts[0] == 0:
                pe.wait_ge(a.o_lo_done.sem, a.o_lo_done.at(u))
            a.values(pe, u, b, kts, lambda kt: (v_hi[b][:, kt, :], v_lo[b][:, kt, :]))

        def take_hi(act, u, b):
            act.wait_ge(a.pv_done.sem, a.pv_done.at(u + 1))
            act.wait_ge(out_done.sem, out_done.at(2 * u - 2))
            act.copy(o_hi[b][:, :], a.O[:, :]).then_inc(a.o_hi_done.sem, 1)

        def take_lo(dve, u, b):
            dve.wait_ge(a.o_hi_done.sem, a.o_hi_done.at(u + 1))
            dve.tensor_tensor(o_lo[b][:, :], a.O[:, :], o_hi[b][:, :].bitcast(F32), ALU.subtract
                              ).then_inc(a.o_lo_done.sem, 1)

        def out_half(pe, h, b, half):
            u = 2 * h + b
            pe.wait_ge(a.o_lo_done.sem, a.o_lo_done.at(u + 1))
            pe.wait_ge(wo_lo_done.sem, wo_lo_done.at(h + 1))
            pe.wait_ge(added.sem, added.at(2 * u + half))
            for t in range(2):
                q = slice((2 * half + t) * P, (2 * half + t + 1) * P)
                ins = split_product(pe, acc[:, t * HID:(t + 1) * HID], (o_hi[b][:, q], o_lo[b][:, q]),
                                    (wo[1][:, :], wo[2][:, :]), True, True)
            ins.then_inc(out_done.sem, 1)

        def add_half(dve, u, b, half):
            n = 2 * u + half
            dve.wait_ge(out_done.sem, out_done.at(n + 1))
            dve.wait_ge(added.sem, added.at(n - 3))
            part = c.x[:, 4 * b + 2 * half:4 * b + 2 * half + 2, :]
            dve.tensor_tensor(part, part, acc[:, :].rearrange("p (t h) -> p t h", h=HID), ALU.add
                              ).then_inc(added.sem, 1)

        def uqk_hi(act, h):
            act.wait_ge(uqk_in.sem, uqk_in.at(80 * (h + 1)))
            act.wait_ge(q_projected.sem, q_projected.at(2 * h))
            act.copy(uq[1][:, :, :], uq[0][:, :, :])
            act.copy(uk[1][:, :], uk[0][:, :]).then_inc(uqk_hi_done.sem, 1)

        def uqk_lo(pool, h):
            pool.wait_ge(uqk_hi_done.sem, uqk_hi_done.at(h + 1))
            pool.tensor_tensor(uq[2][:, :, :], uq[0][:, :, :], uq[1][:, :, :].bitcast(F32), ALU.subtract)
            pool.tensor_tensor(uk[2][:, :], uk[0][:, :], uk[1][:, :].bitcast(F32), ALU.subtract
                               ).then_inc(uqk_lo_done.sem, 1)

        def wo_hi(act, h):
            act.wait_ge(wo_in.sem, wo_in.at(16 * (h + 1)))
            act.wait_ge(out_done.sem, out_done.at(4 * h))
            act.copy(wo[1][:, :], wo[0][:, :]).then_inc(wo_hi_done.sem, 1)

        def wo_lo(pool, h):
            pool.wait_ge(wo_hi_done.sem, wo_hi_done.at(h + 1))
            pool.tensor_tensor(wo[2][:, :], wo[0][:, :], wo[1][:, :].bitcast(F32), ALU.subtract
                               ).then_inc(wo_lo_done.sem, 1)

        def all_heads(step):
            def run(eng):
                step(eng, 0, True, False, True)
                with eng.Fori(1, MLA_HEADS - 2) as h:
                    step(eng, h, False, False, True)
                step(eng, MLA_HEADS - 2, False, False, False)
                step(eng, MLA_HEADS - 1, False, True, False)
            return run

        with nc.Block() as block:
            @block.sync
            def _(sp):
                def load_next_uqk(h):
                    sp.wait_ge(uqk_lo_done.sem, uqk_lo_done.at(h))
                    load_uqk(sp, h)

                def load_uv(h):
                    sp.wait_ge(v_projected.sem, v_projected.at(2 * h))
                    sp.dma_start(uv[0:KV_LAT, :], head_cols(d("W_UV"), h)).then_inc(uv_in.sem, 16)
                    sp.dma_start(uv[KV_LAT:R2, :], head_row(d("b_UV"), h)).then_inc(uv_in.sem, 16)

                def load_wo(h):
                    sp.wait_ge(wo_lo_done.sem, wo_lo_done.at(h))
                    sp.dma_start(wo[0][:, :], d("W_O").rearrange("(n p) h -> n p h", p=P)[bass.ds(h, 1), :, :].rearrange(
                        "o p h -> p (o h)")).then_inc(wo_in.sem, 16)
                load_uv(0)
                load_next_uqk(1)
                with sp.Fori(1, MLA_HEADS - 1) as h:
                    load_next_uqk(h + 1)
                    load_wo(h - 1)
                    load_uv(h)
                load_wo(MLA_HEADS - 2)
                load_uv(MLA_HEADS - 1)
                load_wo(MLA_HEADS - 1)

            @block.tensor
            def _(pe):
                a.open(pe, "pe")
                out_done.open(pe)
                keys_pe(pe, 0, 0)
                queries_pe(pe, 0, 0, 0)
                pe.wait_ge(once_lo.sem, once_lo.at(2))
                key_rope_pe(pe, 0, 0)
                query_rope_pe(pe, 0, 0)
                keys_pe(pe, 0, 1)
                queries_pe(pe, 0, 1, 0)
                for t in range(QT):
                    scores(pe, 0, 0, t)
                    if t == 1:
                        key_rope_pe(pe, 0, 1)
                    if t == 2:
                        query_rope_pe(pe, 0, 1)

                def step(pe, h, first, last, weights):
                    for b in range(BATCH):
                        u = 2 * h + b
                        n = (h + 1, b)
                        for t in range(QT):
                            if not (last and b == 1):
                                scores(pe, u + 1, 1 - b, t)
                            a.turn(pe, u, b, t)
                            prev = not (first and b == 0)
                            if t == 0 and not last:
                                keys_pe(pe, *n)
                                queries_pe(pe, *n, u)
                            if t == 1:
                                if prev:
                                    values(pe, u - 1, 1 - b, [0])
                                if not last:
                                    key_rope_pe(pe, *n)
                                if not first:
                                    out_half(pe, h - 1, b, 0)
                            if t == 2:
                                if prev:
                                    values(pe, u - 1, 1 - b, [1])
                                if not last:
                                    query_rope_pe(pe, *n)
                                values_make_pe(pe, h, b, 2 * MLA_HEADS if last else u + 3)
                            if t == 3:
                                if prev:
                                    values(pe, u - 1, 1 - b, [2, 3])
                                if not first:
                                    out_half(pe, h - 1, b, 1)
                all_heads(step)(pe)
                h, u = MLA_HEADS - 1, MLA_UNITS - 1
                values(pe, u, 1, [0, 1, 2, 3])
                for b in range(BATCH):
                    out_half(pe, h, b, 0)
                    out_half(pe, h, b, 1)

            @block.scalar
            def _(act):
                a.open(act, "act")
                act.wait_ge(based.sem, based.at(1))
                uqk_hi(act, 0)
                act.wait_ge(rot_in.sem, rot_in.at(16 * 5))
                act.copy(wqr[1][:, :], wqr[0][:, :]).then_inc(once_hi.sem, 1)
                act.copy(wkr[1][:, :], wkr[0][:, :]).then_inc(once_hi.sem, 1)
                for b in range(BATCH):
                    keys_act(act, 0, b)
                    queries_act(act, 0, b)
                    if b == 0:
                        key_rope_act(act, 0, b)
                        query_rope_act(act, 0, b)
                for t in range(QT):
                    a.exp(act, 0, 0, t)
                    if t == 1:
                        key_rope_act(act, 0, 1)
                    if t == 2:
                        query_rope_act(act, 0, 1)
                uqk_hi(act, 1)

                def step(act, h, first, last, weights):
                    for b in range(BATCH):
                        u = 2 * h + b
                        n = (h + 1, b)
                        for t in range(QT):
                            if t == 0 and not first:
                                take_hi(act, u - 2, b)
                            a.step_act(act, u, b, t, not (last and b == 1))
                            if t == 0:
                                if not last:
                                    keys_act(act, *n)
                                    queries_act(act, *n)
                            if t == 1 and not last:
                                key_rope_act(act, *n)
                            if t == 2:
                                if not last:
                                    query_rope_act(act, *n)
                                if b == 1 and weights:
                                    uqk_hi(act, h + 2)
                            if t == 3:
                                values_make_act(act, h, b)
                                if b == 1:
                                    wo_hi(act, h)
                all_heads(step)(act)
                for b in range(BATCH):
                    take_hi(act, MLA_UNITS - 2 + b, b)

            @block.vector
            def _(dve):
                a.open(dve, "dve")
                added.open(dve)
                dve.memset(uq[0][Q_LAT_HALF:H1, 0, :], 0.0).then_inc(based.sem, 1)
                dve.wait_ge(once_hi.sem, once_hi.at(2))
                dve.tensor_tensor(wqr[2][:, :], wqr[0][:, :], wqr[1][:, :].bitcast(F32), ALU.subtract
                                  ).then_inc(once_lo.sem, 1)
                dve.tensor_tensor(wkr[2][:, :], wkr[0][:, :], wkr[1][:, :].bitcast(F32), ALU.subtract
                                  ).then_inc(once_lo.sem, 1)
                dve.wait_ge(tables.sem, tables.at(16 * 4))
                for b in range(BATCH):
                    keys_dve(dve, 0, b)
                    queries_dve(dve, 0, b)
                    if b == 0:
                        key_rope_dve(dve, 0, b)
                        query_rope_dve(dve, 0, b)
                for t in range(QT):
                    a.maximum(dve, 0, 0, t)
                    a.invert(dve, 0, 0, t)
                    if t == 1:
                        key_rope_dve(dve, 0, 1)
                    if t == 2:
                        query_rope_dve(dve, 0, 1)
                for t in range(TILES):
                    dve.tensor_tensor(c.x[:, t, :], c.x[:, t, :], bo[:, :], ALU.add).then_inc(based.sem, 1)
                dve.wait_ge(based.sem, based.at(1 + TILES))

                def step(dve, h, first, last, weights):
                    for b in range(BATCH):
                        u = 2 * h + b
                        n = (h + 1, b)
                        for t in range(QT):
                            if not (last and b == 1):
                                a.maximum(dve, u + 1, 1 - b, t)
                            if t == 0 and not first:
                                take_lo(dve, u - 2, b)
                            if t == 2 and not last:
                                query_rope_dve(dve, *n)
                            a.split_lo(dve, u, b, t)
                            if not (last and b == 1):
                                a.invert(dve, u + 1, 1 - b, t)
                            if t == 0:
                                if not last:
                                    keys_dve(dve, *n)
                                    queries_dve(dve, *n)
                            if t == 1 and not last:
                                key_rope_dve(dve, *n)
                            if t == 2 and not first:
                                add_half(dve, u - 2, b, 0)
                            if t == 3:
                                values_make_dve(dve, h, b)
                                if not first:
                                    add_half(dve, u - 2, b, 1)
                all_heads(step)(dve)
                for b in range(BATCH):
                    take_lo(dve, MLA_UNITS - 2 + b, b)
                    add_half(dve, MLA_UNITS - 2 + b, b, 0)
                    add_half(dve, MLA_UNITS - 2 + b, b, 1)

            @block.gpsimd
            def _(pool):
                pool.wait_ge(based.sem, based.at(1))
                uqk_lo(pool, 0)
                key_rope_sum(pool, 0, 0)
                key_rope_lo(pool, 0, 0)
                query_rope_lo(pool, 0, 0)
                for t in range(QT):
                    a.normalise(pool, 0, 0, t)
                    if t == 1:
                        key_rope_sum(pool, 0, 1)
                        key_rope_lo(pool, 0, 1)
                    if t == 2:
                        query_rope_lo(pool, 0, 1)
                uqk_lo(pool, 1)

                def step(pool, h, first, last, weights):
                    for b in range(BATCH):
                        u = 2 * h + b
                        n = (h + 1, b)
                        for t in range(QT):
                            if t == 2 and not last:
                                key_rope_lo(pool, *n)
                            if t == 3 and not last:
                                query_rope_lo(pool, *n)
                            if t == 3 and b == 1 and weights:
                                uqk_lo(pool, h + 2)
                            if not (last and b == 1):
                                a.normalise(pool, u + 1, 1 - b, t)
                            if t == 1 and not last:
                                key_rope_sum(pool, *n)
                            if t == 3 and b == 1:
                                wo_lo(pool, h)
                all_heads(step)(pool)


GQA_HEADS, GQA_KV = 32, 4
GQA_REP = GQA_HEADS // GQA_KV
GQA_UNITS = BATCH * GQA_REP


def gqa_jobs():
    jobs = []
    for u in range(GQA_UNITS):
        ahead = u + 3
        jobs.append((u, "q", ahead % GQA_UNITS, ahead >= GQA_UNITS, "A"))
        for at, kind, which, nxt in ((2, "k", 1, False), (4, "v", 1, False), (9, "k", 0, True), (11, "v", 0, True)):
            if u == at:
                jobs.append((u, kind, which, nxt, "B"))
    return jobs


class GqaFirst:

    def __init__(self, c, ctx, name):
        sb = lambda n, s, dt=F32: c.sb(ctx, f"{name}_{n}", s, dt)
        sem = lambda n: c.sem(ctx, f"{name}_{n}")
        self.c = c
        self.cos, self.sin = sb("cos", [P, SEQ]), sb("sin", [P, SEQ])
        self.kcos, self.ksin = sb("kcos", [P, SEQ]), sb("ksin", [P, SEQ])
        self.eye16, self.mask16 = sb("eye16", [P, P], BF16), sb("mask16", [P, P], BF16)
        self.wq_raw = [sb(f"wq_raw{n}", [P, KT, P]) for n in range(4)]
        self.wo_raw = [sb(f"wo_raw{n}", [P, HID]) for n in range(4)]
        self.wk_raw, self.wv_raw = sb("wk_raw", [P, KT, P]), sb("wv_raw", [P, KT, P])
        self.tables, self.wk_in, self.wv_in = sem("tables"), sem("wk_in"), sem("wv_in")
        self.wq_in, self.wo_in = [sem(f"wq_in{n}") for n in range(4)], [sem(f"wo_in{n}") for n in range(4)]

    def cols(self, w, n):
        return self.c.dram[w].rearrange("(k p) (n d) -> n p k d", p=P, d=P)[bass.ds(n, 1), :, :, :].rearrange(
            "o p k d -> p (o k) d")

    def load(self, sp):
        c = self.c
        sp.dma_start(self.wk_raw[:, :, :], self.cols("L0_ffn_Wk", 0)).then_inc(self.wk_in.sem, 16)
        for dst, src in ((self.kcos, "gqa_kcos"), (self.ksin, "gqa_ksin"), (self.eye16, "eye16"),
                         (self.mask16, "mask16"), (self.cos, "gqa_cos"), (self.sin, "gqa_sin")):
            sp.dma_start(dst[:, :], c.dram[src]).then_inc(self.tables.sem, 16)
        sp.dma_start(self.wv_raw[:, :, :], self.cols("L0_ffn_Wv", 0)).then_inc(self.wv_in.sem, 16)
        for h in range(4):
            sp.dma_start(self.wq_raw[h][:, :, :], self.cols("L0_ffn_Wq", h)).then_inc(self.wq_in[h].sem, 16)
            sp.dma_start(self.wo_raw[h][:, :], c.dram["L0_ffn_Wo"].rearrange("(n p) h -> n p h", p=P)[h, :, :]
                         ).then_inc(self.wo_in[h].sem, 16)


def gqa_phase(c, name, y, first):
    nc = c.nc
    JOBS = gqa_jobs()
    FIRST = [j for j in JOBS if j[3]]
    ROPE = [j for j in JOBS if j[1] != "v"]
    V = [j for j in JOBS if j[1] == "v"]
    N_J, N_R, N_V = len(JOBS), len(ROPE), len(V)
    F_J, F_R, F_V = len(FIRST), sum(j[1] != "v" for j in FIRST), sum(j[1] == "v" for j in FIRST)

    def number(jobs, per, first, job, g, before_loop):
        if before_loop:
            kinds = [j for j in FIRST if j in jobs]
            return kinds.index(job)
        if isinstance(g, int) and g == GQA_KV - 1:
            jobs = [j for j in jobs if not j[3]]
        return g * per + (first + jobs.index(job))

    with ExitStack() as ctx:
        sb = lambda n, s, dt=F32: c.sb(ctx, f"{name}_{n}", s, dt)
        sem = lambda n, k=0: c.sem(ctx, f"{name}_{n}", k)
        a = Attention(c, ctx, name, causal=True)
        X = c.ps(ctx, f"{name}_X")
        acc = [c.ps(ctx, f"{name}_acc{n}") for n in range(2)]
        cos, sin, kcos, ksin, eye16, mask16 = first.cos, first.sin, first.kcos, first.ksin, first.eye16, first.mask16
        wq_raw, wo_raw, wk_raw, wv_raw = first.wq_raw, first.wo_raw, first.wk_raw, first.wv_raw
        wq_hi, wq_lo = sb("wq_hi", [P, GQA_REP, KT, P], F32R), sb("wq_lo", [P, GQA_REP, KT, P], F32R)
        wo_hi, wo_lo = sb("wo_hi", [P, GQA_REP, HID], F32R), sb("wo_lo", [P, GQA_REP, HID], F32R)
        wk_hi, wk_lo = sb("wk_hi", [P, KT, P], F32R), sb("wk_lo", [P, KT, P], F32R)
        k_hi, k_lo = sb("k_hi", [P, TOK], F32R), sb("k_lo", [P, TOK], F32R)
        v_hi, v_lo = sb("v_hi", [P, BATCH, QT, P], F32R), sb("v_lo", [P, BATCH, QT, P], F32R)
        q_hi = [sb(f"q_hi{n}", [P, SEQ], F32R) for n in range(4)]
        q_lo = [sb(f"q_lo{n}", [P, SEQ], F32R) for n in range(4)]
        o_hi = [sb(f"o_hi{n}", [P, SEQ], F32R) for n in range(2)]
        o_lo = [sb(f"o_lo{n}", [P, SEQ], F32R) for n in range(2)]
        part_cos, swapped, part_sin, full, vfull = [sb(n, [P, SEQ]) for n in (
            "part_cos", "swapped", "part_sin", "full", "vfull")]
        tables, wq_in, wo_in, wk_in, wv_in = first.tables, first.wq_in, first.wo_in, first.wk_in, first.wv_in
        wq_hi_done, wq_lo_done = sem("wq_hi_done"), sem("wq_lo_done", 4)
        wo_hi_done, wo_lo_done = sem("wo_hi_done"), sem("wo_lo_done", 4)
        wk_hi_done, wk_lo_done = sem("wk_hi_done"), sem("wk_lo_done")
        projected, x_read = sem("projected", 2), sem("x_read", 2)
        cos_done, sin_done, full_done, r_hi_done, r_lo_done = [sem(n, 2) for n in (
            "cos_done", "sin_done", "full_done", "r_hi_done", "r_lo_done")]
        v_hi_done, v_lo_done = sem("v_hi_done"), sem("v_lo_done", 2)
        out_done, flushed = sem("out_done", 2), sem("flushed", 4)

        def job_numbers(job, g, before_loop=False):
            j = number(JOBS, N_J, F_J, job, g, before_loop)
            kinds, per, first = (V, N_V, F_V) if job[1] == "v" else (ROPE, N_R, F_R)
            return j, number(kinds, per, first, job, g, before_loop)

        def q_number(g, u):
            if u >= 3:
                return number(ROPE, N_R, F_R, (u - 3, "q", u, False, "A"), g, False)
            return g * N_R + 1 + u

        def bank(job, before):
            return (X, *acc)[FIRST.index(job) % 3] if before else X

        def job_pe(pe, job, g, before=False):
            j, n = job_numbers(job, g, before)
            _, kind, which, nxt, _ = job
            gg = 0 if before else (g + 1 if nxt else g)
            pe.wait_ge(x_read.sem, x_read.at(j - 2 if before else j))
            out = bank(job, before)
            if kind == "q":
                pe.wait_ge(wq_lo_done.sem, wq_lo_done.at(8 * gg + which % 8 + 1))
                w = [(wq_hi[:, which % 8, kt, :], wq_lo[:, which % 8, kt, :]) for kt in range(KT)]
                half = which // 8
            elif kind == "k":
                pe.wait_ge(wk_lo_done.sem, wk_lo_done.at(gg + 1))
                w = [(wk_hi[:, kt, :], wk_lo[:, kt, :]) for kt in range(KT)]
                half = which
            else:
                pe.wait_ge(wv_in.sem, wv_in.at(16 * (gg + 1)))
                for t in range(QT):
                    tok = which * SEQ + t * P
                    for kt in range(KT):
                        ins = pe.matmul(out[:, t * P:(t + 1) * P], c.hT[:, kt, tok:tok + P], wv_raw[:, kt, :],
                                        start=kt == 0, stop=kt == KT - 1, skip_group_check=True)
                ins.then_inc(projected.sem, 1)
                return
            toks = slice(half * SEQ, half * SEQ + SEQ)
            for kt in range(KT):
                ins = split_product(pe, out[:, :], w[kt], (c.hT_hi[:, kt, toks], c.hT_lo[:, kt, toks]),
                                    kt == 0, kt == KT - 1)
            ins.then_inc(projected.sem, 1)

        def job_act_read(act, job, g, before=False):
            j, n = job_numbers(job, g, before)
            out = bank(job, before)
            if job[1] == "v":
                act.wait_ge(projected.sem, projected.at(j + 1))
                act.wait_ge(v_lo_done.sem, v_lo_done.at(n))
                act.copy(vfull[:, :], out[:, :]).then_inc(x_read.sem, 1)
                return
            act.wait_ge(cos_done.sem, cos_done.at(n + 1))
            act.wait_ge(sin_done.sem, sin_done.at(n))
            act.copy(swapped[0:64, :], out[64:128, :])
            act.copy(swapped[64:128, :], out[0:64, :]).then_inc(x_read.sem, 1)

        def job_act_hi(act, job, g, before=False):
            j, n = job_numbers(job, g, before)
            _, kind, which, nxt, _ = job
            gg = 0 if before else (g + 1 if nxt else g)
            if kind == "v":
                act.wait_ge(x_read.sem, x_read.at(j + 1))
                if not before:
                    act.wait_ge(a.pv_done.sem, a.pv_done.at(16 * gg - 8 if which == 0 else 16 * gg))
                act.copy(v_hi[:, which, :, :], vfull[:, :].rearrange("p (t d) -> p t d", d=P)).then_inc(v_hi_done.sem, 1)
                return
            act.wait_ge(full_done.sem, full_done.at(n + 1))
            if kind == "q":
                if not before:
                    act.wait_ge(a.scored.sem, a.scored.at(4 * (16 * gg + which) - 12))
                dst = q_hi[which % 4][:, :]
            else:
                if not before:
                    act.wait_ge(a.scored.sem, a.scored.at(4 * (16 * gg - 8 if which == 0 else 16 * gg)))
                dst = k_hi[:, which * SEQ:(which + 1) * SEQ]
            act.copy(dst, full[:, :]).then_inc(r_hi_done.sem, 1)

        def job_dve_cos(dve, job, g, before=False):
            if job[1] == "v":
                return
            j, n = job_numbers(job, g, before)
            dve.wait_ge(projected.sem, projected.at(j + 1))
            dve.wait_ge(full_done.sem, full_done.at(n))
            dve.tensor_tensor(part_cos[:, :], bank(job, before)[:, :], (kcos if job[1] == "k" else cos)[:, :], ALU.mult
                              ).then_inc(cos_done.sem, 1)

        def job_dve_full(dve, job, g, before=False):
            if job[1] == "v":
                return
            j, n = job_numbers(job, g, before)
            dve.wait_ge(sin_done.sem, sin_done.at(n + 1))
            dve.wait_ge(cos_done.sem, cos_done.at(n + 1))
            dve.wait_ge(r_lo_done.sem, r_lo_done.at(n))
            dve.tensor_tensor(full[:, :], part_cos[:, :], part_sin[:, :], ALU.add).then_inc(full_done.sem, 1)

        def job_dve_lo(dve, job, g, before=False):
            if job[1] == "v":
                return
            j, n = job_numbers(job, g, before)
            dve.wait_ge(r_hi_done.sem, r_hi_done.at(n + 1))
            which = job[2]
            if job[1] == "q":
                hi, lo = q_hi[which % 4][:, :], q_lo[which % 4][:, :]
            else:
                hi, lo = [x[:, which * SEQ:(which + 1) * SEQ] for x in (k_hi, k_lo)]
            dve.wait_ge(full_done.sem, full_done.at(n + 1))
            dve.tensor_tensor(lo, full[:, :], hi.bitcast(F32), ALU.subtract).then_inc(r_lo_done.sem, 1)

        def job_pool(pool, job, g, before=False):
            j, n = job_numbers(job, g, before)
            if job[1] == "v":
                pool.wait_ge(v_hi_done.sem, v_hi_done.at(n + 1))
                pool.tensor_tensor(v_lo[:, job[2], :, :], vfull[:, :].rearrange("p (t d) -> p t d", d=P),
                                   v_hi[:, job[2], :, :].bitcast(F32), ALU.subtract).then_inc(v_lo_done.sem, 1)
                return
            pool.wait_ge(x_read.sem, x_read.at(j + 1))
            pool.wait_ge(full_done.sem, full_done.at(n))
            pool.tensor_tensor(part_sin[:, :], swapped[:, :], (ksin if job[1] == "k" else sin)[:, :], ALU.mult
                               ).then_inc(sin_done.sem, 1)

        def wq_hi_split(act, n, h, before=False, g=None):
            act.wait_ge(wq_in[h % 4].sem, wq_in[h % 4].at(16 * (n // 4 + 1) if before else (g + 1) * 32 + (h // 4 + 1) * 16))
            if not before:
                act.wait_ge(projected.sem, projected.at(number(JOBS, N_J, F_J, (5 + h, "q", 8 + h, False, "A"), g, False) + 1))
            act.copy(wq_hi[:, h, :, :], wq_raw[h % 4][:, :, :]).then_inc(wq_hi_done.sem, 1)

        def wq_lo_split(pool, n, h):
            pool.wait_ge(wq_hi_done.sem, wq_hi_done.at(n + 1))
            pool.tensor_tensor(wq_lo[:, h, :, :], wq_raw[h % 4][:, :, :], wq_hi[:, h, :, :].bitcast(F32),
                               ALU.subtract).then_inc(wq_lo_done.sem, 1)

        def wo_hi_split(act, n, h, g=None):
            act.wait_ge(wo_in[h % 4].sem, wo_in[h % 4].at(16 * (n // 4 + 1) if g is None else g * 32 + (h // 4 + 1) * 16))
            if g is not None:
                act.wait_ge(out_done.sem, out_done.at(16 * g - 8 + h + 1))
            act.copy(wo_hi[:, h, :], wo_raw[h % 4][:, :]).then_inc(wo_hi_done.sem, 1)

        def wo_lo_split(pool, n, h):
            pool.wait_ge(wo_hi_done.sem, wo_hi_done.at(n + 1))
            pool.tensor_tensor(wo_lo[:, h, :], wo_raw[h % 4][:, :], wo_hi[:, h, :].bitcast(F32),
                               ALU.subtract).then_inc(wo_lo_done.sem, 1)

        def wk_hi_split(act, g):
            act.wait_ge(wk_in.sem, wk_in.at(16 * (g + 1)))
            if not isinstance(g, int):
                act.wait_ge(projected.sem, projected.at(number(JOBS, N_J, F_J, (2, "k", 1, False, "B"), g - 1, False) + 1))
            act.copy(wk_hi[:, :, :], wk_raw[:, :, :]).then_inc(wk_hi_done.sem, 1)

        def wk_lo_split(pool, g):
            pool.wait_ge(wk_hi_done.sem, wk_hi_done.at(g + 1))
            pool.tensor_tensor(wk_lo[:, :, :], wk_raw[:, :, :], wk_hi[:, :, :].bitcast(F32),
                               ALU.subtract).then_inc(wk_lo_done.sem, 1)

        def load_wq(sp, n, h):
            sp.wait_ge(wq_lo_done.sem, wq_lo_done.at(n - 3))
            sp.dma_start(wq_raw[h % 4][:, :, :], c.dram["L0_ffn_Wq"].rearrange("(k p) (n d) -> n p k d", p=P, d=P)[
                bass.ds(n, 1), :, :, :].rearrange("o p k d -> p (o k) d")).then_inc(wq_in[h % 4].sem, 16)

        def load_wo(sp, n, h):
            sp.wait_ge(wo_lo_done.sem, wo_lo_done.at(n - 3))
            sp.dma_start(wo_raw[h % 4][:, :], c.dram["L0_ffn_Wo"].rearrange("(n p) h -> n p h", p=P)[
                bass.ds(n, 1), :, :].rearrange("o p h -> p (o h)")).then_inc(wo_in[h % 4].sem, 16)

        def load_kv(sp, which, g):
            raw, done, w = (wk_raw, wk_in, "L0_ffn_Wk") if which == "k" else (wv_raw, wv_in, "L0_ffn_Wv")
            sp.dma_start(raw[:, :, :], c.dram[w].rearrange("(k p) (n d) -> n p k d", p=P, d=P)[
                bass.ds(g, 1), :, :, :].rearrange("o p k d -> p (o k) d")).then_inc(done.sem, 16)

        def scores(pe, g, u, t):
            gg, v = (g, u) if u < GQA_UNITS else (g + 1, 0)
            if t == 0:
                pe.wait_ge(r_lo_done.sem, r_lo_done.at(q_number(gg, v) + 1))
            b = v // GQA_REP
            a.scores(pe, 16 * gg + v, v % 2, t, (q_hi[v % 4][:, t * P:(t + 1) * P], q_lo[v % 4][:, t * P:(t + 1) * P]),
                     (k_hi[:, b * SEQ:(b + 1) * SEQ], k_lo[:, b * SEQ:(b + 1) * SEQ]), (eye16[:, :], mask16[:, :]))

        def before(g, u, n):
            return (g, u - n) if u >= n else (g - 1, u - n + GQA_UNITS)

        def values(pe, g, u, kts):
            b = u // GQA_REP
            pe.wait_ge(v_lo_done.sem, v_lo_done.at(2 * g + b + 1))
            if kts[0] == 0:
                pe.wait_ge(a.o_lo_done.sem, a.o_lo_done.at(16 * g + u))
            a.values(pe, 16 * g + u, u % 2, kts, lambda kt: (v_hi[:, b, kt, :], v_lo[:, b, kt, :]))

        def out_project(pe, g, u, tiles):
            h = u % GQA_REP
            pe.wait_ge(wo_lo_done.sem, wo_lo_done.at(8 * g + h + 1))
            pe.wait_ge(a.o_lo_done.sem, a.o_lo_done.at(16 * g + u + 1))
            if h == 0 and tiles[0] == 0:
                pe.wait_ge(flushed.sem, flushed.at(2 * (2 * g + u // GQA_REP)))
            for t in tiles:
                ins = split_product(pe, acc[t // 2][:, t % 2 * HID:t % 2 * HID + HID],
                                    (o_hi[u % 2][:, t * P:(t + 1) * P], o_lo[u % 2][:, t * P:(t + 1) * P]),
                                    (wo_hi[:, h, :], wo_lo[:, h, :]), h == 0 and t % 2 == 0, h == GQA_REP - 1)
            if tiles[-1] == QT - 1:
                ins.then_inc(out_done.sem, 1)

        def flush(dve, g, b):
            dve.wait_ge(out_done.sem, out_done.at(16 * g + 8 * b + 8))
            for n in range(2):
                part = y[:, 4 * b + 2 * n:4 * b + 2 * n + 2, :]
                dve.wait_ge(flushed.sem, flushed.at(2 * (2 * g + b) - 4 + n + 1))
                dve.tensor_tensor(part, part, acc[n][:, :].rearrange("p (t h) -> p t h", h=HID), ALU.add
                                  ).then_inc(flushed.sem, 1)

        def take_hi(act, g, u):
            act.wait_ge(a.pv_done.sem, a.pv_done.at(16 * g + u + 1))
            act.wait_ge(out_done.sem, out_done.at(16 * g + u - 1))
            act.copy(o_hi[u % 2][:, :], a.O[:, :]).then_inc(a.o_hi_done.sem, 1)

        def take_lo(dve, g, u):
            dve.wait_ge(a.o_hi_done.sem, a.o_hi_done.at(16 * g + u + 1))
            dve.tensor_tensor(o_lo[u % 2][:, :], a.O[:, :], o_hi[u % 2][:, :].bitcast(F32), ALU.subtract
                              ).then_inc(a.o_lo_done.sem, 1)

        def jobs_of(u, slot, last):
            return [j for j in JOBS if j[0] == u and j[4] == slot and not (last and j[3])]

        def all_units(eng, unit):
            unit(eng, 0, 0, 2, False)
            unit(eng, 0, 1, 1, False)
            with eng.Fori(0, GQA_KV - 1) as g:
                for u in range(2, GQA_UNITS):
                    unit(eng, g, u, 0, False)
                for u in range(2):
                    unit(eng, g + 1, u, 0, False)
            for u in range(2, GQA_UNITS):
                unit(eng, GQA_KV - 1, u, 0, True)

        with nc.Block() as block:
            @block.sync
            def _(sp):
                for h in range(4, GQA_REP):
                    load_wq(sp, h, h)
                    load_wo(sp, h, h)

                def body(g):
                    sp.wait_ge(wk_lo_done.sem, wk_lo_done.at(g + 1))
                    load_kv(sp, "k", g + 1)
                    j, _ = job_numbers((4, "v", 1, False, "B"), g)
                    sp.wait_ge(projected.sem, projected.at(j + 1))
                    load_kv(sp, "v", g + 1)
                    for h in range(GQA_REP):
                        load_wq(sp, 8 * g + 8 + h, h)
                        load_wo(sp, 8 * g + 8 + h, h)
                with sp.Fori(0, GQA_KV - 1) as g:
                    body(g)

            @block.tensor
            def _(pe):
                a.open(pe, "pe")
                projected.open(pe)
                out_done.open(pe)
                pe.wait_ge(tables.sem, tables.at(96))
                pe.wait_ge(a.cleared.sem, a.cleared.at(4))
                for job in FIRST[:-1]:
                    job_pe(pe, job, 0, True)
                for t in range(QT):
                    scores(pe, 0, 0, t)
                    if t == 1:
                        job_pe(pe, FIRST[-1], 0, True)

                def unit(pe, g, u, missing, last):
                    for t in range(QT):
                        if u + 1 < GQA_UNITS or not last:
                            scores(pe, g, u + 1, t)
                        a.turn(pe, 16 * g + u, u % 2, t)
                        if t == 0:
                            for job in jobs_of(u, "A", last):
                                job_pe(pe, job, g)
                        kts, tiles = ([], [0], [], [1, 2, 3])[t], ([], [0, 1], [2, 3], [])[t]
                        if kts and missing < 2:
                            values(pe, *before(g, u, 1), kts)
                        if tiles and missing < 1:
                            out_project(pe, *before(g, u, 2), tiles)
                        if t == 2:
                            for job in jobs_of(u, "B", last):
                                job_pe(pe, job, g)
                all_units(pe, unit)
                values(pe, GQA_KV - 1, GQA_UNITS - 1, [0, 1, 2, 3])
                for u in (GQA_UNITS - 2, GQA_UNITS - 1):
                    out_project(pe, GQA_KV - 1, u, [0, 1, 2, 3])

            @block.scalar
            def _(act):
                a.open(act, "act")
                x_read.open(act)
                r_hi_done.open(act)
                wk_hi_split(act, 0)
                for h in range(3):
                    wq_hi_split(act, h, h, before=True)
                for n, job in enumerate(FIRST[:-1]):
                    job_act_read(act, job, 0, True)
                    job_act_hi(act, job, 0, True)
                    wo_hi_split(act, n, n)
                    wq_hi_split(act, n + 3, n + 3, before=True)
                for t in range(QT):
                    a.exp(act, 0, 0, t)
                job_act_read(act, FIRST[-1], 0, True)
                job_act_hi(act, FIRST[-1], 0, True)
                wq_hi_split(act, 7, 7, before=True)
                for n in (4, 5):
                    wo_hi_split(act, n, n)

                def unit(act, g, u, missing, last):
                    gp, up = before(g, u, 1)
                    for t in range(QT):
                        a.step_act(act, 16 * g + u, u % 2, t, u + 1 < GQA_UNITS or not last)
                        if t == 0 and missing < 2:
                            for job in jobs_of(up, "A", last):
                                job_act_hi(act, job, gp)
                            for job in jobs_of(up, "B", last):
                                if job[1] == "v":
                                    job_act_hi(act, job, gp)
                        if t == 1:
                            for job in jobs_of(up, "B", last):
                                if job[1] == "k" and missing < 2:
                                    job_act_hi(act, job, gp)
                            for job in jobs_of(u, "A", last):
                                job_act_read(act, job, g)
                        if t == 3:
                            for job in jobs_of(u, "B", last):
                                job_act_read(act, job, g)
                            if missing < 2:
                                take_hi(act, *before(g, u, 1))
                            if u in (0, 1):
                                wo_hi_split(act, 8 * g + 6 + u, 6 + u, g)
                            if not last:
                                if u == 6:
                                    wk_hi_split(act, g + 1)
                                if u >= 8:
                                    wq_hi_split(act, 8 * g + u, u - 8, g=g)
                                if u >= 10:
                                    wo_hi_split(act, 8 * g + u - 2, u - 10, g + 1)
                all_units(act, unit)
                take_hi(act, GQA_KV - 1, GQA_UNITS - 1)

            @block.vector
            def _(dve):
                a.open(dve, "dve")
                for s in (cos_done, full_done, r_lo_done, flushed):
                    s.open(dve)
                a.clear_unseen(dve)
                dve.wait_ge(tables.sem, tables.at(96))
                for job in FIRST[:-1]:
                    job_dve_cos(dve, job, 0, True)
                    job_dve_full(dve, job, 0, True)
                    job_dve_lo(dve, job, 0, True)
                for t in range(QT):
                    a.maximum(dve, 0, 0, t)
                    a.invert(dve, 0, 0, t)
                    if t == 1:
                        job_dve_cos(dve, FIRST[-1], 0, True)
                job_dve_full(dve, FIRST[-1], 0, True)
                job_dve_lo(dve, FIRST[-1], 0, True)

                def unit(dve, g, u, missing, last):
                    gp, up = before(g, u, 1)
                    for t in range(QT):
                        more = u + 1 < GQA_UNITS or not last
                        if t == 3:
                            for job in jobs_of(u, "B", last):
                                job_dve_cos(dve, job, g)
                        if more:
                            a.maximum(dve, 16 * g + u + 1, (u + 1) % 2, t)
                        if t == 0 and missing < 1:
                            take_lo(dve, *before(g, u, 2))
                        a.split_lo(dve, 16 * g + u, u % 2, t)
                        if more:
                            a.invert(dve, 16 * g + u + 1, (u + 1) % 2, t)
                        if t == 0:
                            if missing < 2:
                                for job in jobs_of(up, "A", last):
                                    job_dve_lo(dve, job, gp)
                                for job in jobs_of(up, "B", last):
                                    job_dve_full(dve, job, gp)
                            for job in jobs_of(u, "A", last):
                                job_dve_cos(dve, job, g)
                        if t == 1:
                            if missing < 2:
                                for job in jobs_of(up, "B", last):
                                    job_dve_lo(dve, job, gp)
                        if t == (2 if jobs_of(u, "B", last) else 3):
                            for job in jobs_of(u, "A", last):
                                job_dve_full(dve, job, g)
                        if t == 3:
                            if u == GQA_REP + 1:
                                flush(dve, g, 0)
                            if u == 1 and missing < 1:
                                flush(dve, g - 1, 1)
                all_units(dve, unit)
                for u in (GQA_UNITS - 2, GQA_UNITS - 1):
                    take_lo(dve, GQA_KV - 1, u)
                flush(dve, GQA_KV - 1, 1)

            @block.gpsimd
            def _(pool):
                for s in (sin_done, wq_lo_done, wo_lo_done, v_lo_done):
                    s.open(pool)
                pool.wait_ge(tables.sem, tables.at(96))
                wk_lo_split(pool, 0)
                for h in range(3):
                    wq_lo_split(pool, h, h)
                for n, job in enumerate(FIRST[:-1]):
                    job_pool(pool, job, 0, True)
                    wo_lo_split(pool, n, n)
                    wq_lo_split(pool, n + 3, n + 3)
                for t in range(QT):
                    a.normalise(pool, 0, 0, t)
                job_pool(pool, FIRST[-1], 0, True)
                wq_lo_split(pool, 7, 7)
                for n in (4, 5):
                    wo_lo_split(pool, n, n)

                def unit(pool, g, u, missing, last):
                    gp, up = before(g, u, 1)
                    for t in range(QT):
                        if u + 1 < GQA_UNITS or not last:
                            a.normalise(pool, 16 * g + u + 1, (u + 1) % 2, t)
                        if t == 0 and missing < 2:
                            for job in jobs_of(up, "B", last):
                                job_pool(pool, job, gp)
                        if t == 1:
                            for job in jobs_of(u, "A", last):
                                job_pool(pool, job, g)
                        if t == 3:
                            if u in (0, 1):
                                wo_lo_split(pool, 8 * g + 6 + u, 6 + u)
                            if not last:
                                if u == 6:
                                    wk_lo_split(pool, g + 1)
                                if u >= 8:
                                    wq_lo_split(pool, 8 * g + u, u - 8)
                                if u >= 10:
                                    wo_lo_split(pool, 8 * g + u - 2, u - 10)
                all_units(pool, unit)


EXPERTS, TOPK, INNER = 32, 8, 128


class MoeFirst:

    def __init__(self, c, ctx, name):
        sb = lambda n, s: c.sb(ctx, f"{name}_{n}", s)
        self.c = c
        self.wr, self.bias = sb("wr", [P, KT, EXPERTS]), sb("bias", [P, EXPERTS])
        self.raw = [sb(f"raw{n}", [P, 3 * HID]) for n in range(2)]
        self.router_in = c.sem(ctx, f"{name}_router_in")
        self.raw_in = [c.sem(ctx, f"{name}_raw_in{n}") for n in range(2)]

    def load_expert(self, sp, e, slot, shared=False):
        c = self.c
        if shared:
            src = [c.dram["L0_ffn_Wsg"], c.dram["L0_ffn_Wsu"], c.dram["L0_ffn_Wsd"]]
        else:
            src = [c.dram[f"L0_ffn_{n}"][bass.ds(e, 1), :, :].rearrange("o a b -> (o a) b") for n in ("Wg", "Wu", "Wd")]
        for n in range(2):
            sp.dma_start(self.raw[slot][:, n * HID:(n + 1) * HID].rearrange("p (k i) -> p k i", i=INNER),
                         src[n].rearrange("(k p) i -> p k i", p=P)).then_inc(self.raw_in[slot].sem, 16)
        sp.dma_start(self.raw[slot][:, 2 * HID:3 * HID], src[2]).then_inc(self.raw_in[slot].sem, 16)

    def load(self, sp):
        c = self.c
        sp.dma_start(self.wr[:, :, :], c.dram["L0_ffn_Wr"].rearrange("(k p) e -> p k e", p=P)
                     ).then_inc(self.router_in.sem, 16)
        sp.dma_start(self.bias[:, :], c.dram["L0_ffn_expert_bias"].rearrange("(a e) -> a e", a=1)
                     .partition_broadcast(P)).then_inc(self.router_in.sem, 16)
        for e in range(2):
            self.load_expert(sp, e, e)


def router_phase(c, name, w_table, first):
    nc = c.nc
    with ExitStack() as ctx:
        sb = lambda n, s: c.sb(ctx, f"{name}_{n}", s)
        sem = lambda n: c.sem(ctx, f"{name}_{n}")
        wr, bias, loaded = first.wr, first.bias, first.router_in
        score = sb("score", [P, TILES, EXPERTS])
        biased = sb("biased", [P, TILES, EXPERTS])
        best = sb("best", [P, TILES, 8])
        rest = sb("rest", [P, TILES, EXPERTS])
        chosen = sb("chosen", [P, TILES, EXPERTS])
        wsel = sb("wsel", [P, TILES, EXPERTS])
        total = sb("total", [P, TILES])
        inv = sb("inv", [P, TILES])
        wnorm = sb("wnorm", [P, TILES, EXPERTS])
        wT = sb("wT", [EXPERTS, TOK])
        ones = sb("ones", [1, TOK])
        logits = c.ps(ctx, f"{name}_logits")
        turned_ps = [c.ps(ctx, f"{name}_wT{n}") for n in range(2)]
        (logit, scored, bias_added, topped, replaced, marked, picked, summed, inverted, weighted,
         turned, copied, one, stored) = [sem(n) for n in (
            "logit", "scored", "bias_added", "topped", "replaced", "marked", "picked", "summed",
            "inverted", "weighted", "turned", "copied", "one", "stored")]
        with nc.Block() as block:
            @block.sync
            def _(sp):
                sp.wait_ge(one.sem, one.at(1))
                sp.dma_start(w_table[EXPERTS:EXPERTS + 1, :], ones[:, :]).then_inc(stored.sem, 16)
                sp.wait_ge(copied.sem, copied.at(2))
                sp.dma_start(w_table[0:EXPERTS, :], wT[:, :]).then_inc(stored.sem, 16)
                sp.wait_ge(stored.sem, stored.at(32))

            @block.tensor
            def _(pe):
                pe.wait_ge(loaded.sem, loaded.at(32))
                for t in range(TILES):
                    for kt in range(KT):
                        ins = pe.matmul(logits[:, t * EXPERTS:(t + 1) * EXPERTS], c.hT[:, kt, t * P:(t + 1) * P],
                                        wr[:, kt, :], start=kt == 0, stop=kt == KT - 1)
                ins.then_inc(logit.sem, 1)
                pe.wait_ge(weighted.sem, weighted.at(1))
                for t in range(TILES):
                    ins = pe.transpose(turned_ps[t // 4][0:EXPERTS, t % 4 * P:(t % 4 + 1) * P], wnorm[:, t, :],
                                       c.ident[:, :])
                    if t % 4 == 3:
                        ins.then_inc(turned.sem, 1)

            @block.scalar
            def _(act):
                act.wait_ge(logit.sem, logit.at(1))
                act.activation(score[:, :, :], logits[:, 0:TILES * EXPERTS].rearrange("p (t e) -> p t e", e=EXPERTS),
                               ACT.Sigmoid).then_inc(scored.sem, 1)

            @block.vector
            def _(dve):
                dve.memset(ones[:, :], 1.0).then_inc(one.sem, 1)
                dve.wait_ge(scored.sem, scored.at(1))
                for t in range(TILES):
                    dve.tensor_tensor(biased[:, t, :], score[:, t, :], bias[:, :], ALU.add).then_inc(bias_added.sem, 1)
                for t in range(TILES):
                    dve.wait_ge(bias_added.sem, bias_added.at(t + 1))
                    dve.max(best[:, t, :], biased[:, t, :]).then_inc(topped.sem, 1)
                for t in range(TILES):
                    dve.wait_ge(topped.sem, topped.at(t + 1))
                    dve.match_replace(out=rest[:, t, :], in_to_replace=best[:, t, :], in_values=biased[:, t, :],
                                      imm_value=-3e38).then_inc(replaced.sem, 1)
                dve.wait_ge(replaced.sem, replaced.at(TILES))
                dve.tensor_tensor(chosen[:, :, :], rest[:, :, :], biased[:, :, :], ALU.not_equal).then_inc(marked.sem, 1)
                dve.wait_ge(marked.sem, marked.at(1))
                dve.tensor_tensor(wsel[:, :, :], chosen[:, :, :], score[:, :, :], ALU.mult).then_inc(picked.sem, 1)
                dve.wait_ge(picked.sem, picked.at(1))
                dve.tensor_reduce(total[:, :], wsel[:, :, :], AX_X, ALU.add).then_inc(summed.sem, 1)
                dve.wait_ge(summed.sem, summed.at(1))
                dve.reciprocal(inv[:, :], total[:, :]).then_inc(inverted.sem, 1)
                dve.wait_ge(inverted.sem, inverted.at(1))
                dve.tensor_tensor(wnorm[:, :, :], wsel[:, :, :], inv[:, :].unsqueeze(2).broadcast_to([P, TILES, EXPERTS]),
                                  ALU.mult).then_inc(weighted.sem, 1)
                for n in range(2):
                    dve.wait_ge(turned.sem, turned.at(n + 1))
                    dve.tensor_copy(wT[:, n * 512:(n + 1) * 512], turned_ps[n][0:EXPERTS, :]).then_inc(copied.sem, 1)


def expert_phase(c, name, w_table, y, first):
    nc = c.nc
    WG, WU, WD = 0, HID, 2 * HID
    COLS = 3 * HID
    units = lambda e, half: 2 * e + half
    with ExitStack() as ctx:
        sb = lambda n, s, dt=F32: c.sb(ctx, f"{name}_{n}", s, dt)
        sem = lambda n, k=0: c.sem(ctx, f"{name}_{n}", k)
        raw, raw_in = first.raw, first.raw_in
        w_hi = [sb(f"w_hi{n}", [P, COLS], F32R) for n in range(2)]
        w_lo = [sb(f"w_lo{n}", [P, COLS], F32R) for n in range(2)]
        weight = [sb(f"weight{n}", [P, TOK]) for n in range(2)]
        gate = [sb(f"gate{n}", [P, 512]) for n in range(2)]
        scaled = [sb(f"scaled{n}", [P, 512]) for n in range(2)]
        inner = [sb(f"inner{n}", [P, 512]) for n in range(2)]
        a_hi = [sb(f"a_hi{n}", [P, 512], F32R) for n in range(2)]
        a_lo = [sb(f"a_lo{n}", [P, 512], F32R) for n in range(2)]
        G = [c.ps(ctx, f"{name}_G{n}") for n in range(2)]
        U = [c.ps(ctx, f"{name}_U{n}") for n in range(2)]
        acc = [c.ps(ctx, f"{name}_acc{n}") for n in range(4)]
        weight_in = [sem(f"weight_in{n}") for n in range(2)]
        gu_hi, gu_lo, d_hi, d_lo = sem("gu_hi", 2), sem("gu_lo", 2), sem("d_hi", 2), sem("d_lo", 2)
        projected, gated, weighed, multiplied = sem("projected", 2), sem("gated", 2), sem("weighed", 2), sem("multiplied", 2)
        a_hi_done, a_lo_done, down_done = sem("a_hi_done", 2), sem("a_lo_done", 2), sem("down_done", 4)
        y_added, summed = sem("y_added"), sem("summed")
        GU, DN = slice(0, WD), slice(WD, COLS)

        def load(sp, e, slot, shared=False):
            if not (isinstance(e, int) and e < 2):
                sp.wait_ge(d_hi.sem, d_hi.at(e - 1))
                sp.wait_ge(d_lo.sem, d_lo.at(e - 1))
                first.load_expert(sp, e, slot, shared)
            sp.wait_ge(weighed.sem, weighed.at(2 * e - 2))
            row = w_table[EXPERTS:EXPERTS + 1, :] if shared else w_table[bass.ds(e, 1), :]
            sp.dma_start(weight[slot][:, :], row.rearrange("o n -> (o n)").partition_broadcast(P)
                         ).then_inc(weight_in[slot].sem, 16)

        def split_hi(act, e, slot, nth, cols):
            act.wait_ge(raw_in[slot].sem, raw_in[slot].at(48 * (nth + 1)))
            used = projected if cols is GU else down_done
            act.wait_ge(used.sem, used.at(2 * e - 2))
            act.copy(w_hi[slot][:, cols], raw[slot][:, cols]).then_inc((gu_hi if cols is GU else d_hi).sem, 1)

        def split_lo(dve, e, slot, cols):
            hi_done, used = (gu_hi, projected) if cols is GU else (d_hi, down_done)
            dve.wait_ge(hi_done.sem, hi_done.at(e + 1))
            dve.wait_ge(used.sem, used.at(2 * e - 2))
            dve.tensor_tensor(w_lo[slot][:, cols], raw[slot][:, cols], w_hi[slot][:, cols].bitcast(F32),
                              ALU.subtract).then_inc((gu_lo if cols is GU else d_lo).sem, 1)

        def project(pe, e, half, slot):
            u = 2 * e + half
            if half == 0:
                pe.wait_ge(gu_lo.sem, gu_lo.at(e + 1))
            pe.wait_ge(gated.sem, gated.at(u - 1))
            for bank, base in ((G[half], WG), (U[half], WU)):
                if base == WU:
                    pe.wait_ge(multiplied.sem, multiplied.at(u - 1))
                for kt in range(KT):
                    cols = slice(base + kt * P, base + (kt + 1) * P)
                    toks = slice(half * 512, half * 512 + 512)
                    ins = split_product(pe, bank[:, :], (w_hi[slot][:, cols], w_lo[slot][:, cols]),
                                        (c.hT_hi[:, kt, toks], c.hT_lo[:, kt, toks]), kt == 0, kt == KT - 1)
            ins.then_inc(projected.sem, 1)

        def down(pe, e, half, slot, first=False):
            if half == 0:
                pe.wait_ge(d_lo.sem, d_lo.at(e + 1))
            pe.wait_ge(a_lo_done.sem, a_lo_done.at(2 * e + half + 1))
            for t in range(4):
                bank = acc[2 * half + t // 2]
                cols = slice(t * P, (t + 1) * P)
                ins = split_product(pe, bank[:, t % 2 * HID:t % 2 * HID + HID], (a_hi[half][:, cols], a_lo[half][:, cols]),
                                    (w_hi[slot][:, DN], w_lo[slot][:, DN]), first and t % 2 == 0, True)
            ins.then_inc(down_done.sem, 1)

        def silu(act, e, half):
            u = 2 * e + half
            act.wait_ge(projected.sem, projected.at(u + 1))
            act.wait_ge(weighed.sem, weighed.at(u - 1))
            act.activation(gate[half][:, :], G[half][:, :], ACT.Silu).then_inc(gated.sem, 1)

        def inner_hi(act, e, half):
            u = 2 * e + half
            act.wait_ge(multiplied.sem, multiplied.at(u + 1))
            act.wait_ge(down_done.sem, down_done.at(u - 1))
            act.copy(a_hi[half][:, :], inner[half][:, :]).then_inc(a_hi_done.sem, 1)

        def weigh(pool, e, half, slot, nth):
            u = 2 * e + half
            pool.wait_ge(weight_in[slot].sem, weight_in[slot].at(16 * (nth + 1)))
            pool.wait_ge(gated.sem, gated.at(u + 1))
            pool.wait_ge(multiplied.sem, multiplied.at(u - 1))
            pool.tensor_tensor(scaled[half][:, :], gate[half][:, :], weight[slot][:, half * 512:half * 512 + 512],
                               ALU.mult).then_inc(weighed.sem, 1)

        def multiply(dve, e, half):
            u = 2 * e + half
            dve.wait_ge(weighed.sem, weighed.at(u + 1))
            dve.wait_ge(projected.sem, projected.at(u + 1))
            dve.wait_ge(a_lo_done.sem, a_lo_done.at(u - 1))
            dve.tensor_tensor(inner[half][:, :], U[half][:, :], scaled[half][:, :], ALU.mult).then_inc(multiplied.sem, 1)

        def inner_lo(dve, e, half):
            u = 2 * e + half
            dve.wait_ge(a_hi_done.sem, a_hi_done.at(u + 1))
            dve.wait_ge(down_done.sem, down_done.at(u - 1))
            dve.tensor_tensor(a_lo[half][:, :], inner[half][:, :], a_hi[half][:, :].bitcast(F32),
                              ALU.subtract).then_inc(a_lo_done.sem, 1)

        PAIRS = EXPERTS // 2
        with nc.Block() as block:
            @block.sync
            def _(sp):
                for e in range(2):
                    load(sp, e, e)
                with sp.Fori(0, PAIRS - 1) as i:
                    for s in range(2):
                        load(sp, i * 2 + s + 2, s)
                load(sp, EXPERTS, 0, shared=True)

            @block.tensor
            def _(pe):
                projected.open(pe)
                down_done.open(pe)
                project(pe, 0, 0, 0)
                project(pe, 0, 1, 0)

                def pair(e, first=False):
                    project(pe, e + 1, 0, 1)
                    down(pe, e, 0, 0, first)
                    project(pe, e + 1, 1, 1)
                    down(pe, e, 1, 0, first)
                    project(pe, e + 2, 0, 0)
                    down(pe, e + 1, 0, 1)
                    project(pe, e + 2, 1, 0)
                    down(pe, e + 1, 1, 1)
                pair(0, True)
                with pe.Fori(1, PAIRS) as i:
                    pair(i * 2)
                down(pe, EXPERTS, 0, 0)
                down(pe, EXPERTS, 1, 0)

            @block.scalar
            def _(act):
                for s in (gu_hi, d_hi, gated, a_hi_done):
                    s.open(act)
                split_hi(act, 0, 0, 0, GU)
                split_hi(act, 0, 0, 0, DN)
                split_hi(act, 1, 1, 0, GU)
                silu(act, 0, 0)
                inner_hi(act, 0, 0)
                silu(act, 0, 1)

                def pair(e, i, last=False):
                    inner_hi(act, e, 1)
                    silu(act, e + 1, 0)
                    split_hi(act, e + 1, 1, i, DN)
                    inner_hi(act, e + 1, 0)
                    split_hi(act, e + 2, 0, i + 1, GU)
                    silu(act, e + 1, 1)
                    inner_hi(act, e + 1, 1)
                    silu(act, e + 2, 0)
                    split_hi(act, e + 2, 0, i + 1, DN)
                    inner_hi(act, e + 2, 0)
                    if not last:
                        split_hi(act, e + 3, 1, i + 1, GU)
                    silu(act, e + 2, 1)
                with act.Fori(0, PAIRS - 1) as i:
                    pair(i * 2, i)
                pair(EXPERTS - 2, PAIRS - 1, last=True)
                inner_hi(act, EXPERTS, 1)

            @block.gpsimd
            def _(pool):
                weighed.open(pool)
                with pool.Fori(0, PAIRS) as i:
                    for s in range(2):
                        for half in range(2):
                            weigh(pool, i * 2 + s, half, s, i)
                for half in range(2):
                    weigh(pool, EXPERTS, half, 0, PAIRS)

            @block.vector
            def _(dve):
                for s in (gu_lo, d_lo, multiplied, a_lo_done):
                    s.open(dve)
                split_lo(dve, 0, 0, GU)
                split_lo(dve, 0, 0, DN)
                split_lo(dve, 1, 1, GU)
                multiply(dve, 0, 0)
                inner_lo(dve, 0, 0)

                def pair(e, last=False):
                    multiply(dve, e, 1)
                    inner_lo(dve, e, 1)
                    split_lo(dve, e + 1, 1, DN)
                    multiply(dve, e + 1, 0)
                    inner_lo(dve, e + 1, 0)
                    split_lo(dve, e + 2, 0, GU)
                    multiply(dve, e + 1, 1)
                    inner_lo(dve, e + 1, 1)
                    split_lo(dve, e + 2, 0, DN)
                    multiply(dve, e + 2, 0)
                    inner_lo(dve, e + 2, 0)
                    if not last:
                        split_lo(dve, e + 3, 1, GU)
                with dve.Fori(0, PAIRS - 1) as i:
                    pair(i * 2)
                pair(EXPERTS - 2, last=True)
                multiply(dve, EXPERTS, 1)
                inner_lo(dve, EXPERTS, 1)
                dve.tensor_tensor(c.x[:, :, :], c.x[:, :, :], y[:, :, :], ALU.add).then_inc(y_added.sem, 1)
                dve.wait_ge(y_added.sem, y_added.at(1))
                dve.wait_ge(down_done.sem, down_done.at(2 * EXPERTS + 2))
                for n in range(4):
                    part = c.x[:, 2 * n:2 * n + 2, :]
                    dve.tensor_tensor(part, part, acc[n][:, :].rearrange("p (t h) -> p t h", h=HID),
                                      ALU.add).then_inc(summed.sem, 1)


MHA_HEADS, MHA_D = 16, 16
GROUP = 4
GROUPS = MHA_HEADS // GROUP
MHA_HALF = MHA_HEADS // 2
DIAG = P + MHA_D
HALF_COLS = MHA_HALF * DIAG


def mha_phase(c, name):
    nc = c.nc
    with ExitStack() as ctx:
        sb = lambda n, s, dt=F32: c.sb(ctx, f"{name}_{n}", s, dt)
        sem = lambda n, k=0: c.sem(ctx, f"{name}_{n}", k)
        a = Attention(c, ctx, name, causal=True)
        X = [c.ps(ctx, f"{name}_X{n}") for n in range(3)]
        acc = X[1:3]
        eye16, mask16 = sb("eye16", [P, P], BF16), sb("mask16", [P, P], BF16)
        w_raw = a.prob[0][:, :, :].rearrange("p a b -> p (a b)").rearrange("p (k m) -> p k m", k=KT)
        wv = a.prob[1][:, 0, :].rearrange("p (k m) -> p k m", k=KT)
        w_hi, w_lo = sb("w_hi", [P, KT, 2 * GROUPS * P], F32R), sb("w_lo", [P, KT, 2 * GROUPS * P], F32R)
        wo = sb("wo", [P, KT, HID])
        qk_hi, qk_lo = sb("qk_hi", [P, 2 * GROUPS, SEQ], F32R), sb("qk_lo", [P, 2 * GROUPS, SEQ], F32R)
        v_full = c.hT[:, :, :].rearrange("p k t -> p (k t)").rearrange("p (t h) -> p t h", h=HID)
        v_hi, v_lo = [sb(n, [P, QT, 2 * HALF_COLS], F32R) for n in ("v_hi", "v_lo")]
        z = sb("z", [P, SEQ])
        loaded, w_hi_done, w_lo_done, zeroed = sem("loaded"), sem("w_hi_done"), sem("w_lo_done"), sem("zeroed")
        v_made, v_kept, wv_in = sem("v_made"), sem("v_kept"), sem("wv_in")
        projected, qk_hi_done, qk_lo_done = sem("projected"), sem("qk_hi_done"), sem("qk_lo_done", 3)
        v_hi_done, v_lo_done = sem("v_hi_done"), sem("v_lo_done")
        out_done, added = sem("out_done", 2), sem("added", 1)
        JOBS = 2 * GROUPS

        def v_bank(t):
            return (*a.S, *a.T)[t // 2][:, t % 2 * HID:t % 2 * HID + HID]

        def qk_pe(pe, b, n):
            j = JOBS * b + n
            pe.wait_ge(qk_lo_done.sem, qk_lo_done.at(j - 2))
            pe.wait_ge(added.sem, added.at(2 * b))
            for kt in range(KT):
                ins = split_product(pe, X[n % 3][:, :], (w_hi[:, kt, n * P:(n + 1) * P], w_lo[:, kt, n * P:(n + 1) * P]),
                                    (c.hT_hi[:, kt, bass.ds(b * SEQ, SEQ)], c.hT_lo[:, kt, bass.ds(b * SEQ, SEQ)]),
                                    kt == 0, kt == KT - 1)
            ins.then_inc(projected.sem, 1)

        def scale(n):
            return 1.0 / float(np.sqrt(MHA_D)) if n < GROUPS else 1.0

        def qk_act(act, b, n):
            act.wait_ge(projected.sem, projected.at(JOBS * b + n + 1))
            act.activation(qk_hi[:, n, :], X[n % 3][:, :], ACT.Copy, scale=scale(n)).then_inc(qk_hi_done.sem, 1)

        def qk_dve(dve, b, n):
            dve.wait_ge(qk_hi_done.sem, qk_hi_done.at(JOBS * b + n + 1))
            dve.scalar_tensor_tensor(out=qk_lo[:, n, :], in0=X[n % 3][:, :], scalar=scale(n),
                                     in1=qk_hi[:, n, :].bitcast(F32), op0=ALU.mult, op1=ALU.subtract
                                     ).then_inc(qk_lo_done.sem, 1)

        def spread(x, kt):
            return x[:, kt, :].rearrange("p (h c) -> p h c", c=DIAG)[:, :, 0:MHA_D]

        def v_of(b, kt):
            return v_full[:, bass.ds(b * QT + kt, 1), :].rearrange("p o (h d) -> p (o h) d", d=MHA_D)

        def v_split_hi(act, b):
            act.wait_ge(a.pv_done.sem, a.pv_done.at(MHA_HEADS * b))
            for kt in range(QT):
                ins = act.copy(spread(v_hi, kt), v_of(b, kt))
            ins.then_inc(v_hi_done.sem, 1)

        def v_split_lo(pool, b):
            pool.wait_ge(v_hi_done.sem, v_hi_done.at(b + 1))
            for kt in range(QT):
                ins = pool.tensor_tensor(spread(v_lo, kt), v_of(b, kt), spread(v_hi, kt).bitcast(F32), ALU.subtract)
            ins.then_inc(v_lo_done.sem, 1)

        def scores(pe, b, h, t):
            rows = slice(32 * (h % GROUP), 32 * (h % GROUP) + 32)
            q, k = h // GROUP, GROUPS + h // GROUP
            pe.wait_ge(qk_lo_done.sem, qk_lo_done.at(JOBS * b + k + 1))
            a.scores(pe, MHA_HEADS * b + h, h % 2, t,
                     (qk_hi[rows, q, t * P:(t + 1) * P], qk_lo[rows, q, t * P:(t + 1) * P]),
                     (qk_hi[rows, k, :], qk_lo[rows, k, :]), (eye16[:, :], mask16[:, :]))

        def values(pe, b, h, kts):
            j = h % MHA_HALF
            col = h // MHA_HALF * HALF_COLS + j * P
            pe.wait_ge(v_lo_done.sem, v_lo_done.at(b + 1))
            if j == 0 and kts[0] == 0:
                pe.wait_ge(a.o_lo_done.sem, a.o_lo_done.at(2 * b + h // MHA_HALF))
            a.values(pe, MHA_HEADS * b + h, h % 2, kts, lambda kt: (v_hi[:, kt, col:col + P], v_lo[:, kt, col:col + P]),
                     start=j == 0, stop=j == MHA_HALF - 1)

        def take(dve, b, half):
            dve.wait_ge(a.pv_done.sem, a.pv_done.at(MHA_HEADS * b + MHA_HALF * (half + 1)))
            dve.wait_ge(out_done.sem, out_done.at(2 * b + half))
            dve.tensor_copy(z[:, :], a.O[:, :]).then_inc(a.o_lo_done.sem, 1)

        def out_project(pe, b, half):
            pe.wait_ge(a.o_lo_done.sem, a.o_lo_done.at(2 * b + half + 1))
            for t in range(QT):
                ins = pe.matmul(acc[t // 2][:, t % 2 * HID:t % 2 * HID + HID], z[:, t * P:(t + 1) * P],
                                wo[:, half, :], start=half == 0 and t % 2 == 0, stop=half == 1,
                                skip_group_check=True)
            ins.then_inc(out_done.sem, 1)

        def add(dve, b):
            dve.wait_ge(out_done.sem, out_done.at(2 * b + 2))
            for n in range(2):
                part = c.x[:, bass.ds(4 * b + 2 * n, 2), :]
                dve.tensor_tensor(part, part, acc[n][:, :].rearrange("p (t h) -> p t h", h=HID), ALU.add
                                  ).then_inc(added.sem, 1)

        with nc.Block() as block:
            @block.sync
            def _(sp):
                sp.dma_start(wv[:, :, :], c.dram["mha_wv"].rearrange("(k p) m -> p k m", p=P)).then_inc(wv_in.sem, 16)
                for n, w in enumerate(("mha_wq", "mha_wk")):
                    sp.dma_start(w_raw[:, :, n * GROUPS * P:(n + 1) * GROUPS * P],
                                 c.dram[w].rearrange("(k p) m -> p k m", p=P)).then_inc(loaded.sem, 16)
                sp.dma_start(wo[:, :, :], c.dram["mha_wo"].rearrange("(k p) m -> p k m", p=P)).then_inc(loaded.sem, 16)
                sp.dma_start(eye16[:, :], c.dram["eye16"]).then_inc(loaded.sem, 16)
                sp.dma_start(mask16[:, :], c.dram["mask16"]).then_inc(loaded.sem, 16)

            @block.tensor
            def _(pe):
                a.open(pe, "pe")
                out_done.open(pe)
                pe.wait_ge(wv_in.sem, wv_in.at(16))
                for t in range(TILES):
                    for kt in range(KT):
                        ins = pe.matmul(v_bank(t), c.hT[:, kt, t * P:(t + 1) * P], wv[:, kt, :],
                                        start=kt == 0, stop=kt == KT - 1, skip_group_check=True)
                ins.then_inc(v_made.sem, 1)
                pe.wait_ge(v_kept.sem, v_kept.at(TILES))
                pe.wait_ge(loaded.sem, loaded.at(80))
                pe.wait_ge(w_lo_done.sem, w_lo_done.at(KT))
                pe.wait_ge(a.cleared.sem, a.cleared.at(4))
                with pe.Fori(0, BATCH) as b:
                    for n in range(JOBS):
                        qk_pe(pe, b, n)
                    for t in range(QT):
                        scores(pe, b, 0, t)
                    for h in range(MHA_HEADS):
                        for t in range(QT):
                            if h + 1 < MHA_HEADS:
                                scores(pe, b, h + 1, t)
                            a.turn(pe, MHA_HEADS * b + h, h % 2, t)
                            if h > 0 and t in (1, 3):
                                values(pe, b, h - 1, [0] if t == 1 else [1, 2, 3])
                        if h == MHA_HALF + 1:
                            out_project(pe, b, 0)
                    values(pe, b, MHA_HEADS - 1, [0, 1, 2, 3])
                    out_project(pe, b, 1)

            @block.scalar
            def _(act):
                a.open(act, "act")
                act.wait_ge(loaded.sem, loaded.at(80))
                for kt in range(KT):
                    act.copy(w_hi[:, kt, :], w_raw[:, kt, :]).then_inc(w_hi_done.sem, 1)
                with act.Fori(0, BATCH) as b:
                    for n in range(JOBS):
                        qk_act(act, b, n)
                    act.wait_ge(v_kept.sem, v_kept.at(TILES))
                    act.wait_ge(zeroed.sem, zeroed.at(2))
                    v_split_hi(act, b)
                    for t in range(QT):
                        a.exp(act, MHA_HEADS * b, 0, t)
                    for h in range(MHA_HEADS):
                        for t in range(QT):
                            a.step_act(act, MHA_HEADS * b + h, h % 2, t, h + 1 < MHA_HEADS)

            @block.vector
            def _(dve):
                a.open(dve, "dve")
                qk_lo_done.open(dve)
                added.open(dve)
                dve.wait_ge(v_made.sem, v_made.at(1))
                for t in range(TILES):
                    dve.tensor_copy(v_full[:, t, :], v_bank(t)).then_inc(v_kept.sem, 1)
                for kt in range(KT):
                    dve.wait_ge(w_hi_done.sem, w_hi_done.at(kt + 1))
                    dve.tensor_tensor(w_lo[:, kt, :], w_raw[:, kt, :], w_hi[:, kt, :].bitcast(F32), ALU.subtract
                                      ).then_inc(w_lo_done.sem, 1)
                a.clear_unseen(dve)
                with dve.Fori(0, BATCH) as b:
                    for n in range(JOBS):
                        qk_dve(dve, b, n)
                    for t in range(QT):
                        a.maximum(dve, MHA_HEADS * b, 0, t)
                        a.invert(dve, MHA_HEADS * b, 0, t)
                    for h in range(MHA_HEADS):
                        for t in range(QT):
                            a.step_dve(dve, MHA_HEADS * b + h, h % 2, t, h + 1 < MHA_HEADS)
                            if h == MHA_HALF + 1 and t == 0:
                                take(dve, b, 0)
                    take(dve, b, 1)
                    add(dve, b)

            @block.gpsimd
            def _(pool):
                for x in (v_hi, v_lo):
                    pool.memset(x[:, :, :].bitcast(F32), 0.0).then_inc(zeroed.sem, 1)
                pool.wait_ge(zeroed.sem, zeroed.at(2))
                with pool.Fori(0, BATCH) as b:
                    v_split_lo(pool, b)
                    for t in range(QT):
                        a.normalise(pool, MHA_HEADS * b, 0, t)
                    for h in range(MHA_HEADS - 1):
                        for t in range(QT):
                            a.normalise(pool, MHA_HEADS * b + h + 1, (h + 1) % 2, t)


def ffn(c, name, w_table):
    with ExitStack() as ctx:
        y = c.sb(ctx, f"{name}_y", [P, TILES, HID])
        column = lambda w: c.dram[w].rearrange("(k p) -> p k", p=P)
        with ExitStack() as attention:
            first = GqaFirst(c, attention, f"{name}g1")
            norm_phase(c, f"{name}n1", c.x, False, dst=y, transpose=False, prefetch=first.load)
            norm_phase(c, f"{name}n2", y, True, weight=column("L0_ffn_ln1_w"))
            gqa_phase(c, f"{name}g", y, first)
        c.clear_sems()
        first = MoeFirst(c, ctx, f"{name}m1")
        norm_phase(c, f"{name}n3", y, True, weight=column("L0_ffn_ln2_w"), prefetch=first.load)
        router_phase(c, f"{name}r", w_table, first)
        expert_phase(c, f"{name}e", w_table, y, first)


def hybrid_kernel(nc, dram, out):
    w_table = nc.dram_tensor("w_table", (EXPERTS + 1, TOK), F32, kind="Internal").ap()
    with ExitStack() as ctx:
        c = Chip(nc, ctx, dram, out)
        load_phase(c)
        norm_phase(c, "an", c.x, False, split=False)
        mla_phase(c, "a")
        ffn(c, "f0", w_table)
        norm_phase(c, "bn", c.x, False)
        mha_phase(c, "b")
        ffn(c, "f1", w_table)
        store_phase(c)



def rotary(dim):
    inv = (1.0 / THETA ** (np.arange(0, dim, 2, dtype=np.float32) / np.float32(dim))).astype(np.float32)
    angle = (np.arange(SEQ, dtype=np.float32)[:, None] * inv[None, :]).astype(np.float32)
    return np.cos(angle).T.astype(np.float32), np.sin(angle).T.astype(np.float32)


def consts():
    bf16 = np.dtype("bfloat16")
    cos, sin = rotary(128)
    k_cos, k_sin = np.concatenate([cos, cos]), np.concatenate([-sin, sin])
    scale = np.float32(1.0 / np.sqrt(128.0))
    above = np.triu(np.full((P, P), -1e30, np.float32), k=1)
    c64, s64 = rotary(64)
    return {
        "mla_kcos": np.concatenate([c64, c64]), "mla_ksin": np.concatenate([-s64, -s64]),
        "mla_qrot": np.concatenate([c64, -s64]),
        "ident": np.eye(P, dtype=np.float32),
        "eye16": np.eye(P).astype(bf16),
        "mask16": above.astype(bf16),
        "gqa_kcos": k_cos, "gqa_ksin": k_sin,
        "gqa_cos": k_cos * scale, "gqa_sin": k_sin * scale,
    }


def mha_columns(w):
    out = np.zeros((HID, MHA_HEADS, 2 * MHA_D), np.float32)
    out[:, :, 0:MHA_D] = w.T.reshape(HID, MHA_HEADS, MHA_D)
    return out.reshape(HID, MHA_HEADS * 2 * MHA_D)


def mha_weights(wq, wk, wv, wo):
    return {"mha_wq": mha_columns(wq), "mha_wk": mha_columns(wk),
            "mha_wv": np.ascontiguousarray(wv.T), "mha_wo": np.ascontiguousarray(wo.T)}


def kernel(**inputs):
    import concourse.bacc as _bacc
    from concourse.bass_utils import run_bass_kernel_spmd as _run

    arrays = {n: np.ascontiguousarray(a) for n, a in inputs.items()}
    arrays.update(mha_weights(*[arrays.pop(f"L0_attn_b_{n}") for n in ("Wq", "Wk", "Wv", "Wo")]))
    arrays.update(consts())
    nc = _bacc.Bacc("TRN2", target_bir_lowering=False, num_devices=1)
    dram = {n: nc.dram_tensor(f"in_{n}", a.shape, mybir.dt.from_np(a.dtype), kind="ExternalInput").ap()
            for n, a in arrays.items()}
    out = nc.dram_tensor("out_0", (BATCH, SEQ, HID), F32, kind="ExternalOutput").ap()
    hybrid_kernel(nc, dram, out)
    r = _run(nc, [{f"in_{n}": a for n, a in arrays.items()}], core_ids=[0])
    return r.results[0]["out_0"]
```
